# Optimizing a Trainium2 kernel written in Bass

```python
import numpy as np
import jax
import jax.numpy as jnp

def _softmax(x, axis=-1):
    return jax.nn.softmax(x, axis=axis)

def _gelu(x):
    return jax.nn.gelu(x, approximate=True)

def _silu(x):
    return jax.nn.silu(x)

def _sigmoid(x):
    return jax.nn.sigmoid(x)

def _layernorm(x, axis=-1, eps=1e-05):
    m = jnp.mean(x, axis=axis, keepdims=True)
    v = jnp.var(x, axis=axis, keepdims=True)
    return (x - m) / jnp.sqrt(v + eps)

def _scatter_add(tgt, idx, src, axis=0):
    return tgt.at[idx].add(src)

def _segment_sum(src, seg, n):
    return jax.ops.segment_sum(src, seg, n)
kernel_name = 'mk_xattn_ffn_d4_seqx_r4_a7dfb1'

def setup_inputs(seed: int=0):
    np.random.seed(seed)
    _w = jnp.asarray

    def _rec_inputs():
        import jax
        import jax.numpy as jnp
        _rk = jax.random.key(seed)
        x = 0.002226 + 0.9996 * jax.random.normal(jax.random.fold_in(_rk, 1), (8, 112, 256), jnp.float32)
        _lenS = 112 - jax.random.randint(jax.random.fold_in(_rk, 7), (8,), 0, max(1, 112 // 4) + 1, jnp.int32)
        _lenS2 = 375 - jax.random.randint(jax.random.fold_in(_rk, 8), (8,), 0, max(1, 375 // 4) + 1, jnp.int32)
        _ctx_1024P = jax.random.normal(jax.random.fold_in(_rk, 11), (8, 16, 256), jnp.float32)
        _ctx_1024c = jax.random.dirichlet(jax.random.fold_in(_rk, 511), 0.3 * jnp.ones((16,), jnp.float32), (8, 375))
        _ctx_1024t = jnp.einsum('bsk,bkd->bsd', _ctx_1024c, _ctx_1024P)
        _ctx_1024t = _ctx_1024t * jax.lax.rsqrt(jnp.mean(jnp.square(_ctx_1024t)) + 1e-12) * 0.953939
        ctx_1024 = -0.000125008 + 0.999885 * (_ctx_1024t + 0.3 * jax.random.normal(jax.random.fold_in(_rk, 611), (8, 375, 256), jnp.float32))
        _validS = jnp.arange(112)[None, :] < _lenS[:, None]
        _validS2 = jnp.arange(375)[None, :] < _lenS2[:, None]
        _causal = jnp.tril(jnp.ones((112, 112), dtype=bool))
        mask_BxS2_bk0 = jnp.logical_not(jnp.broadcast_to(_validS2[:, :], (8, 375)))
        return (x, ctx_1024, mask_BxS2_bk0)
    x, ctx_1024, mask_BxS2_bk0 = _rec_inputs()

    def _L0_xattn_setup():
        import jax, jax.numpy as jnp
        import numpy as np
        DIM = 256
        HEADS = 16
        DIM_HEAD = 64
        INNER = HEADS * DIM_HEAD
        EPS = 1e-05

        def layernorm(t, g, b):
            mu = jnp.mean(t, axis=-1, keepdims=True)
            var = jnp.var(t, axis=-1, keepdims=True)
            return (t - mu) * jax.lax.rsqrt(var + EPS) * g + b
        key = jax.random.key(seed)
        ks = jax.random.split(key, 8)
        b, n, m = (8, 1024, 64)
        x = jax.random.normal(ks[0], (b, n, DIM), dtype=jnp.float32)
        latents = jax.random.normal(ks[1], (b, m, DIM), dtype=jnp.float32)
        mask = jax.random.randint(ks[2], (b, n), 0, 2).astype(bool)
        s = 0.02
        Wq = jax.random.normal(ks[3], (DIM, INNER), dtype=jnp.float32) * s
        Wkv = jax.random.normal(ks[4], (DIM, 2 * INNER), dtype=jnp.float32) * s
        Wout = jax.random.normal(ks[5], (INNER, DIM), dtype=jnp.float32) * s
        ln_x_g = jnp.ones((DIM,), jnp.float32)
        ln_x_b = jnp.zeros((DIM,), jnp.float32)
        ln_l_g = jnp.ones((DIM,), jnp.float32)
        ln_l_b = jnp.zeros((DIM,), jnp.float32)
        ln_o_g = jnp.ones((DIM,), jnp.float32)
        ln_o_b = jnp.zeros((DIM,), jnp.float32)
        return {'x': x, 'latents': latents, 'mask': mask, 'ln_x_g': ln_x_g, 'ln_x_b': ln_x_b, 'ln_l_g': ln_l_g, 'ln_l_b': ln_l_b, 'Wq': Wq, 'Wkv': Wkv, 'Wout': Wout, 'ln_o_g': ln_o_g, 'ln_o_b': ln_o_b}
    _L0_xattn_all = _L0_xattn_setup()
    _L0_xattn_in = {k: v for k, v in _L0_xattn_all.items() if k in ('ln_x_g', 'ln_x_b', 'ln_l_g', 'ln_l_b', 'Wq', 'Wkv', 'Wout', 'ln_o_g', 'ln_o_b')}
    del _L0_xattn_all

    def _L0_ffn_setup():
        import jax, jax.numpy as jnp
        import numpy as np
        H = 256
        I = 512
        E = 16
        K = 2
        B, T = (2, 512)
        key = jax.random.key(seed)
        k1, k2, k3, k4 = jax.random.split(key, 4)
        x = jax.random.normal(k1, (B, T, H), dtype=jnp.float32)
        Wg = jax.random.normal(k2, (E, H), dtype=jnp.float32) * 0.02
        W1 = jax.random.normal(k3, (E, I, H), dtype=jnp.float32) * 0.02
        W2 = jax.random.normal(k4, (E, H, I), dtype=jnp.float32) * 0.02
        return {'x': x, 'Wg': Wg, 'W1': W1, 'W2': W2}
    _L0_ffn_all = _L0_ffn_setup()
    _L0_ffn_in = {k: v for k, v in _L0_ffn_all.items() if k in ('Wg', 'W1', 'W2')}
    del _L0_ffn_all

    def _L1_xattn_setup():
        import jax, jax.numpy as jnp
        import numpy as np
        import math
        D_MODEL = 256
        N_HEADS = 16
        key = jax.random.key(seed)
        ks = jax.random.split(key, 11)
        N, L, S = (2, 512, 512)
        d = D_MODEL
        s = 1.0 / math.sqrt(d)
        return {'queries': jax.random.normal(ks[0], (N, L, d), dtype=jnp.float32), 'keys': jax.random.normal(ks[1], (N, S, d), dtype=jnp.float32), 'values': jax.random.normal(ks[2], (N, S, d), dtype=jnp.float32), 'Wq': jax.random.normal(ks[3], (d, d), dtype=jnp.float32) * s, 'bq': jax.random.normal(ks[4], (d,), dtype=jnp.float32) * s, 'Wk': jax.random.normal(ks[5], (d, d), dtype=jnp.float32) * s, 'bk': jax.random.normal(ks[6], (d,), dtype=jnp.float32) * s, 'Wv': jax.random.normal(ks[7], (d, d), dtype=jnp.float32) * s, 'bv': jax.random.normal(ks[8], (d,), dtype=jnp.float32) * s, 'Wo': jax.random.normal(ks[9], (d, d), dtype=jnp.float32) * s, 'bo': jax.random.normal(ks[10], (d,), dtype=jnp.float32) * s}
    _L1_xattn_all = _L1_xattn_setup()
    _L1_xattn_in = {k: v for k, v in _L1_xattn_all.items() if k in ('Wq', 'bq', 'Wk', 'bk', 'Wv', 'bv', 'Wo', 'bo')}
    del _L1_xattn_all

    def _L1_ffn_setup():
        import jax, jax.numpy as jnp
        import numpy as np
        BLOCK = 32
        W_BITS = 4
        ACT_BITS = 16

        def act_qdq(x):
            qmax = 2.0 ** (ACT_BITS - 1) - 1.0
            scale = jnp.maximum(jnp.max(jnp.abs(x)) / qmax, 1e-12)
            return jnp.clip(jnp.round(x / scale), -qmax - 1.0, qmax) * scale

        def fixed_qdq_u16(x):
            scale = 1.0 / 65536.0
            return jnp.clip(jnp.round(x / scale), 0.0, 65535.0) * scale

        def lpbq_dequant(w):
            O, I = w.shape
            qmax = 2.0 ** (W_BITS - 1) - 1.0
            wb = w.reshape(O, I // BLOCK, BLOCK)
            s = jnp.maximum(jnp.max(jnp.abs(wb), axis=-1, keepdims=True) / qmax, 1e-12)
            wq = jnp.clip(jnp.round(wb / s), -qmax - 1.0, qmax) * s
            return wq.reshape(O, I)
        key = jax.random.key(seed)
        k1, k2, k3, k4 = jax.random.split(key, 4)
        B, S, H, I = (2, 1024, 256, 768)
        x = jax.random.normal(k1, (B, S, H), jnp.float32)
        w_gate = jax.random.normal(k2, (I, H), jnp.float32) * 0.02
        w_up = jax.random.normal(k3, (I, H), jnp.float32) * 0.02
        w_down = jax.random.normal(k4, (H, I), jnp.float32) * 0.02
        return {'x': x, 'w_gate': w_gate, 'w_up': w_up, 'w_down': w_down}
    _L1_ffn_all = _L1_ffn_setup()
    _L1_ffn_in = {k: v for k, v in _L1_ffn_all.items() if k in ('w_gate', 'w_up', 'w_down')}
    del _L1_ffn_all

    def _L2_xattn_setup():
        import jax, jax.numpy as jnp
        import numpy as np
        DIM = 256
        HEADS = 16
        DIM_HEAD = 64
        INNER = HEADS * DIM_HEAD
        EPS = 1e-05

        def layer_norm(x, gamma, beta):
            mu = jnp.mean(x, axis=-1, keepdims=True)
            var = jnp.mean(jnp.square(x - mu), axis=-1, keepdims=True)
            return (x - mu) * jax.lax.rsqrt(var + EPS) * gamma + beta
        key = jax.random.key(seed)
        ks = jax.random.split(key, 6)
        b, n1, n2 = (8, 1024, 64)
        x = jax.random.normal(ks[0], (b, n1, DIM), dtype=jnp.float32)
        latents = jax.random.normal(ks[1], (b, n2, DIM), dtype=jnp.float32)
        s = 1.0 / np.sqrt(DIM)
        Wq = jax.random.normal(ks[2], (DIM, INNER), dtype=jnp.float32) * s
        Wkv = jax.random.normal(ks[3], (DIM, 2 * INNER), dtype=jnp.float32) * s
        Wout = jax.random.normal(ks[4], (INNER, DIM), dtype=jnp.float32) * (1.0 / np.sqrt(INNER))
        g1 = jnp.ones((DIM,), jnp.float32)
        b1 = jnp.zeros((DIM,), jnp.float32)
        g2 = jnp.ones((DIM,), jnp.float32)
        b2 = jnp.zeros((DIM,), jnp.float32)
        return {'x': x, 'latents': latents, 'g1': g1, 'b1': b1, 'g2': g2, 'b2': b2, 'Wq': Wq, 'Wkv': Wkv, 'Wout': Wout}
    _L2_xattn_all = _L2_xattn_setup()
    _L2_xattn_in = {k: v for k, v in _L2_xattn_all.items() if k in ('g1', 'b1', 'g2', 'b2', 'Wq', 'Wkv', 'Wout')}
    del _L2_xattn_all

    def _L2_ffn_setup():
        import jax, jax.numpy as jnp
        import numpy as np
        D_MODEL = 256
        D_HIDDEN = 1024
        NUM_EXPERT = 8
        TOP_K = 2
        B, N = (1, 2048)

        def _expert_mlp(x, W1, b1, W2, b2, W3, b3):
            h = jax.nn.gelu(jnp.einsum('bnd,dh->bnh', x, W1) + b1, approximate=False)
            h = jax.nn.gelu(jnp.einsum('bnh,hk->bnk', h, W2) + b2, approximate=False)
            return jnp.einsum('bnh,hd->bnd', h, W3) + b3
        key = jax.random.key(seed)
        ks = jax.random.split(key, 8)
        s1 = 1.0 / np.sqrt(D_MODEL)
        s2 = 1.0 / np.sqrt(D_HIDDEN)
        return {'x': jax.random.normal(ks[0], (B, N, D_MODEL), jnp.float32), 'expert_tokens': jax.random.normal(ks[1], (NUM_EXPERT, D_MODEL), jnp.float32), 'W1': jax.random.normal(ks[2], (NUM_EXPERT, D_MODEL, D_HIDDEN), jnp.float32) * s1, 'b1': jnp.zeros((NUM_EXPERT, D_HIDDEN), jnp.float32), 'W2': jax.random.normal(ks[3], (NUM_EXPERT, D_HIDDEN, D_HIDDEN), jnp.float32) * s2, 'b2': jnp.zeros((NUM_EXPERT, D_HIDDEN), jnp.float32), 'W3': jax.random.normal(ks[4], (NUM_EXPERT, D_HIDDEN, D_MODEL), jnp.float32) * s2, 'b3': jnp.zeros((NUM_EXPERT, D_MODEL), jnp.float32)}
    _L2_ffn_all = _L2_ffn_setup()
    _L2_ffn_in = {k: v for k, v in _L2_ffn_all.items() if k in ('expert_tokens', 'W1', 'b1', 'W2', 'b2', 'W3', 'b3')}
    del _L2_ffn_all

    def _L3_xattn_setup():
        import jax, jax.numpy as jnp
        import numpy as np
        D = 256
        NUM_ITERS = 3
        EPS = 1e-06
        SCALE = D ** (-0.5)

        def rmsnorm(x, w, eps=EPS):
            return x * jax.lax.rsqrt(jnp.mean(x * x, axis=-1, keepdims=True) + eps) * w

        def gru_cell(x, h, wih, whh, bih, bhh):
            gx = x @ wih.T + bih
            gh = h @ whh.T + bhh
            xr, xz, xn = jnp.split(gx, 3, axis=-1)
            hr, hz, hn = jnp.split(gh, 3, axis=-1)
            r = jax.nn.sigmoid(xr + hr)
            z = jax.nn.sigmoid(xz + hz)
            n = jnp.tanh(xn + r * hn)
            return (1.0 - z) * n + z * h
        key = jax.random.key(seed)
        ks = jax.random.split(key, 8)
        B, K, M, d = (8, 64, 1024, D)
        w_std = d ** (-0.5)
        return {'slots': jax.random.normal(ks[0], (B, K, d), jnp.float32), 'P': jax.random.normal(ks[1], (B, M, d), jnp.float32), 'Wq': jax.random.normal(ks[2], (d, d), jnp.float32) * w_std, 'Wk': jax.random.normal(ks[3], (d, d), jnp.float32) * w_std, 'Wv': jax.random.normal(ks[4], (d, d), jnp.float32) * w_std, 'gru_wih': jax.random.normal(ks[5], (3 * d, d), jnp.float32) * w_std, 'gru_whh': jax.random.normal(ks[6], (3 * d, d), jnp.float32) * w_std, 'gru_bih': jnp.zeros((3 * d,), jnp.float32), 'gru_bhh': jnp.zeros((3 * d,), jnp.float32), 'slot_norm_w': jnp.ones((d,), jnp.float32), 'input_norm_w': jnp.ones((d,), jnp.float32)}
    _L3_xattn_all = _L3_xattn_setup()
    _L3_xattn_in = {k: v for k, v in _L3_xattn_all.items() if k in ('Wq', 'Wk', 'Wv', 'gru_wih', 'gru_whh', 'gru_bih', 'gru_bhh', 'slot_norm_w', 'input_norm_w')}
    del _L3_xattn_all

    def _L3_ffn_setup():
        import jax, jax.numpy as jnp
        import numpy as np
        D_MODEL = 256
        NUM_TILES = 64
        TPC = 8
        NUM_CLUSTERS = NUM_TILES // TPC
        GRID = 16
        COMP_H = 64
        NUM_KNOTS = 8
        EPS_LN = 1e-05

        def _calibrate(scores, knots, temperature):
            K = knots.shape[0]
            normalized = jax.nn.sigmoid(scores / (temperature[0] + 1e-06))
            idx_float = normalized * (K - 1)
            idx_low = jnp.clip(idx_float.astype(jnp.int32), 0, K - 2)
            idx_high = idx_low + 1
            t = idx_float - idx_low.astype(scores.dtype)
            val_low = knots[idx_low]
            val_high = knots[idx_high]
            return val_low + t * (val_high - val_low)

        def _forward(x, signatures_raw, knot_values, temperature, compress_w1, compress_b1, compress_w2, compress_b2, spline_w1, spline_b1, spline_w2, spline_b2, directions, norm_gamma, norm_beta, output_scale):
            B, T, D = x.shape
            xf = x.reshape(-1, D)
            q = jnp.where(signatures_raw > 0.3, 1.0, jnp.where(signatures_raw < -0.3, -1.0, 0.0)).astype(signatures_raw.dtype)
            sigs = signatures_raw + jax.lax.stop_gradient(q - signatures_raw)
            cluster_sigs = jnp.sign(sigs.reshape(NUM_CLUSTERS, TPC, D).mean(axis=1))
            cluster_scores = xf @ cluster_sigs.T
            cluster_gates = _calibrate(cluster_scores, knot_values, temperature)
            cluster_idx = jnp.argmax(cluster_gates, axis=-1)
            tile_scores = xf @ sigs.T
            tile_gates = _calibrate(tile_scores, knot_values, temperature)
            gates_by_cluster = tile_gates.reshape(-1, NUM_CLUSTERS, TPC)
            sel_gates = jnp.take_along_axis(gates_by_cluster, cluster_idx[:, None, None], axis=1)[:, 0, :]
            local_idx = jnp.argmax(sel_gates, axis=-1)
            tile_idx = cluster_idx * TPC + local_idx
            h = jax.nn.gelu(xf @ compress_w1 + compress_b1, approximate=False)
            comp = jnp.tanh(h @ compress_w2 + compress_b2)
            w1 = spline_w1[tile_idx]
            b1 = spline_b1[tile_idx]
            hh = jax.nn.relu(jnp.einsum('ni,nig->ng', comp, w1) + b1)
            w2 = spline_w2[tile_idx]
            b2 = spline_b2[tile_idx]
            mag = jnp.einsum('ng,ngo->no', hh, w2) + b2
            ffn_out = mag * directions[tile_idx] * output_scale[0]
            y = xf + ffn_out
            mu = y.mean(axis=-1, keepdims=True)
            var = ((y - mu) ** 2).mean(axis=-1, keepdims=True)
            y = (y - mu) / jnp.sqrt(var + EPS_LN) * norm_gamma + norm_beta
            return y.reshape(B, T, D)
        key = jax.random.key(seed)
        ks = jax.random.split(key, 12)
        B, T = (4, 1024)
        x = jax.random.normal(ks[0], (B, T, D_MODEL), dtype=jnp.float32)
        signatures_raw = jax.random.normal(ks[1], (NUM_TILES, D_MODEL), dtype=jnp.float32) * 0.5
        knot_values = jax.nn.sigmoid(jnp.linspace(-3.0, 3.0, NUM_KNOTS).astype(jnp.float32))
        temperature = jnp.ones((1,), dtype=jnp.float32)
        compress_w1 = jax.random.normal(ks[2], (D_MODEL, COMP_H), dtype=jnp.float32) * (1.0 / np.sqrt(D_MODEL))
        compress_b1 = jnp.zeros((COMP_H,), dtype=jnp.float32)
        compress_w2 = jax.random.normal(ks[3], (COMP_H, 2), dtype=jnp.float32) * (1.0 / np.sqrt(COMP_H))
        compress_b2 = jnp.zeros((2,), dtype=jnp.float32)
        spline_w1 = jax.random.normal(ks[4], (NUM_TILES, 2, GRID), dtype=jnp.float32) * (1.0 / np.sqrt(2.0))
        spline_b1 = jnp.zeros((NUM_TILES, GRID), dtype=jnp.float32)
        spline_w2 = jax.random.normal(ks[5], (NUM_TILES, GRID, 1), dtype=jnp.float32) * (1.0 / np.sqrt(GRID))
        spline_b2 = jnp.zeros((NUM_TILES, 1), dtype=jnp.float32)
        directions = jax.random.normal(ks[6], (NUM_TILES, D_MODEL), dtype=jnp.float32) * 0.02
        norm_gamma = jnp.ones((D_MODEL,), dtype=jnp.float32)
        norm_beta = jnp.zeros((D_MODEL,), dtype=jnp.float32)
        output_scale = jnp.ones((1,), dtype=jnp.float32) * 0.1
        return dict(x=x, signatures_raw=signatures_raw, knot_values=knot_values, temperature=temperature, compress_w1=compress_w1, compress_b1=compress_b1, compress_w2=compress_w2, compress_b2=compress_b2, spline_w1=spline_w1, spline_b1=spline_b1, spline_w2=spline_w2, spline_b2=spline_b2, directions=directions, norm_gamma=norm_gamma, norm_beta=norm_beta, output_scale=output_scale)
    _L3_ffn_all = _L3_ffn_setup()
    _L3_ffn_in = {k: v for k, v in _L3_ffn_all.items() if k in ('signatures_raw', 'knot_values', 'temperature', 'compress_w1', 'compress_b1', 'compress_w2', 'compress_b2', 'spline_w1', 'spline_b1', 'spline_w2', 'spline_b2', 'directions', 'norm_gamma', 'norm_beta', 'output_scale')}
    del _L3_ffn_all
    return {'x': x, 'ctx_1024': ctx_1024, 'mask_BxS2_bk0': mask_BxS2_bk0, 'L0_xattn_ln_x_g': _L0_xattn_in['ln_x_g'], 'L0_xattn_ln_x_b': _L0_xattn_in['ln_x_b'], 'L0_xattn_ln_l_g': _L0_xattn_in['ln_l_g'], 'L0_xattn_ln_l_b': _L0_xattn_in['ln_l_b'], 'L0_xattn_Wq': _L0_xattn_in['Wq'], 'L0_xattn_Wkv': _L0_xattn_in['Wkv'], 'L0_xattn_Wout': _L0_xattn_in['Wout'], 'L0_xattn_ln_o_g': _L0_xattn_in['ln_o_g'], 'L0_xattn_ln_o_b': _L0_xattn_in['ln_o_b'], 'L0_ffn_Wg': _L0_ffn_in['Wg'], 'L0_ffn_W1': _L0_ffn_in['W1'], 'L0_ffn_W2': _L0_ffn_in['W2'], 'L1_xattn_Wq': _L1_xattn_in['Wq'], 'L1_xattn_bq': _L1_xattn_in['bq'], 'L1_xattn_Wk': _L1_xattn_in['Wk'], 'L1_xattn_bk': _L1_xattn_in['bk'], 'L1_xattn_Wv': _L1_xattn_in['Wv'], 'L1_xattn_bv': _L1_xattn_in['bv'], 'L1_xattn_Wo': _L1_xattn_in['Wo'], 'L1_xattn_bo': _L1_xattn_in['bo'], 'L1_ffn_w_gate': _L1_ffn_in['w_gate'], 'L1_ffn_w_up': _L1_ffn_in['w_up'], 'L1_ffn_w_down': _L1_ffn_in['w_down'], 'L2_xattn_g1': _L2_xattn_in['g1'], 'L2_xattn_b1': _L2_xattn_in['b1'], 'L2_xattn_g2': _L2_xattn_in['g2'], 'L2_xattn_b2': _L2_xattn_in['b2'], 'L2_xattn_Wq': _L2_xattn_in['Wq'], 'L2_xattn_Wkv': _L2_xattn_in['Wkv'], 'L2_xattn_Wout': _L2_xattn_in['Wout'], 'L2_ffn_expert_tokens': _L2_ffn_in['expert_tokens'], 'L2_ffn_W1': _L2_ffn_in['W1'], 'L2_ffn_b1': _L2_ffn_in['b1'], 'L2_ffn_W2': _L2_ffn_in['W2'], 'L2_ffn_b2': _L2_ffn_in['b2'], 'L2_ffn_W3': _L2_ffn_in['W3'], 'L2_ffn_b3': _L2_ffn_in['b3'], 'L3_xattn_Wq': _L3_xattn_in['Wq'], 'L3_xattn_Wk': _L3_xattn_in['Wk'], 'L3_xattn_Wv': _L3_xattn_in['Wv'], 'L3_xattn_gru_wih': _L3_xattn_in['gru_wih'], 'L3_xattn_gru_whh': _L3_xattn_in['gru_whh'], 'L3_xattn_gru_bih': _L3_xattn_in['gru_bih'], 'L3_xattn_gru_bhh': _L3_xattn_in['gru_bhh'], 'L3_xattn_slot_norm_w': _L3_xattn_in['slot_norm_w'], 'L3_xattn_input_norm_w': _L3_xattn_in['input_norm_w'], 'L3_ffn_signatures_raw': _L3_ffn_in['signatures_raw'], 'L3_ffn_knot_values': _L3_ffn_in['knot_values'], 'L3_ffn_temperature': _L3_ffn_in['temperature'], 'L3_ffn_compress_w1': _L3_ffn_in['compress_w1'], 'L3_ffn_compress_b1': _L3_ffn_in['compress_b1'], 'L3_ffn_compress_w2': _L3_ffn_in['compress_w2'], 'L3_ffn_compress_b2': _L3_ffn_in['compress_b2'], 'L3_ffn_spline_w1': _L3_ffn_in['spline_w1'], 'L3_ffn_spline_b1': _L3_ffn_in['spline_b1'], 'L3_ffn_spline_w2': _L3_ffn_in['spline_w2'], 'L3_ffn_spline_b2': _L3_ffn_in['spline_b2'], 'L3_ffn_directions': _L3_ffn_in['directions'], 'L3_ffn_norm_gamma': _L3_ffn_in['norm_gamma'], 'L3_ffn_norm_beta': _L3_ffn_in['norm_beta'], 'L3_ffn_output_scale': _L3_ffn_in['output_scale']}

def reference(x, ctx_1024, mask_BxS2_bk0, L0_xattn_ln_x_g, L0_xattn_ln_x_b, L0_xattn_ln_l_g, L0_xattn_ln_l_b, L0_xattn_Wq, L0_xattn_Wkv, L0_xattn_Wout, L0_xattn_ln_o_g, L0_xattn_ln_o_b, L0_ffn_Wg, L0_ffn_W1, L0_ffn_W2, L1_xattn_Wq, L1_xattn_bq, L1_xattn_Wk, L1_xattn_bk, L1_xattn_Wv, L1_xattn_bv, L1_xattn_Wo, L1_xattn_bo, L1_ffn_w_gate, L1_ffn_w_up, L1_ffn_w_down, L2_xattn_g1, L2_xattn_b1, L2_xattn_g2, L2_xattn_b2, L2_xattn_Wq, L2_xattn_Wkv, L2_xattn_Wout, L2_ffn_expert_tokens, L2_ffn_W1, L2_ffn_b1, L2_ffn_W2, L2_ffn_b2, L2_ffn_W3, L2_ffn_b3, L3_xattn_Wq, L3_xattn_Wk, L3_xattn_Wv, L3_xattn_gru_wih, L3_xattn_gru_whh, L3_xattn_gru_bih, L3_xattn_gru_bhh, L3_xattn_slot_norm_w, L3_xattn_input_norm_w, L3_ffn_signatures_raw, L3_ffn_knot_values, L3_ffn_temperature, L3_ffn_compress_w1, L3_ffn_compress_b1, L3_ffn_compress_w2, L3_ffn_compress_b2, L3_ffn_spline_w1, L3_ffn_spline_b1, L3_ffn_spline_w2, L3_ffn_spline_b2, L3_ffn_directions, L3_ffn_norm_gamma, L3_ffn_norm_beta, L3_ffn_output_scale):
    import jax
    import jax.numpy as jnp

    def _L0_xattn_ref(x, latents, mask, ln_x_g, ln_x_b, ln_l_g, ln_l_b, Wq, Wkv, Wout, ln_o_g, ln_o_b):
        import jax, jax.numpy as jnp
        import numpy as np
        DIM = 256
        HEADS = 16
        DIM_HEAD = 64
        INNER = HEADS * DIM_HEAD
        EPS = 1e-05

        def layernorm(t, g, b):
            mu = jnp.mean(t, axis=-1, keepdims=True)
            var = jnp.var(t, axis=-1, keepdims=True)
            return (t - mu) * jax.lax.rsqrt(var + EPS) * g + b
        b, n, _ = x.shape
        m = latents.shape[1]
        scale = DIM_HEAD ** (-0.5)
        xn = layernorm(x, ln_x_g, ln_x_b)
        ln = layernorm(latents, ln_l_g, ln_l_b)
        q = ln @ Wq
        kv_input = jnp.concatenate((xn, ln), axis=1)
        kv = kv_input @ Wkv
        k, v = jnp.split(kv, 2, axis=-1)

        def heads(t):
            return t.reshape(t.shape[0], t.shape[1], HEADS, DIM_HEAD).transpose(0, 2, 1, 3)
        q, k, v = (heads(q) * scale, heads(k), heads(v))
        sim = jnp.einsum('bhid,bhjd->bhij', q, k)
        mask_full = jnp.concatenate((mask, jnp.ones((b, m), dtype=bool)), axis=1)
        max_neg = -jnp.finfo(sim.dtype).max
        sim = jnp.where(mask_full[:, None, None, :], sim, max_neg)
        attn = jax.nn.softmax(sim.astype(jnp.float32), axis=-1).astype(sim.dtype)
        out = jnp.einsum('bhij,bhjd->bhid', attn, v)
        out = out.transpose(0, 2, 1, 3).reshape(b, m, INNER)
        out = out @ Wout
        return layernorm(out, ln_o_g, ln_o_b)

    def _L0_ffn_ref(x, Wg, W1, W2):
        import jax, jax.numpy as jnp
        import numpy as np
        H = 256
        I = 512
        E = 16
        K = 2
        B, T = (2, 512)
        Bq, Tq, Hq = x.shape
        nt = Bq * Tq
        x_flat = x.reshape(nt, Hq)
        gate_logits = x_flat @ Wg.T
        gate_probs = jax.nn.softmax(gate_logits, axis=-1)
        topk_vals, topk_idx = jax.lax.top_k(gate_probs, K)
        rows = jnp.arange(nt)[:, None]
        cw = jnp.zeros((nt, E), dtype=x.dtype).at[rows, topk_idx].add(topk_vals)
        y_flat = jnp.zeros_like(x_flat)
        for e in range(E):
            h = jax.nn.silu(x_flat @ W1[e].T)
            o = h @ W2[e].T
            y_flat = y_flat + cw[:, e:e + 1] * o
        return y_flat.reshape(Bq, Tq, Hq)

    def _L1_xattn_ref(queries, keys, values, Wq, bq, Wk, bk, Wv, bv, Wo, bo):
        import jax, jax.numpy as jnp
        import numpy as np
        import math
        D_MODEL = 256
        N_HEADS = 16
        N, L, _ = queries.shape
        S = keys.shape[1]
        H = N_HEADS
        q = (queries @ Wq.T + bq).reshape(N, L, H, -1)
        k = (keys @ Wk.T + bk).reshape(N, S, H, -1)
        v = (values @ Wv.T + bv).reshape(N, S, H, -1)
        D = k.shape[-1]
        sm = jnp.einsum('nlhd,nshd->nlhs', q, k) / math.sqrt(D)
        causal_mask = jnp.triu(jnp.ones((L, S), dtype=bool), k=1)
        sm = jnp.where(causal_mask[None, :, None, :], -jnp.inf, sm)
        sm = jax.nn.softmax(sm, axis=-1)
        attn = jnp.einsum('nlhs,nshd->nlhd', sm, v)
        new_values = attn.reshape(N, L, H * D)
        return new_values @ Wo.T + bo

    def _L1_ffn_ref(x, w_gate, w_up, w_down):
        import jax, jax.numpy as jnp
        import numpy as np
        BLOCK = 32
        W_BITS = 4
        ACT_BITS = 16

        def act_qdq(x):
            qmax = 2.0 ** (ACT_BITS - 1) - 1.0
            scale = jnp.maximum(jnp.max(jnp.abs(x)) / qmax, 1e-12)
            return jnp.clip(jnp.round(x / scale), -qmax - 1.0, qmax) * scale

        def fixed_qdq_u16(x):
            scale = 1.0 / 65536.0
            return jnp.clip(jnp.round(x / scale), 0.0, 65535.0) * scale

        def lpbq_dequant(w):
            O, I = w.shape
            qmax = 2.0 ** (W_BITS - 1) - 1.0
            wb = w.reshape(O, I // BLOCK, BLOCK)
            s = jnp.maximum(jnp.max(jnp.abs(wb), axis=-1, keepdims=True) / qmax, 1e-12)
            wq = jnp.clip(jnp.round(wb / s), -qmax - 1.0, qmax) * s
            return wq.reshape(O, I)
        x = act_qdq(x)
        up = act_qdq(x @ lpbq_dequant(w_up).T)
        gate = act_qdq(x @ lpbq_dequant(w_gate).T)
        sig = fixed_qdq_u16(jax.nn.sigmoid(gate))
        gate = act_qdq(gate * sig)
        o = act_qdq(gate * up)
        return o @ lpbq_dequant(w_down).T

    def _L2_xattn_ref(x, latents, g1, b1, g2, b2, Wq, Wkv, Wout):
        import jax, jax.numpy as jnp
        import numpy as np
        DIM = 256
        HEADS = 16
        DIM_HEAD = 64
        INNER = HEADS * DIM_HEAD
        EPS = 1e-05

        def layer_norm(x, gamma, beta):
            mu = jnp.mean(x, axis=-1, keepdims=True)
            var = jnp.mean(jnp.square(x - mu), axis=-1, keepdims=True)
            return (x - mu) * jax.lax.rsqrt(var + EPS) * gamma + beta
        b, l, _ = latents.shape
        xn = layer_norm(x, g1, b1)
        ln = layer_norm(latents, g2, b2)
        q = ln @ Wq
        kv_input = jnp.concatenate([xn, ln], axis=1)
        kv = kv_input @ Wkv
        k, v = jnp.split(kv, 2, axis=-1)

        def heads(t):
            return t.reshape(t.shape[0], t.shape[1], HEADS, DIM_HEAD).transpose(0, 2, 1, 3)
        q, k, v = (heads(q), heads(k), heads(v))
        scale = 1.0 / np.sqrt(np.sqrt(DIM_HEAD))
        logits = jnp.einsum('bhqd,bhkd->bhqk', q * scale, k * scale)
        w = jax.nn.softmax(logits.astype(jnp.float32), axis=-1).astype(logits.dtype)
        out = jnp.einsum('bhqk,bhkd->bhqd', w, v)
        out = out.transpose(0, 2, 1, 3).reshape(b, l, INNER)
        return out @ Wout

    def _L2_ffn_ref(x, expert_tokens, W1, b1, W2, b2, W3, b3):
        import jax, jax.numpy as jnp
        import numpy as np
        D_MODEL = 256
        D_HIDDEN = 1024
        NUM_EXPERT = 8
        TOP_K = 2
        B, N = (1, 2048)

        def _expert_mlp(x, W1, b1, W2, b2, W3, b3):
            h = jax.nn.gelu(jnp.einsum('bnd,dh->bnh', x, W1) + b1, approximate=False)
            h = jax.nn.gelu(jnp.einsum('bnh,hk->bnk', h, W2) + b2, approximate=False)
            return jnp.einsum('bnh,hd->bnd', h, W3) + b3
        scores = jnp.einsum('bnd,ed->bne', x, expert_tokens)
        _, topk_idx = jax.lax.top_k(scores, TOP_K)
        outputs = jnp.zeros_like(x)
        num_expert = W1.shape[0]
        for i in range(num_expert):
            w = jnp.mean((topk_idx == i).astype(x.dtype), axis=-1, keepdims=True)
            y = _expert_mlp(x, W1[i], b1[i], W2[i], b2[i], W3[i], b3[i])
            outputs = outputs + y * w
        return outputs

    def _L3_xattn_ref(slots, P, Wq, Wk, Wv, gru_wih, gru_whh, gru_bih, gru_bhh, slot_norm_w, input_norm_w):
        import jax, jax.numpy as jnp
        import numpy as np
        D = 256
        NUM_ITERS = 3
        EPS = 1e-06
        SCALE = D ** (-0.5)

        def rmsnorm(x, w, eps=EPS):
            return x * jax.lax.rsqrt(jnp.mean(x * x, axis=-1, keepdims=True) + eps) * w

        def gru_cell(x, h, wih, whh, bih, bhh):
            gx = x @ wih.T + bih
            gh = h @ whh.T + bhh
            xr, xz, xn = jnp.split(gx, 3, axis=-1)
            hr, hz, hn = jnp.split(gh, 3, axis=-1)
            r = jax.nn.sigmoid(xr + hr)
            z = jax.nn.sigmoid(xz + hz)
            n = jnp.tanh(xn + r * hn)
            return (1.0 - z) * n + z * h
        Pn = rmsnorm(P, input_norm_w)
        k_proj = Pn @ Wk.T
        v_proj = Pn @ Wv.T
        for _ in range(NUM_ITERS):
            sn = rmsnorm(slots, slot_norm_w)
            q_proj = sn @ Wq.T
            scores = jnp.einsum('bkd,bmd->bkm', q_proj, k_proj) * SCALE
            attn = jax.nn.softmax(scores, axis=-2)
            attn = attn / (jnp.sum(attn, axis=-1, keepdims=True) + EPS)
            updates = jnp.einsum('bkm,bmd->bkd', attn, v_proj)
            slots = gru_cell(updates, slots, gru_wih, gru_whh, gru_bih, gru_bhh)
        return slots

    def _L3_ffn_ref(x, signatures_raw, knot_values, temperature, compress_w1, compress_b1, compress_w2, compress_b2, spline_w1, spline_b1, spline_w2, spline_b2, directions, norm_gamma, norm_beta, output_scale):
        import jax, jax.numpy as jnp
        import numpy as np
        D_MODEL = 256
        NUM_TILES = 64
        TPC = 8
        NUM_CLUSTERS = NUM_TILES // TPC
        GRID = 16
        COMP_H = 64
        NUM_KNOTS = 8
        EPS_LN = 1e-05

        def _calibrate(scores, knots, temperature):
            K = knots.shape[0]
            normalized = jax.nn.sigmoid(scores / (temperature[0] + 1e-06))
            idx_float = normalized * (K - 1)
            idx_low = jnp.clip(idx_float.astype(jnp.int32), 0, K - 2)
            idx_high = idx_low + 1
            t = idx_float - idx_low.astype(scores.dtype)
            val_low = knots[idx_low]
            val_high = knots[idx_high]
            return val_low + t * (val_high - val_low)

        def _forward(x, signatures_raw, knot_values, temperature, compress_w1, compress_b1, compress_w2, compress_b2, spline_w1, spline_b1, spline_w2, spline_b2, directions, norm_gamma, norm_beta, output_scale):
            B, T, D = x.shape
            xf = x.reshape(-1, D)
            q = jnp.where(signatures_raw > 0.3, 1.0, jnp.where(signatures_raw < -0.3, -1.0, 0.0)).astype(signatures_raw.dtype)
            sigs = signatures_raw + jax.lax.stop_gradient(q - signatures_raw)
            cluster_sigs = jnp.sign(sigs.reshape(NUM_CLUSTERS, TPC, D).mean(axis=1))
            cluster_scores = xf @ cluster_sigs.T
            cluster_gates = _calibrate(cluster_scores, knot_values, temperature)
            cluster_idx = jnp.argmax(cluster_gates, axis=-1)
            tile_scores = xf @ sigs.T
            tile_gates = _calibrate(tile_scores, knot_values, temperature)
            gates_by_cluster = tile_gates.reshape(-1, NUM_CLUSTERS, TPC)
            sel_gates = jnp.take_along_axis(gates_by_cluster, cluster_idx[:, None, None], axis=1)[:, 0, :]
            local_idx = jnp.argmax(sel_gates, axis=-1)
            tile_idx = cluster_idx * TPC + local_idx
            h = jax.nn.gelu(xf @ compress_w1 + compress_b1, approximate=False)
            comp = jnp.tanh(h @ compress_w2 + compress_b2)
            w1 = spline_w1[tile_idx]
            b1 = spline_b1[tile_idx]
            hh = jax.nn.relu(jnp.einsum('ni,nig->ng', comp, w1) + b1)
            w2 = spline_w2[tile_idx]
            b2 = spline_b2[tile_idx]
            mag = jnp.einsum('ng,ngo->no', hh, w2) + b2
            ffn_out = mag * directions[tile_idx] * output_scale[0]
            y = xf + ffn_out
            mu = y.mean(axis=-1, keepdims=True)
            var = ((y - mu) ** 2).mean(axis=-1, keepdims=True)
            y = (y - mu) / jnp.sqrt(var + EPS_LN) * norm_gamma + norm_beta
            return y.reshape(B, T, D)
        return _forward(x, signatures_raw, knot_values, temperature, compress_w1, compress_b1, compress_w2, compress_b2, spline_w1, spline_b1, spline_w2, spline_b2, directions, norm_gamma, norm_beta, output_scale)
    x = x + _L0_xattn_ref(ctx_1024, _layernorm(x, axis=-1), mask_BxS2_bk0, L0_xattn_ln_x_g, L0_xattn_ln_x_b, L0_xattn_ln_l_g, L0_xattn_ln_l_b, L0_xattn_Wq, L0_xattn_Wkv, L0_xattn_Wout, L0_xattn_ln_o_g, L0_xattn_ln_o_b)
    x = x + _L0_ffn_ref(_layernorm(x, axis=-1), L0_ffn_Wg, L0_ffn_W1, L0_ffn_W2)
    x = x + _L1_xattn_ref(_layernorm(x, axis=-1), ctx_1024, ctx_1024, L1_xattn_Wq, L1_xattn_bq, L1_xattn_Wk, L1_xattn_bk, L1_xattn_Wv, L1_xattn_bv, L1_xattn_Wo, L1_xattn_bo)
    x = x + _L1_ffn_ref(_layernorm(x, axis=-1), L1_ffn_w_gate, L1_ffn_w_up, L1_ffn_w_down)
    x = x + _L2_xattn_ref(ctx_1024, _layernorm(x, axis=-1), L2_xattn_g1, L2_xattn_b1, L2_xattn_g2, L2_xattn_b2, L2_xattn_Wq, L2_xattn_Wkv, L2_xattn_Wout)
    x = x + _L2_ffn_ref(_layernorm(x, axis=-1), L2_ffn_expert_tokens, L2_ffn_W1, L2_ffn_b1, L2_ffn_W2, L2_ffn_b2, L2_ffn_W3, L2_ffn_b3)
    x = x + _L3_xattn_ref(_layernorm(x, axis=-1), ctx_1024, L3_xattn_Wq, L3_xattn_Wk, L3_xattn_Wv, L3_xattn_gru_wih, L3_xattn_gru_whh, L3_xattn_gru_bih, L3_xattn_gru_bhh, L3_xattn_slot_norm_w, L3_xattn_input_norm_w)
    x = x + _L3_ffn_ref(_layernorm(x, axis=-1), L3_ffn_signatures_raw, L3_ffn_knot_values, L3_ffn_temperature, L3_ffn_compress_w1, L3_ffn_compress_b1, L3_ffn_compress_w2, L3_ffn_compress_b2, L3_ffn_spline_w1, L3_ffn_spline_b1, L3_ffn_spline_w2, L3_ffn_spline_b2, L3_ffn_directions, L3_ffn_norm_gamma, L3_ffn_norm_beta, L3_ffn_output_scale)
    return x

_drawn_inputs = setup_inputs


def setup_inputs(seed=0):
    import zlib

    import numpy as np

    out = dict(_drawn_inputs(seed))
    spreads = {'L0_xattn_ln_x_g': (1.0, 0.2),
     'L0_xattn_ln_x_b': (0.0, 0.1),
     'L0_xattn_ln_l_g': (1.0, 0.2),
     'L0_xattn_ln_l_b': (0.0, 0.1),
     'L0_xattn_ln_o_g': (1.0, 0.2),
     'L0_xattn_ln_o_b': (0.0, 0.1),
     'L2_xattn_g1': (1.0, 0.2),
     'L2_xattn_b1': (0.0, 0.1),
     'L2_xattn_g2': (1.0, 0.2),
     'L2_xattn_b2': (0.0, 0.1),
     'L2_ffn_b1': (0.0, 0.44),
     'L2_ffn_b2': (0.0, 0.302),
     'L2_ffn_b3': (0.0, 0.1),
     'L3_xattn_gru_bih': (0.0, 0.1),
     'L3_xattn_gru_bhh': (0.0, 0.349),
     'L3_xattn_slot_norm_w': (1.0, 0.6),
     'L3_xattn_input_norm_w': (1.0, 0.2),
     'L3_ffn_compress_b1': (0.0, 0.8),
     'L3_ffn_compress_b2': (0.0, 2.0),
     'L3_ffn_spline_b1': (0.0, 2.0),
     'L3_ffn_spline_b2': (0.0, 2.0),
     'L3_ffn_norm_gamma': (1.0, 0.2),
     'L3_ffn_norm_beta': (0.0, 0.1)}
    factors = {'L0_ffn_Wg': 4.711,
     'L0_ffn_W1': 3.607,
     'L0_ffn_W2': 3.901,
     'L1_xattn_bk': 64.0,
     'L3_ffn_signatures_raw': 8.0,
     'L3_ffn_knot_values': 8.0,
     'L3_ffn_compress_w1': 8.0,
     'L3_ffn_compress_w2': 8.0,
     'L3_ffn_spline_w1': 8.0,
     'L3_ffn_spline_w2': 8.0,
     'L3_ffn_directions': 8.0}
    for name, (base, spread) in spreads.items():
        noise = np.random.default_rng([zlib.crc32(name.encode()), seed]).standard_normal(out[name].shape)
        drawn = base * np.exp(spread * noise) if base else spread * noise
        out[name] = jnp.asarray(drawn.astype(out[name].dtype))
    for name, factor in factors.items():
        out[name] = (out[name] * factor).astype(out[name].dtype)
    return out
```

```python
from contextlib import ExitStack

import concourse.bass as bass
from concourse import mybir

F32 = mybir.dt.float32
U8 = mybir.dt.uint8
ALU = mybir.AluOpType
ACT = mybir.ActivationFunctionType
AX = mybir.AxisListType

B = 8
T = 112
S = 375
D = 256
P = 128
DC = D // P
N = B * T
HALF = N // 2
HB = B // 2
SC = 3
SP_ = S // SC
LN_EPS = 1e-5
BIG = 3.0e38
ROUND = 12582912.0


class Link:

    def __init__(self, eng, sem):
        self.eng, self.sem, self.count, self.base = eng, sem, 0, None

    def __call__(self, ins):
        ins.then_inc(self.sem, 1)
        self.count += 1
        self.eng.wait_ge(self.sem, self.count if self.base is None else self.base + self.count)


class Core:

    def __init__(self, nc, ctx):
        def sb(name, shape, dt=F32):
            return ctx.enter_context(nc.sbuf_tensor(name, shape, dt))

        self.nc = nc
        self.sems = []
        self.x = sb("x_sb", [T, B, D])
        self.xn = sb("xn_sb", [T, B, D])
        self.xnT = sb("xnT_sb", [P, DC, N])
        self.ident = sb("ident", [P, P])
        self.stats = sb("stats", [T, B, 6])
        self.moments = sb("moments", [T, B, 2])
        self.std = sb("std", [T, B])
        self.rstd = sb("rstd", [T, B])
        self.bank = [ctx.enter_context(nc.psum_tensor(f"bank{i}", [P, 512], F32)) for i in range(8)]

    def sem(self, name):
        self.sems.append(self.nc.alloc_semaphore(name))
        return self.sems[-1]

    def recycle(self):
        self.nc.clear_and_free_semaphores(self.sems)
        self.nc.all_engine_barrier()
        self.sems = []


def layer_norm_rows(core, link, act_turn, dve, src, dst, sem_var, sem_std):
    nc = core.nc
    for b in range(B):
        last = nc.vector.bn_stats(core.stats[:, b, :], src[:, b, :])
    link(last)
    for b in range(B):
        last = nc.vector.bn_aggr(core.moments[:, b, :], core.stats[:, b, :])
    link(last)
    nc.vector.tensor_scalar(core.std[:, :], core.moments[:, :, 1], LN_EPS, None, ALU.add).then_inc(sem_var, 1)
    dve.wait_ge(sem_std, act_turn)
    link(nc.vector.reciprocal(core.rstd[:, :], core.std[:, :]))
    for b in range(B):
        last = nc.vector.tensor_scalar(dst[:, b, :], src[:, b, :], core.moments[:, b, 0:1],
                                       core.rstd[:, b:b + 1], ALU.subtract, ALU.mult)
    link(last)


def root_step(core, act, turn, sem_var, sem_std):
    act.wait_ge(sem_var, turn)
    core.nc.scalar.activation(core.std[:, :], core.std[:, :], ACT.Sqrt).then_inc(sem_std, 1)


def transpose_rows(core, pe, src, banks, sem_done):
    for c in range(DC):
        for half in range(2):
            for q in range(HB):
                ins = pe.transpose(core.bank[banks[2 * c + half]][:, q * T:(q + 1) * T],
                                   src[:, half * HB + q, c * P:(c + 1) * P], core.ident[0:T, 0:T])
            ins.then_inc(sem_done, 1)


def setup(nc, core, a):
    with ExitStack() as ctx:
        sem = lambda n: core.sem(n)
        x_loaded, zeroed, ident_made = sem("setup_x_loaded"), sem("setup_zeroed"), sem("setup_ident")
        block = ctx.enter_context(nc.Block())

        @block.sync
        def _(sp):
            sp.dma_start(core.x[:, :, :], a["x"]).then_inc(x_loaded, 16)
            sp.wait_ge(x_loaded, 16)

        @block.gpsimd
        def _(pool):
            nc.gpsimd.memset(core.ident[:, :], 0.0).then_inc(zeroed, 1)
            pool.wait_ge(zeroed, 1)
            nc.gpsimd.affine_select(out=core.ident[:, :], in_=core.ident[:, :], compare_op=ALU.not_equal,
                                    fill=1.0, base=0, pattern=[[-1, P]], channel_multiplier=1
                                    ).then_inc(ident_made, 1)
            pool.wait_ge(ident_made, 1)


def context_norm(nc, core, a, ctx_zT):
    with ExitStack() as ctx:
        sb = lambda n, s, dt=F32: ctx.enter_context(nc.sbuf_tensor(n, s, dt))
        sem = lambda n: core.sem(n)
        NT = B * SC
        rows = sb("cn_rows", [SP_, NT, D])
        stats = sb("cn_stats", [SP_, NT, 6])
        mom = sb("cn_mom", [SP_, NT, 2])
        std = sb("cn_std", [SP_, NT])
        rstd = sb("cn_rstd", [SP_, NT])
        loaded = [sem(f"cn_loaded{i}") for i in range(2)]
        order, var_ready, std_ready = sem("cn_order"), sem("cn_var"), sem("cn_std_ready")
        z_ready, turned, taken = sem("cn_z_ready"), sem("cn_turned"), sem("cn_taken")
        block = ctx.enter_context(nc.Block())

        @block.sync
        def _(sp):
            for i in range(2):
                h = slice(i * NT // 2, (i + 1) * NT // 2)
                sp.dma_start(rows[:, h, :], a["ctx_rows"][:, h, :]).then_inc(loaded[i], 16)

        @block.vector
        def _(dve):
            link = Link(dve, order)
            for t in range(NT):
                if t % (NT // 2) == 0:
                    dve.wait_ge(loaded[t // (NT // 2)], 16)
                last = nc.vector.bn_stats(stats[:, t, :], rows[:, t, :])
            link(last)
            for t in range(NT):
                last = nc.vector.bn_aggr(mom[:, t, :], stats[:, t, :])
            link(last)
            nc.vector.tensor_scalar(std[:, :], mom[:, :, 1], LN_EPS, None, ALU.add).then_inc(var_ready, 1)
            dve.wait_ge(std_ready, 1)
            link(nc.vector.reciprocal(rstd[:, :], std[:, :]))
            for t in range(NT):
                nc.vector.tensor_scalar(rows[:, t, :], rows[:, t, :], mom[:, t, 0:1], rstd[:, t:t + 1],
                                        ALU.subtract, ALU.mult).then_inc(z_ready, 1)
                if t % SC == SC - 1 and t >= 2 * SC - 1:
                    g = t // SC - 1
                    dve.wait_ge(turned, 2 * g + 1)
                    nc.vector.tensor_copy(ctx_zT[:, 0, g * S:(g + 1) * S],
                                          core.bank[(2 * g) % 4][:, 0:S]).then_inc(taken, 1)
            dve.wait_ge(turned, 2 * B - 1)
            nc.vector.tensor_copy(ctx_zT[:, 0, (B - 1) * S:B * S],
                                  core.bank[(2 * B - 2) % 4][:, 0:S]).then_inc(taken, 1)

        @block.scalar
        def _(act):
            act.wait_ge(var_ready, 1)
            nc.scalar.activation(std[:, :], std[:, :], ACT.Sqrt).then_inc(std_ready, 1)
            for g in range(B):
                act.wait_ge(turned, 2 * g + 2)
                nc.scalar.activation(ctx_zT[:, 1, g * S:(g + 1) * S], core.bank[(2 * g + 1) % 4][:, 0:S],
                                     ACT.Copy).then_inc(std_ready, 1)

        @block.tensor
        def _(pe):
            for g in range(B):
                pe.wait_ge(z_ready, SC * (g + 1))
                for c in range(DC):
                    if g >= 2 and c == 0:
                        pe.wait_ge(taken, g - 1)
                    if g >= 2 and c == 1:
                        pe.wait_ge(std_ready, g)
                    for k in range(SC):
                        ins = pe.transpose(core.bank[(2 * g + c) % 4][:, k * SP_:(k + 1) * SP_],
                                           rows[:, g * SC + k, c * P:(c + 1) * P], core.ident[0:SP_, 0:SP_])
                    ins.then_inc(turned, 1)


def latent_attention(nc, core, a, ctx_zT, L, masked):
    H, HD = 16, 64
    INNER = H * HD
    KEYS = S + T
    KC = 4
    KL = [min(P, KEYS - k * P) for k in range(KC)]
    JC = INNER // P
    with ExitStack() as ctx:
        sb = lambda n, s, dt=F32: ctx.enter_context(nc.sbuf_tensor(f"{L}_{n}", s, dt))
        sem = lambda n: core.sem(f"{L}_{n}")
        wq, wkv = sb("wq", [P, DC, INNER]), sb("wkv", [P, DC, 2 * INNER])
        wout = sb("wout", [P, JC, D])
        gains = sb("gains", [P, 4, DC])
        kvT = sb("kvT", [P, DC, KEYS])
        qT, kT = sb("qT", [P, JC, T]), sb("kT", [P, JC, KEYS])
        v = sb("v", [P, KC, INNER])
        probs = sb("probs", [T, 2, KEYS])
        probsT = sb("probsT", [P, 2, KC, T])
        peak, npeak, total = sb("peak", [T, H]), sb("npeak", [T, H]), sb("total", [T, H])
        rtotal = sb("rtotal", [T, H])
        heads, headsT = sb("heads", [T, INNER]), sb("headsT", [P, JC, T])
        if masked:
            mask_u8 = sb("mask_u8", [T, B, S], U8)
            bias = sb("bias", [T, 2, KEYS])
            masked_s = sb("masked_s", [T, 2, KEYS])
            gain_o, off_o = sb("gain_o", [T, D]), sb("off_o", [T, D])
            raw = sb("raw", [T, B, D])
            carrier = sb("carrier", [T, 1])
        w_loaded, small_loaded = sem("w_loaded"), sem("small_loaded")
        dve_order, var_ready, std_ready = sem("dve_order"), sem("var_ready"), sem("std_ready")
        turned, latents_ready, kv_ready = sem("turned"), sem("latents_ready"), sem("kv_ready")
        proj_done, qk_taken, v_taken = sem("proj_done"), sem("qk_taken"), sem("v_taken")
        scores_done, peak_ready, exp_done = sem("scores_done"), sem("peak_ready"), sem("exp_done")
        probs_turned, probsT_ready, pv_done = sem("probs_turned"), sem("probsT_ready"), sem("pv_done")
        heads_ready, heads_turned, headsT_ready = sem("heads_ready"), sem("heads_turned"), sem("headsT_ready")
        out_done, out_taken = sem("out_done"), sem("out_taken")
        QG, KG, VG = 2, JC, 2 * KC
        G = QG + KG + VG
        NORMS = 2
        block = ctx.enter_context(nc.Block())

        @block.sync
        def _(sp):
            sp.dma_start(gains[:, :, :], a[f"{L}_gains"]).then_inc(small_loaded, 16)
            n_small = 1
            if masked:
                sp.dma_start(mask_u8[:, :, :], a["mask"]).then_inc(small_loaded, 16)
                sp.dma_start(gain_o[:, :], a[f"{L}_gain_o"]).then_inc(small_loaded, 16)
                sp.dma_start(off_o[:, :], a[f"{L}_off_o"]).then_inc(small_loaded, 16)
            sp.dma_start(wq[:, :, :], a[f"{L}_wq"]).then_inc(w_loaded, 16)
            sp.dma_start(wkv[:, :, :], a[f"{L}_wkv"]).then_inc(w_loaded, 16)
            sp.dma_start(wout[:, :, :], a[f"{L}_wout"]).then_inc(w_loaded, 16)

        @block.vector
        def _(dve):
            link = Link(dve, dve_order)
            layer_norm_rows(core, link, 1, dve, core.x, core.xn, var_ready, std_ready)
            layer_norm_rows(core, link, 2, dve, core.xn, core.xn, var_ready, std_ready)
            dve.wait_ge(small_loaded, 64 if masked else 16)
            for c in range(DC):
                for half in range(2):
                    dve.wait_ge(turned, 2 * c + half + 1)
                    last = nc.vector.tensor_scalar(
                        core.xnT[:, c, half * HALF:(half + 1) * HALF], core.bank[2 * c + half][:, 0:HALF],
                        gains[:, 2, c:c + 1], gains[:, 3, c:c + 1], ALU.mult, ALU.add)
            link(last)
            if masked:
                link(nc.vector.memset(bias[:, :, :], 0.0))

            def prepare(b):
                for c in range(DC):
                    nc.vector.tensor_scalar(kvT[:, c, 0:S], ctx_zT[:, c, bass.ds(b * S, S)],
                                            gains[:, 0, c:c + 1], gains[:, 1, c:c + 1],
                                            ALU.mult, ALU.add).then_inc(kv_ready, 1)
                nc.vector.tensor_copy(kvT[:, :, S:KEYS], core.xnT[:, :, bass.ds(b * T, T)]).then_inc(kv_ready, 1)

            def mask_bias(b, slot):
                link(nc.vector.tensor_scalar(bias[:, slot, 0:S], mask_u8[:, b, :], -1.0, BIG,
                                             ALU.add, ALU.mult))

            prepare(0)

            def batch(b, last_batch):
                if masked:
                    mask_bias(b, 0)
                for n in range(VG):
                    dve.wait_ge(proj_done, b * G + QG + KG + n + 1)
                    nc.vector.tensor_copy(v[0:KL[n // 2], n // 2, (n % 2) * 512:(n % 2 + 1) * 512],
                                          core.bank[(QG + KG + n) % 4][0:KL[n // 2], :]).then_inc(v_taken, 1)

                def find_peak(h):
                    dve.wait_ge(scores_done, b * H + h + 1)
                    src = core.bank[h % 2][0:T, 0:KEYS]
                    if masked:
                        if h >= 2:
                            dve.wait_ge(exp_done, b * H + h - 1)
                        nc.vector.memset(carrier[:, :], 0.0)
                        link(nc.vector.tensor_tensor_reduce(masked_s[:, h % 2, :], src, bias[:, 0, :], 1.0,
                                                            -BIG, ALU.add, ALU.max, peak[:, h:h + 1]))
                        nc.vector.tensor_scalar(npeak[:, h:h + 1], peak[:, h:h + 1], -1.0, None,
                                                ALU.mult).then_inc(peak_ready, 1)
                    else:
                        nc.vector.tensor_reduce(npeak[:, h:h + 1], src, AX.X, ALU.max,
                                                negate=True).then_inc(peak_ready, 1)

                find_peak(0)
                for h in range(H):
                    if h + 1 < H:
                        find_peak(h + 1)
                    dve.wait_ge(probs_turned, b * H + h + 1)
                    if h >= 2:
                        dve.wait_ge(pv_done, b * H + h - 1)
                    src = core.bank[2 + h % 2]
                    nc.vector.tensor_copy(
                        probsT[:, h % 2, 0:KC - 1, :],
                        src[:, 0:(KC - 1) * T].rearrange("p (k t) -> p k t", t=T)).then_inc(probsT_ready, 1)
                    nc.vector.tensor_copy(probsT[0:KL[-1], h % 2, KC - 1, :],
                                          src[0:KL[-1], (KC - 1) * T:KC * T]).then_inc(probsT_ready, 1)
                    if h == 4 and not last_batch:
                        prepare(b + 1)
                dve.wait_ge(exp_done, b * H + H)
                link(nc.vector.reciprocal(rtotal[:, :], total[:, :]))
                dve.wait_ge(pv_done, b * H + H)
                for g in range(2):
                    nc.vector.tensor_tensor(
                        heads[:, g * 512:(g + 1) * 512].rearrange("p (h d) -> p h d", d=HD),
                        core.bank[4 + g][0:T, :].rearrange("p (h d) -> p h d", d=HD),
                        rtotal[:, g * 8:(g + 1) * 8].unsqueeze(2).broadcast_to([T, 8, HD]),
                        ALU.mult).then_inc(heads_ready, 1)
                dve.wait_ge(out_done, b + 1)
                if masked:
                    nc.vector.tensor_copy(raw[:, b, :], core.bank[7][0:T, 0:D]).then_inc(out_taken, 1)
                else:
                    nc.vector.tensor_tensor(core.x[:, b, :], core.x[:, b, :], core.bank[7][0:T, 0:D],
                                            ALU.add).then_inc(out_taken, 1)

            per_batch = (1 + H if masked else 0) + 1
            start = link.count
            with dve.Fori(0, B - 1) as b:
                link.base = b * per_batch
                batch(b, False)
                assert link.count == start + per_batch
            link.base, link.count = None, start + (B - 1) * per_batch
            batch(B - 1, True)
            if masked:
                dve.wait_ge(out_taken, B)
                layer_norm_rows(core, link, NORMS + 1, dve, raw, raw, var_ready, std_ready)
                for b in range(B):
                    last = nc.vector.tensor_tensor(raw[:, b, :], raw[:, b, :], gain_o[:, :], ALU.mult)
                link(last)
                for b in range(B):
                    last = nc.vector.tensor_tensor(raw[:, b, :], raw[:, b, :], off_o[:, :], ALU.add)
                link(last)
                nc.vector.tensor_tensor(core.x[:, :, :], core.x[:, :, :], raw[:, :, :], ALU.add)

        @block.scalar
        def _(act):
            for n in range(NORMS):
                root_step(core, act, n + 1, var_ready, std_ready)

            def batch(b):
                for g in range(QG):
                    act.wait_ge(proj_done, b * G + g + 1)
                    nc.scalar.activation(qT[:, 4 * g:4 * g + 4, :],
                                         core.bank[g][:, 0:4 * T].rearrange("p (j t) -> p j t", t=T),
                                         ACT.Copy, scale=HD ** -0.5).then_inc(qk_taken, 1)
                for j in range(JC):
                    act.wait_ge(proj_done, b * G + QG + j + 1)
                    nc.scalar.activation(kT[:, j, :], core.bank[(QG + j) % 4][:, 0:KEYS],
                                         ACT.Copy).then_inc(qk_taken, 1)
                for h in range(H):
                    act.wait_ge(peak_ready, b * H + h + 1)
                    if h >= 2:
                        act.wait_ge(probs_turned, b * H + h - 1)
                    src = masked_s[:, h % 2, :] if masked else core.bank[h % 2][0:T, 0:KEYS]
                    nc.scalar.activation(probs[:, h % 2, :], src, ACT.Exp, bias=npeak[:, h:h + 1],
                                         accum_out=total[:, h:h + 1]).then_inc(exp_done, 1)
                for g in range(2):
                    act.wait_ge(heads_turned, b * 2 + g + 1)
                    nc.scalar.activation(headsT[:, 4 * g:4 * g + 4, :],
                                         core.bank[6][:, 0:4 * T].rearrange("p (j t) -> p j t", t=T),
                                         ACT.Copy).then_inc(headsT_ready, 1)

            with act.Fori(0, B - 1) as b:
                batch(b)
            batch(B - 1)
            if masked:
                root_step(core, act, NORMS + 1, var_ready, std_ready)

        @block.tensor
        def _(pe):
            pe.wait_ge(dve_order, 8)
            transpose_rows(core, pe, core.xn, [0, 1, 2, 3], turned)
            pe.wait_ge(w_loaded, 48)

            def batch(b):
                pe.wait_ge(kv_ready, b * 3 + 3)
                for g in range(QG):
                    for j in range(4 * g, 4 * g + 4):
                        for c in range(DC):
                            ins = pe.matmul(core.bank[g][:, (j % 4) * T:(j % 4 + 1) * T],
                                            wq[:, c, j * P:(j + 1) * P], kvT[:, c, S:KEYS],
                                            start=(c == 0), stop=(c == DC - 1))
                    ins.then_inc(proj_done, 1)
                for j in range(JC):
                    n = QG + j
                    if n >= 4:
                        pe.wait_ge(qk_taken, b * (QG + KG) + n - 3)
                    for c in range(DC):
                        ins = pe.matmul(core.bank[n % 4][:, 0:KEYS], wkv[:, c, j * P:(j + 1) * P],
                                        kvT[:, c, :], start=(c == 0), stop=(c == DC - 1))
                    ins.then_inc(proj_done, 1)
                for i in range(VG):
                    n = QG + KG + i
                    k, hf = i // 2, i % 2
                    if i < 4:
                        pe.wait_ge(qk_taken, b * (QG + KG) + n - 3)
                    else:
                        pe.wait_ge(v_taken, b * VG + i - 3)
                    for c in range(DC):
                        ins = pe.matmul(core.bank[n % 4][0:KL[k], :], kvT[:, c, k * P:k * P + KL[k]],
                                        wkv[:, c, INNER + hf * 512:INNER + (hf + 1) * 512],
                                        start=(c == 0), stop=(c == DC - 1))
                    ins.then_inc(proj_done, 1)
                pe.wait_ge(v_taken, b * VG + VG)

                def scores(h):
                    if h >= 2:
                        pe.wait_ge(peak_ready, b * H + h - 1)
                        if not masked:
                            pe.wait_ge(exp_done, b * H + h - 1)
                    r = slice((h % 2) * HD, (h % 2 + 1) * HD)
                    pe.matmul(core.bank[h % 2][0:T, 0:KEYS], qT[r, h // 2, :], kT[r, h // 2, :],
                              start=True, stop=True).then_inc(scores_done, 1)

                def values(h):
                    pe.wait_ge(probsT_ready, b * 2 * H + 2 * h + 2)
                    for k in range(KC):
                        ins = pe.matmul(core.bank[4 + h // 8][0:T, (h % 8) * HD:(h % 8 + 1) * HD],
                                        probsT[0:KL[k], h % 2, k, :],
                                        v[0:KL[k], k, h * HD:(h + 1) * HD],
                                        start=(k == 0), stop=(k == KC - 1))
                    ins.then_inc(pv_done, 1)

                scores(0)
                scores(1)
                for h in range(H):
                    pe.wait_ge(exp_done, b * H + h + 1)
                    if h >= 2:
                        pe.wait_ge(probsT_ready, b * 2 * H + 2 * h - 2)
                    for k in range(KC):
                        ins = pe.transpose(core.bank[2 + h % 2][0:KL[k], k * T:(k + 1) * T],
                                           probs[:, h % 2, k * P:k * P + KL[k]], core.ident[0:T, 0:T])
                    ins.then_inc(probs_turned, 1)
                    if h + 2 < H:
                        scores(h + 2)
                    if h >= 1:
                        values(h - 1)
                values(H - 1)
                pe.wait_ge(heads_ready, b * 2 + 2)
                for g in range(2):
                    if g == 1:
                        pe.wait_ge(headsT_ready, b * 2 + 1)
                    for j in range(4 * g, 4 * g + 4):
                        ins = pe.transpose(core.bank[6][:, (j % 4) * T:(j % 4 + 1) * T],
                                           heads[:, j * P:(j + 1) * P], core.ident[0:T, 0:T])
                    ins.then_inc(heads_turned, 1)
                pe.wait_ge(headsT_ready, b * 2 + 2)
                for j in range(JC):
                    ins = pe.matmul(core.bank[7][0:T, 0:D], headsT[:, j, :], wout[:, j, :],
                                    start=(j == 0), stop=(j == JC - 1))
                ins.then_inc(out_done, 1)

            with pe.Fori(0, B - 1) as b:
                batch(b)
            batch(B - 1)


def norm_to_features(core, pe, order, turned):
    pe.wait_ge(order, 4)
    transpose_rows(core, pe, core.xn, [0, 1, 2, 3], turned)


def take_features(core, dve, turned, xT_ready, first=1):
    for c in range(DC):
        for half in range(2):
            dve.wait_ge(turned, 2 * c + half + first)
            core.nc.vector.tensor_copy(core.xnT[:, c, half * HALF:(half + 1) * HALF],
                                       core.bank[2 * c + half][:, 0:HALF]).then_inc(xT_ready, 1)


def count_down(nc, pool, tile, E, sem):
    nc.gpsimd.iota(tile, pattern=[[0, B], [-1, E]], base=E, channel_multiplier=0,
                   allow_small_or_imprecise_dtypes=True).then_inc(sem, 1)


def top_two(nc, link, value, E, places, peak, rank, pick1, pick2, work):
    over = lambda t: t.unsqueeze(2).broadcast_to([T, B, E])
    for pick, src in ((pick1, value), (pick2, work)):
        link(nc.vector.tensor_reduce(peak[:, :], src[:, :, :], AX.X, ALU.max))
        link(nc.vector.tensor_tensor(pick[:, :, :], src[:, :, :], over(peak[:, :]), ALU.is_equal))
        link(nc.vector.tensor_tensor(pick[:, :, :], pick[:, :, :], places[:, :, :], ALU.mult))
        link(nc.vector.tensor_reduce(rank[:, :], pick[:, :, :], AX.X, ALU.max))
        link(nc.vector.tensor_tensor(pick[:, :, :], places[:, :, :], over(rank[:, :]), ALU.is_equal))
        if pick is pick1:
            link(nc.vector.tensor_scalar(work[:, :, :], pick1[:, :, :], -BIG, None, ALU.mult))
            link(nc.vector.tensor_tensor(work[:, :, :], work[:, :, :], value[:, :, :], ALU.add))


def routed_experts(nc, core, a, L, E, I, hidden, act_func, softmax):
    IC = I // P
    TILES = (2 * N - E) // P + E
    NBUF = 3
    ROUNDS = -(-TILES // NBUF)
    TILES = ROUNDS * NBUF
    MG = 2
    GR = IC // MG
    with ExitStack() as ctx:
        sb = lambda n, s, dt=F32: ctx.enter_context(nc.sbuf_tensor(f"{L}_{n}", s, dt))
        sem = lambda n: core.sem(f"{L}_{n}")
        gate = sb("gate", [P, DC, E])
        w_up, w_down = sb("w_up", [P, NBUF, DC, I]), sb("w_down", [P, NBUF, IC, D])
        offsets = hidden == 2
        if offsets:
            w_mid = sb("w_mid", [P, NBUF, IC, I])
            b_hid = sb("b_hid", [P, NBUF, 2, IC])
            b_down = sb("b_down", [P, NBUF, D])
        rows = sb("rows", [P, NBUF, D])
        rowsT = sb("rowsT", [P, DC, P])
        h1T = sb("h1T", [P, IC, P])
        h2T = sb("h2T", [P, IC, P]) if offsets else h1T
        result = sb("result", [P, NBUF, D])
        zeros = sb("zeros", [P, D])
        if offsets:
            got = w_mid[0:T, 0].rearrange("p k i -> p (k i)")[:, 0:2 * B * D].rearrange(
                "p (n b d) -> p n b d", n=2, b=B)
        else:
            got = sb("got", [T, 2, B, D])
        places, prob, work = sb("places", [T, B, E]), sb("prob", [T, B, E]), sb("work", [T, B, E])
        pick1, pick2, both = sb("pick1", [T, B, E]), sb("pick2", [T, B, E]), sb("both", [T, B, E])
        peak, rank, total = sb("peak", [T, B]), sb("rank", [T, B]), sb("total", [T, B])
        weight = sb("weight", [T, 2, B])
        earlier, ones = sb("earlier", [T, T]), sb("ones", [T, T])
        before, count = sb("before", [T, B, E]), sb("count", [T, E])
        tiles, first = sb("tiles", [T, E]), sb("first", [T, E])
        slot = sb("slot", [T, B, E])
        slot_f, slot_u = sb("slot_f", [T, 2, B]), sb("slot_u", [T, 2, B], mybir.dt.uint32)
        tile_no, owner = sb("tile_no", [1, TILES]), sb("owner", [1, TILES])
        owner_i = sb("owner_i", [1, TILES], mybir.dt.int32)
        sorted_rows = nc.dram_tensor(f"{L}_sorted_rows", ((TILES + 1) * P, D), F32).ap()
        sorted_out = nc.dram_tensor(f"{L}_sorted_out", (TILES * P, D), F32).ap()

        gate_loaded = sem("gate_loaded")
        w_loaded = [sem(f"w_loaded{i}") for i in range(NBUF)]
        x_loaded = [sem(f"x_loaded{i}") for i in range(NBUF)]
        dve_order, var_ready, std_ready, turned = sem("dve_order"), sem("var_ready"), sem("std_ready"), sem("turned")
        xT_ready, made, logits_done = sem("xT_ready"), sem("made"), sem("logits_done")
        shifted, exp_done = sem("shifted"), sem("exp_done")
        both_ready, prefix_done = sem("both_ready"), sem("prefix_done")
        slots_ready, owner_ready = sem("slots_ready"), sem("owner_ready")
        zero_made, zero_filled, scattered = sem("zero_made"), sem("zero_filled"), sem("scattered")
        rows_turned, rowsT_ready = sem("rows_turned"), sem("rowsT_ready")
        hid_done, h_ready, down_done, result_ready = sem("hid_done"), sem("h_ready"), sem("down_done"), sem("result_ready")
        stored = sem("stored")
        gathered = [sem(f"gathered{b}") for b in range(B)]
        W_DMAS = 5 if offsets else 2
        HG = hidden * GR
        DOWN = (4, 5, 7)
        block = ctx.enter_context(nc.Block())

        @block.sync
        def _(sp):
            sp.dma_start(gate[:, :, :], a[f"{L}_gate"]).then_inc(gate_loaded, 16)
            sp.wait_ge(zero_made, 1)
            sp.dma_start(sorted_rows.rearrange("(t p) d -> p t d", p=P),
                         zeros[:, :].unsqueeze(1).broadcast_to([P, TILES + 1, D])).then_inc(zero_filled, 16)

            def load_weights(tile, s):
                e = sp.value_load(owner_i[0:1, bass.ds(tile, 1)], min_val=0, max_val=E - 1)
                e = bass.ds(e, 1)
                sp.dma_start(w_up[:, s], a[f"{L}_w_up"][e][0]).then_inc(w_loaded[s], 16)
                if offsets:
                    sp.dma_start(b_hid[:, s], a[f"{L}_b_hid"][e][0]).then_inc(w_loaded[s], 16)
                    sp.dma_start(w_mid[:, s], a[f"{L}_w_mid"][e][0]).then_inc(w_loaded[s], 16)
                    sp.dma_start(b_down[:, s], a[f"{L}_b_down"][e][0]).then_inc(w_loaded[s], 16)
                sp.dma_start(w_down[:, s], a[f"{L}_w_down"][e][0]).then_inc(w_loaded[s], 16)

            def load_rows(tile, s):
                sp.dma_start(rows[:, s, :], sorted_rows[bass.ds(tile * P, P), :]).then_inc(x_loaded[s], 16)

            def store_result(tile, s):
                sp.wait_ge(result_ready, tile + 1)
                sp.dma_start(sorted_out[bass.ds(tile * P, P), :], result[:, s, :]).then_inc(stored, 16)

            sp.wait_ge(owner_ready, 1)
            for s in range(NBUF):
                load_weights(s, s)
            sp.wait_ge(scattered, 16 * 2 * B)
            for s in range(NBUF):
                load_rows(s, s)
            with sp.Fori(0, ROUNDS - 1) as r:
                for s in range(NBUF):
                    store_result(r * NBUF + s, s)
                    load_weights(r * NBUF + NBUF + s, s)
                    load_rows(r * NBUF + NBUF + s, s)
            for s in range(NBUF):
                if s == 0:
                    sp.wait_ge(down_done, TILES - NBUF + 1)
                    load_rows(TILES, 0)
                store_result(TILES - NBUF + s, s)

        @block.gpsimd
        def _(pool):
            nc.gpsimd.memset(zeros[:, :], 0.0).then_inc(zero_made, 1)
            count_down(nc, pool, places[:, :, :], E, made)
            nc.gpsimd.iota(tile_no[:, :], pattern=[[1, TILES]], base=0, channel_multiplier=0,
                           allow_small_or_imprecise_dtypes=True).then_inc(made, 1)
            nc.gpsimd.memset(ones[:, :], 1.0).then_inc(made, 1)
            pool.wait_ge(made, 3)
            nc.gpsimd.affine_select(out=earlier[:, :], in_=ones[:, :], compare_op=ALU.is_gt, fill=0.0, base=0,
                                    pattern=[[1, T]], channel_multiplier=-1).then_inc(made, 1)
            pool.wait_ge(zero_filled, 16)
            pool.wait_ge(slots_ready, 1)
            for n in range(2):
                for b in range(B):
                    nc.gpsimd.indirect_dma_start(
                        out=sorted_rows, out_offset=bass.IndirectOffsetOnAxis(slot_u[:, n, b:b + 1], 0),
                        in_=core.xn[:, b, :], in_offset=None).then_inc(scattered, 16)
            pool.wait_ge(stored, 16 * (NBUF + TILES))
            for b in range(B):
                for n in range(2):
                    nc.gpsimd.indirect_dma_start(
                        out=got[:, n, b, :], out_offset=None, in_=sorted_out,
                        in_offset=bass.IndirectOffsetOnAxis(slot_u[:, n, b:b + 1], 0)).then_inc(gathered[b], 16)

        @block.vector
        def _(dve):
            link = Link(dve, dve_order)
            tt, ts, reduce = nc.vector.tensor_tensor, nc.vector.tensor_scalar, nc.vector.tensor_reduce
            layer_norm_rows(core, link, 1, dve, core.x, core.xn, var_ready, std_ready)
            take_features(core, dve, turned, xT_ready)
            dve.wait_ge(logits_done, 1)
            logits = core.bank[4][0:T, 0:B * E].rearrange("p (b e) -> p b e", e=E)
            over = lambda t: t.unsqueeze(2).broadcast_to([T, B, E])
            if softmax:
                link(reduce(peak[:, :], logits, AX.X, ALU.max))
                tt(prob[:, :, :], logits, over(peak[:, :]), ALU.subtract).then_inc(shifted, 1)
                dve.wait_ge(exp_done, 1)
                link(reduce(total[:, :], prob[:, :, :], AX.X, ALU.add))
                link(nc.vector.reciprocal(total[:, :], total[:, :]))
                link(tt(prob[:, :, :], prob[:, :, :], over(total[:, :]), ALU.mult))
            else:
                link(nc.vector.tensor_copy(prob[:, :, :], logits))
            dve.wait_ge(made, 4)
            top_two(nc, link, prob, E, places, peak, rank, pick1, pick2, work)
            tt(both[:, :, :], pick1[:, :, :], pick2[:, :, :], ALU.add).then_inc(both_ready, 1)
            if softmax:
                for n, pick in enumerate((pick1, pick2)):
                    link(tt(work[:, :, :], pick[:, :, :], prob[:, :, :], ALU.mult))
                    link(reduce(weight[:, n, :], work[:, :, :], AX.X, ALU.add))
            else:
                link(nc.vector.memset(weight[:, :, :], 0.5))
            dve.wait_ge(prefix_done, 1)
            sums = core.bank[5][0:T, 0:B * E].rearrange("p (b e) -> p b e", e=E)
            link(nc.vector.memset(before[:, 0, :], 0.0))
            for b in range(B):
                dst = before[:, b + 1, :] if b + 1 < B else count[:, :]
                link(tt(dst, before[:, b, :], sums[:, b, :], ALU.add))
            link(ts(tiles[:, :], count[:, :], 0.0, None, ALU.is_gt))
            for k in range(1, N // P):
                link(nc.vector.scalar_tensor_tensor(out=tiles[:, :], in0=count[:, :], scalar=float(k * P),
                                                    in1=tiles[:, :], op0=ALU.is_gt, op1=ALU.add))
            link(nc.vector.memset(first[:, 0:1], 0.0))
            for e in range(1, E):
                link(tt(first[:, e:e + 1], first[:, e - 1:e], tiles[:, e - 1:e], ALU.add))
            link(ts(owner[:, :], tile_no[:, :], first[0:1, 1:2], None, ALU.is_ge))
            for e in range(2, E):
                link(nc.vector.scalar_tensor_tensor(out=owner[:, :], in0=tile_no[:, :], scalar=first[0:1, e:e + 1],
                                                    in1=owner[:, :], op0=ALU.is_ge, op1=ALU.add))
            nc.vector.tensor_copy(owner_i[:, :], owner[:, :]).then_inc(owner_ready, 1)
            link(ts(first[:, :], first[:, :], float(P), None, ALU.mult))
            link(tt(slot[:, :, :], before[:, :, :], first[:, :].unsqueeze(1).broadcast_to([T, B, E]), ALU.add))
            link(tt(slot[:, :, :], slot[:, :, :],
                    core.bank[6][0:T, 0:B * E].rearrange("p (b e) -> p b e", e=E), ALU.add))
            for n, pick in enumerate((pick1, pick2)):
                link(tt(pick[:, :, :], pick[:, :, :], slot[:, :, :], ALU.mult))
                link(reduce(slot_f[:, n, :], pick[:, :, :], AX.X, ALU.add))
            nc.vector.tensor_copy(slot_u[:, :, :], slot_f[:, :, :]).then_inc(slots_ready, 1)

            def take_rows(tile, s):
                dve.wait_ge(rows_turned, tile + 1)
                nc.vector.tensor_copy(rowsT[:, :, :],
                                      core.bank[6][:, 0:DC * P].rearrange("p (c t) -> p c t", t=P)
                                      ).then_inc(rowsT_ready, 1)

            def take_result(tile, s):
                dve.wait_ge(down_done, tile + 1)
                dve.wait_ge(stored, tile * 16 + 16)
                dst, src = result[:, s, :], core.bank[DOWN[s]][:, 0:D]
                if offsets:
                    ins = tt(dst, src, b_down[:, s, :], ALU.add)
                else:
                    ins = nc.vector.tensor_copy(dst, src)
                ins.then_inc(result_ready, 1)

            nc.vector.engine_nop().then_inc(stored, 16 * NBUF)
            take_rows(0, 0)
            with dve.Fori(0, ROUNDS) as r:
                for s in range(NBUF):
                    take_rows(r * NBUF + s + 1, s + 1)
                    take_result(r * NBUF + s, s)
            for b in range(B):
                dve.wait_ge(gathered[b], 32)
                for n in range(2):
                    link(nc.vector.scalar_tensor_tensor(out=core.x[:, b, :], in0=got[:, n, b, :],
                                                        scalar=weight[:, n, b:b + 1], in1=core.x[:, b, :],
                                                        op0=ALU.mult, op1=ALU.add))

        @block.scalar
        def _(act):
            root_step(core, act, 1, var_ready, std_ready)
            if softmax:
                act.wait_ge(shifted, 1)
                nc.scalar.activation(prob[:, :, :], prob[:, :, :], ACT.Exp).then_inc(exp_done, 1)
            with act.Fori(0, ROUNDS) as r:
                for s in range(NBUF):
                    if offsets:
                        act.wait_ge(w_loaded[s], r * 16 * W_DMAS + 16 * W_DMAS)
                    for g in range(HG):
                        layer, q = g // GR, g % GR
                        dst = (h1T, h2T)[layer]
                        act.wait_ge(hid_done, (r * NBUF + s) * HG + g + 1)
                        if offsets:
                            for m in range(q * MG, (q + 1) * MG):
                                ins = nc.scalar.activation(dst[:, m, :],
                                                           core.bank[g % 4][:, (m % MG) * P:(m % MG + 1) * P],
                                                           act_func, bias=b_hid[:, s, layer, m:m + 1])
                        else:
                            ins = nc.scalar.activation(
                                dst[:, q * MG:(q + 1) * MG, :],
                                core.bank[g % 4][:, 0:MG * P].rearrange("p (m t) -> p m t", t=P), act_func)
                        ins.then_inc(h_ready, 1)

        @block.tensor
        def _(pe):
            norm_to_features(core, pe, dve_order, turned)
            pe.wait_ge(xT_ready, 4)
            pe.wait_ge(gate_loaded, 16)
            for b in range(B):
                for c in range(DC):
                    ins = pe.matmul(core.bank[4][0:T, b * E:(b + 1) * E], core.xnT[:, c, b * T:(b + 1) * T],
                                    gate[:, c, :], start=(c == 0), stop=(c == DC - 1))
            ins.then_inc(logits_done, 1)
            pe.wait_ge(both_ready, 1)
            pe.matmul(core.bank[5][0:T, 0:B * E], ones[:, :], both[:, :, :].rearrange("p b e -> p (b e)"),
                      start=True, stop=True)
            pe.matmul(core.bank[6][0:T, 0:B * E], earlier[:, :], both[:, :, :].rearrange("p b e -> p (b e)"),
                      start=True, stop=True).then_inc(prefix_done, 1)

            def turn_rows(round_, s, tile):
                pe.wait_ge(x_loaded[s % NBUF], round_ * 16 + 16)
                for c in range(DC):
                    ins = pe.transpose(core.bank[6][:, c * P:(c + 1) * P], rows[:, s % NBUF, c * P:(c + 1) * P],
                                       core.ident[:, :])
                ins.then_inc(rows_turned, 1)

            pe.wait_ge(slots_ready, 1)
            turn_rows(0, 0, 0)
            with pe.Fori(0, ROUNDS) as r:
                for s in range(NBUF):
                    tile = r * NBUF + s
                    pe.wait_ge(w_loaded[s], r * 16 * W_DMAS + 16 * W_DMAS)
                    pe.wait_ge(rowsT_ready, tile + 1)
                    for layer in range(hidden):
                        w, src, K = ((w_up, None, DC), (w_mid if offsets else None, h1T, IC))[layer]
                        for q in range(GR):
                            g = layer * GR + q
                            if g >= 4:
                                pe.wait_ge(h_ready, tile * HG + g - 3)
                            for m in range(q * MG, (q + 1) * MG):
                                for k in range(K):
                                    if layer and q == 0 and m == 0 and k % MG == 0 and k:
                                        pe.wait_ge(h_ready, tile * HG + k // MG + 1)
                                    rhs = h1T[:, k, :] if layer else rowsT[:, k, :]
                                    ins = pe.matmul(core.bank[g % 4][:, (m % MG) * P:(m % MG + 1) * P],
                                                    w[:, s, k, m * P:(m + 1) * P], rhs,
                                                    start=(k == 0), stop=(k == K - 1))
                            ins.then_inc(hid_done, 1)
                    turn_rows(r + (1 if s + 1 == NBUF else 0), s + 1, tile + 1)
                    for k in range(IC):
                        if k % MG == 0:
                            pe.wait_ge(h_ready, tile * HG + (hidden - 1) * GR + k // MG + 1)
                        ins = pe.matmul(core.bank[DOWN[s]][:, 0:D], h2T[:, k, :], w_down[:, s, k, :],
                                        start=(k == 0), stop=(k == IC - 1))
                    ins.then_inc(down_done, 1)


def causal_attention(nc, core, a):
    H, HD, PAD, L = 16, 16, 32, "A1"
    J = H // 4
    with ExitStack() as ctx:
        sb = lambda n, s, dt=F32: ctx.enter_context(nc.sbuf_tensor(f"{L}_{n}", s, dt))
        sem = lambda n: core.sem(f"{L}_{n}")
        wqk = sb("wqk", [P, 2, DC, D])
        padded = sb("padded", [P, 2, DC, H, PAD])
        wv, wo = sb("wv", [P, DC, D]), sb("wo", [P, DC, D])
        bqk = sb("bqk", [P, 2, J])
        bv, bo = sb("bv", [T, D]), sb("bo", [T, D])
        ctxT = sb("ctxT", [P, DC, N])
        rowsT = sb("rowsT", [P, DC, T])
        causal = sb("causal", [T, 4, T])
        qT, kT = sb("qT", [P, J, T]), sb("kT", [P, J, T])
        v = sb("v", [T, D])
        score, prob = sb("score", [T, J, 4, T]), sb("prob", [T, J, 4, T])
        probT = sb("probT", [T, J, 4, T])
        npeak, total, rtotal = sb("npeak", [T, H]), sb("total", [T, H]), sb("rtotal", [T, H])
        heads, headsT = sb("heads", [T, D]), sb("headsT", [P, DC, T])
        w_loaded = sem("w_loaded")
        dve_order, var_ready, std_ready, turned = sem("dve_order"), sem("var_ready"), sem("std_ready"), sem("turned")
        xT_ready, zeroed, masked = sem("xT_ready"), sem("zeroed"), sem("masked")
        padded_ready, rows_ready, proj_done = sem("padded_ready"), sem("rows_ready"), sem("proj_done")
        qk_ready, v_ready, scores_done = sem("qk_ready"), sem("v_ready"), sem("scores_done")
        peak_ready, exp_done, probs_turned = sem("peak_ready"), sem("exp_done"), sem("probs_turned")
        probT_ready, pv_done, heads_ready = sem("probT_ready"), sem("pv_done"), sem("heads_ready")
        heads_turned, headsT_ready, out_done = sem("heads_turned"), sem("headsT_ready"), sem("out_done")
        block = ctx.enter_context(nc.Block())

        @block.sync
        def _(sp):
            sp.wait_ge(zeroed, 1)
            for n, name in enumerate(("A1_bq", "A1_bk")):
                for r in range(4):
                    sp.dma_start(bqk[r * PAD:r * PAD + HD, n, :], a[name][r]).then_inc(w_loaded, 16)
            sp.dma_start(wqk[:, :, :, :], a["A1_wqk"]).then_inc(w_loaded, 16)
            sp.dma_start(ctxT[:, :, :], a["A1_ctxT"]).then_inc(w_loaded, 16)
            sp.dma_start(wv[:, :, :], a["A1_wv"]).then_inc(w_loaded, 16)
            sp.dma_start(wo[:, :, :], a["A1_wo"]).then_inc(w_loaded, 16)
            sp.dma_start(bv[:, :], a["A1_bv"]).then_inc(w_loaded, 16)
            sp.dma_start(bo[:, :], a["A1_bo"]).then_inc(w_loaded, 16)
        LOADS = 14 * 16

        @block.gpsimd
        def _(pool):
            nc.gpsimd.memset(bqk[:, :, :], 0.0).then_inc(zeroed, 1)
            nc.gpsimd.memset(padded[:, :, :, :, :], 0.0).then_inc(zeroed, 1)
            nc.gpsimd.memset(causal[:, :, :], 0.0).then_inc(zeroed, 1)
            pool.wait_ge(zeroed, 3)
            nc.gpsimd.affine_select(out=causal[:, :, :], in_=causal[:, :, :], compare_op=ALU.is_ge,
                                    fill=-BIG, base=0, pattern=[[0, 4], [-1, T]],
                                    channel_multiplier=1).then_inc(masked, 1)

        @block.vector
        def _(dve):
            link = Link(dve, dve_order)
            layer_norm_rows(core, link, 1, dve, core.x, core.xn, var_ready, std_ready)
            take_features(core, dve, turned, xT_ready)
            dve.wait_ge(w_loaded, LOADS)
            dve.wait_ge(zeroed, 3)
            for n in range(2):
                for c in range(DC):
                    nc.vector.tensor_copy(padded[:, n, c, :, 0:HD],
                                          wqk[:, n, c, :].rearrange("p (h d) -> p h d", d=HD)
                                          ).then_inc(padded_ready, 1)
            dve.wait_ge(masked, 1)
            nc.vector.tensor_copy(rowsT[:, :, :], ctxT[:, :, 0:T]).then_inc(rows_ready, 1)

            def batch(b, last_batch):
                dve.wait_ge(proj_done, b * 3 + 3)
                nc.vector.tensor_tensor(v[:, :], core.bank[6][0:T, 0:D], bv[:, :], ALU.add).then_inc(v_ready, 1)
                if not last_batch:
                    nc.vector.tensor_copy(rowsT[:, :, :],
                                          ctxT[:, :, bass.ds((b + 1) * T, T)]).then_inc(rows_ready, 1)
                for j in range(J):
                    dve.wait_ge(scores_done, b * J + j + 1)
                    link(nc.vector.scalar_tensor_tensor(
                        out=score[:, j, :, :], in0=core.bank[j][0:T, 0:4 * T].rearrange("p (r t) -> p r t", t=T),
                        scalar=HD ** -0.5, in1=causal[:, :, :], op0=ALU.mult, op1=ALU.add))
                    nc.vector.tensor_reduce(npeak[:, 4 * j:4 * j + 4], score[:, j, :, :], AX.X, ALU.max,
                                            negate=True).then_inc(peak_ready, 1)
                for j in range(J):
                    dve.wait_ge(probs_turned, b * J + j + 1)
                    nc.vector.tensor_copy(probT[:, j, :, :],
                                          core.bank[4 + j % 2][0:T, 0:4 * T].rearrange("p (r t) -> p r t", t=T)
                                          ).then_inc(probT_ready, 1)
                dve.wait_ge(exp_done, b * H + H)
                link(nc.vector.reciprocal(rtotal[:, :], total[:, :]))
                dve.wait_ge(pv_done, b + 1)
                nc.vector.tensor_tensor(
                    heads[:, :].rearrange("p (h d) -> p h d", d=HD),
                    core.bank[7][0:T, 0:D].rearrange("p (h d) -> p h d", d=HD),
                    rtotal[:, :].unsqueeze(2).broadcast_to([T, H, HD]), ALU.mult).then_inc(heads_ready, 1)
                dve.wait_ge(out_done, b + 1)
                link(nc.vector.tensor_tensor(core.x[:, b, :], core.x[:, b, :], core.bank[7][0:T, D:2 * D],
                                             ALU.add))
                link(nc.vector.tensor_tensor(core.x[:, b, :], core.x[:, b, :], bo[:, :], ALU.add))

            per_batch = J + 3
            start = link.count
            with dve.Fori(0, B - 1) as b:
                link.base = b * per_batch
                batch(b, False)
                assert link.count == start + per_batch
            link.base, link.count = None, start + (B - 1) * per_batch
            batch(B - 1, True)

        @block.scalar
        def _(act):
            root_step(core, act, 1, var_ready, std_ready)
            act.wait_ge(w_loaded, LOADS)
            with act.Fori(0, B) as b:
                for n, dst in enumerate((qT, kT)):
                    act.wait_ge(proj_done, b * 3 + n + 1)
                    for j in range(J):
                        ins = nc.scalar.activation(dst[:, j, :], core.bank[4 + n][:, j * T:(j + 1) * T],
                                                   ACT.Identity, bias=bqk[:, n, j:j + 1])
                    ins.then_inc(qk_ready, 1)
                for j in range(J):
                    act.wait_ge(peak_ready, b * J + j + 1)
                    for r in range(4):
                        h = 4 * r + j
                        nc.scalar.activation(prob[:, j, r, :], score[:, j, r, :], ACT.Exp,
                                             bias=npeak[:, 4 * j + r:4 * j + r + 1],
                                             accum_out=total[:, h:h + 1]).then_inc(exp_done, 1)
                act.wait_ge(heads_turned, b + 1)
                nc.scalar.activation(headsT[:, :, :],
                                     core.bank[6][:, 0:DC * T].rearrange("p (c t) -> p c t", t=T),
                                     ACT.Copy).then_inc(headsT_ready, 1)

        @block.tensor
        def _(pe):
            norm_to_features(core, pe, dve_order, turned)
            pe.wait_ge(xT_ready, 4)
            pe.wait_ge(padded_ready, 2 * DC)
            with pe.Fori(0, B) as b:
                pe.wait_ge(rows_ready, b + 1)
                for n, src in enumerate((core.xnT, ctxT)):
                    for j in range(J):
                        for c in range(DC):
                            ins = pe.matmul(core.bank[4 + n][:, j * T:(j + 1) * T],
                                            padded[:, n, c, 4 * j:4 * j + 4, :].rearrange("p h d -> p (h d)"),
                                            src[:, c, bass.ds(b * T, T)], start=(c == 0), stop=(c == DC - 1))
                    ins.then_inc(proj_done, 1)
                for c in range(DC):
                    ins = pe.matmul(core.bank[6][0:T, 0:D], rowsT[:, c, :], wv[:, c, :],
                                    start=(c == 0), stop=(c == DC - 1))
                ins.then_inc(proj_done, 1)
                pe.wait_ge(qk_ready, b * 2 + 2)
                for r in range(4):
                    for j in range(J):
                        g = slice(r * PAD, (r + 1) * PAD)
                        ins = pe.matmul(core.bank[r][0:T, j * T:(j + 1) * T], qT[g, j, :], kT[g, j, :],
                                        start=True, stop=True)
                    ins.then_inc(scores_done, 1)
                pe.wait_ge(v_ready, b + 1)

                def values(j):
                    pe.wait_ge(probT_ready, b * J + j + 1)
                    for r in range(4):
                        h = 4 * r + j
                        ins = pe.matmul(core.bank[7][0:T, h * HD:(h + 1) * HD], probT[:, j, r, :],
                                        v[:, h * HD:(h + 1) * HD], start=True, stop=True)
                    return ins

                for j in range(J):
                    pe.wait_ge(exp_done, b * H + 4 * j + 4)
                    if j >= 2:
                        pe.wait_ge(probT_ready, b * J + j - 1)
                    for r in range(4):
                        ins = pe.transpose(core.bank[4 + j % 2][0:T, r * T:(r + 1) * T], prob[:, j, r, :],
                                           core.ident[0:T, 0:T])
                    ins.then_inc(probs_turned, 1)
                    if j >= 1:
                        values(j - 1)
                values(J - 1).then_inc(pv_done, 1)
                pe.wait_ge(heads_ready, b + 1)
                for c in range(DC):
                    ins = pe.transpose(core.bank[6][:, c * T:(c + 1) * T], heads[:, c * P:(c + 1) * P],
                                       core.ident[0:T, 0:T])
                ins.then_inc(heads_turned, 1)
                pe.wait_ge(headsT_ready, b + 1)
                for c in range(DC):
                    ins = pe.matmul(core.bank[7][0:T, D:2 * D], headsT[:, c, :], wo[:, c, :],
                                    start=(c == 0), stop=(c == DC - 1))
                ins.then_inc(out_done, 1)


def quantized_ffn(nc, core, a):
    I, BLOCK, L = 768, 32, "F1"
    IC = I // P
    W_MAX, A_MAX, TINY = 7.0, 32767.0, 1e-12
    NBLK = I * D // P // BLOCK
    with ExitStack() as ctx:
        sb = lambda n, s, dt=F32: ctx.enter_context(nc.sbuf_tensor(f"{L}_{n}", s, dt))
        sem = lambda n: core.sem(f"{L}_{n}")
        w = sb("w", [P, 3, I * D // P])
        w_scale, w_rscale = sb("w_scale", [P, 3 * NBLK]), sb("w_rscale", [P, 3 * NBLK])
        gate_upT = sb("gate_upT", [P, 2, DC, I])
        downT = sb("downT", [P, IC, D])
        gate_up = sb("gate_up", [P, 2, IC, N])
        sig = sb("sig", [P, IC, N])
        local = sb("local", [P, 5, 2 * 2 * IC])
        amax, most = sb("amax", [P, 5]), sb("most", [P, 5])
        scale, rscale = sb("scale", [P, 5]), sb("rscale", [P, 5])
        w_loaded, dve_order = sem("w_loaded"), sem("dve_order")
        var_ready, std_ready, turned, xT_ready = sem("var_ready"), sem("std_ready"), sem("turned"), sem("xT_ready")
        w_ready, w_turned, wT_ready = sem("w_ready"), sem("w_turned"), sem("wT_ready")
        cleared, amax_ready, most_ready = sem("cleared"), sem("amax_ready"), sem("most_ready")
        xq_ready, gu_done, gu_taken, gu_seen = sem("xq_ready"), sem("gu_done"), sem("gu_taken"), sem("gu_seen")
        gate_ready, sig_ready, o_ready = sem("gate_ready"), sem("sig_ready"), sem("o_ready")
        down_done, x_added = sem("down_done"), sem("x_added")
        ROUNDS = 4
        block = ctx.enter_context(nc.Block())

        @block.sync
        def _(sp):
            sp.dma_start(w[:, :, :], a["F1_w"]).then_inc(w_loaded, 16)

        @block.gpsimd
        def _(pool):
            nc.gpsimd.memset(amax[:, :], 0.0).then_inc(cleared, 1)
            for r, cols in enumerate(((0, 1), (1, 3), (3, 4), (4, 5))):
                pool.wait_ge(amax_ready, r + 1)
                nc.gpsimd.partition_all_reduce(most[:, cols[0]:cols[1]], amax[:, cols[0]:cols[1]], P,
                                               bass.bass_isa.ReduceOp.max).then_inc(most_ready, 1)

        @block.vector
        def _(dve):
            link = Link(dve, dve_order)
            layer_norm_rows(core, link, 1, dve, core.x, core.xn, var_ready, std_ready)

            def scales(r, lo, hi):
                dve.wait_ge(most_ready, r + 1)
                link(nc.vector.tensor_scalar(scale[:, lo:hi], most[:, lo:hi], 1.0 / A_MAX, TINY,
                                             ALU.mult, ALU.max))
                link(nc.vector.reciprocal(rscale[:, lo:hi], scale[:, lo:hi]))

            def quantize(t, n, rows=P):
                link(nc.vector.tensor_scalar(t, t, rscale[0:rows, n:n + 1], ROUND, ALU.mult, ALU.add))
                link(nc.vector.tensor_scalar(t, t, -ROUND, -A_MAX - 1.0, ALU.add, ALU.max))
                return nc.vector.tensor_scalar(t, t, A_MAX, scale[0:rows, n:n + 1], ALU.min, ALU.mult)

            dve.wait_ge(cleared, 1)
            nc.vector.tensor_reduce(amax[0:T, 0:1], core.xn[:, :, :], AX.XY, ALU.max,
                                    apply_absolute_value=True).then_inc(amax_ready, 1)
            dve.wait_ge(w_loaded, 16)
            blocks = w[:, :, :].rearrange("p m (n k) -> p (m n) k", k=BLOCK)
            over = lambda t: t.unsqueeze(2).broadcast_to([P, 3 * NBLK, BLOCK])
            link(nc.vector.tensor_reduce(w_scale[:, :], blocks, AX.X, ALU.max, apply_absolute_value=True))
            link(nc.vector.tensor_scalar(w_scale[:, :], w_scale[:, :], 1.0 / W_MAX, TINY, ALU.mult, ALU.max))
            link(nc.vector.reciprocal(w_rscale[:, :], w_scale[:, :]))
            link(nc.vector.tensor_tensor(blocks, blocks, over(w_rscale[:, :]), ALU.mult))
            link(nc.vector.tensor_scalar(w[:, :, :], w[:, :, :], ROUND, -ROUND, ALU.add, ALU.add))
            link(nc.vector.tensor_scalar(w[:, :, :], w[:, :, :], -W_MAX - 1.0, W_MAX, ALU.max, ALU.min))
            nc.vector.tensor_tensor(blocks, blocks, over(w_scale[:, :]), ALU.mult).then_inc(w_ready, 1)
            scales(0, 0, 1)
            quantize(core.xn[:, :, :], 0, T).then_inc(xq_ready, 1)
            take_features(core, dve, turned, xT_ready)
            for n in range(2 * 2 * IC):
                dve.wait_ge(gu_done, n + 1)
                ins = nc.vector.tensor_reduce(local[:, 1 + n // (2 * IC), n % (2 * IC):n % (2 * IC) + 1],
                                              core.bank[n % 4][:, 0:HALF], AX.X, ALU.max,
                                              apply_absolute_value=True)
                ins.then_inc(gu_seen, 1)
            dve.wait_ge(gu_seen, 2 * 2 * IC)
            nc.vector.tensor_reduce(amax[:, 1:3], local[:, 1:3, 0:2 * IC], AX.X, ALU.max).then_inc(amax_ready, 1)
            scales(1, 1, 3)
            dve.wait_ge(gu_taken, 2 * 2 * IC)
            quantize(gate_up[:, 0], 1).then_inc(gate_ready, 1)
            link(quantize(gate_up[:, 1], 2))
            dve.wait_ge(sig_ready, 1)
            link(nc.vector.tensor_scalar(sig[:, :, :], sig[:, :, :], 65536.0, ROUND, ALU.mult, ALU.add))
            link(nc.vector.tensor_scalar(sig[:, :, :], sig[:, :, :], -ROUND, 0.0, ALU.add, ALU.max))
            link(nc.vector.tensor_scalar(sig[:, :, :], sig[:, :, :], 65535.0, 1.0 / 65536.0, ALU.min, ALU.mult))
            for n, other in ((3, sig[:, :, :]), (4, gate_up[:, 1])):
                g = gate_up[:, 0]
                link(nc.vector.tensor_tensor(g, g, other, ALU.mult))
                nc.vector.tensor_reduce(amax[:, n:n + 1], g, AX.XY, ALU.max,
                                        apply_absolute_value=True).then_inc(amax_ready, 1)
                scales(n - 1, n, n + 1)
                last = quantize(g, n)
                if n == 3:
                    link(last)
            last.then_inc(o_ready, 1)
            for b in range(B):
                dve.wait_ge(down_done, b + 1)
                nc.vector.tensor_tensor(core.x[:, b, :], core.x[:, b, :], core.bank[4 + b % 4][0:T, 0:D],
                                        ALU.add).then_inc(x_added, 1)

        @block.scalar
        def _(act):
            root_step(core, act, 1, var_ready, std_ready)
            for g in range(9):
                act.wait_ge(w_turned, g + 1)
                if g < 6:
                    dst = gate_upT[:, g // 3, :, (g % 3) * 2 * P:(g % 3 + 1) * 2 * P]
                    src = core.bank[4 + g % 4][:, :].rearrange("p (c i) -> p c i", c=DC)
                else:
                    dst = downT[:, 2 * (g - 6):2 * (g - 6) + 2, :]
                    src = core.bank[4 + g % 4][:, :].rearrange("p (i d) -> p i d", i=2)
                nc.scalar.activation(dst, src, ACT.Copy).then_inc(wT_ready, 1)
            for n in range(2 * 2 * IC):
                act.wait_ge(gu_seen, n + 1)
                m, half = n % (2 * IC) // 2, n % 2
                nc.scalar.activation(gate_up[:, n // (2 * IC), m, half * HALF:(half + 1) * HALF],
                                     core.bank[n % 4][:, 0:HALF], ACT.Copy).then_inc(gu_taken, 1)
            act.wait_ge(gate_ready, 1)
            nc.scalar.activation(sig[:, :, :], gate_up[:, 0], ACT.Sigmoid).then_inc(sig_ready, 1)

        @block.tensor
        def _(pe):
            pe.wait_ge(w_ready, 1)
            for g in range(9):
                if g >= 4:
                    pe.wait_ge(wT_ready, g - 3)
                for q in range(4):
                    if g < 6:
                        c, i = q // 2, (g % 3) * 2 + q % 2
                        piece = w[:, g // 3, i * D + c * P:i * D + (c + 1) * P]
                    else:
                        c, i = q % 2, (g - 6) * 2 + q // 2
                        piece = w[:, 2, c * I + i * P:c * I + (i + 1) * P]
                    ins = pe.transpose(core.bank[4 + g % 4][:, q * P:(q + 1) * P], piece, core.ident[:, :])
                ins.then_inc(w_turned, 1)
            pe.wait_ge(xq_ready, 1)
            transpose_rows(core, pe, core.xn, [0, 1, 2, 3], turned)
            pe.wait_ge(xT_ready, 4)
            pe.wait_ge(wT_ready, 9)
            for n in range(2 * 2 * IC):
                m, half = n % (2 * IC) // 2, n % 2
                if n >= 4:
                    pe.wait_ge(gu_taken, n - 3)
                for c in range(DC):
                    ins = pe.matmul(core.bank[n % 4][:, 0:HALF], gate_upT[:, n // (2 * IC), c, m * P:(m + 1) * P],
                                    core.xnT[:, c, half * HALF:(half + 1) * HALF],
                                    start=(c == 0), stop=(c == DC - 1))
                ins.then_inc(gu_done, 1)
            pe.wait_ge(o_ready, 1)
            for b in range(B):
                if b >= 4:
                    pe.wait_ge(x_added, b - 3)
                for m in range(IC):
                    ins = pe.matmul(core.bank[4 + b % 4][0:T, 0:D], gate_up[:, 0, m, b * T:(b + 1) * T],
                                    downT[:, m, :], start=(m == 0), stop=(m == IC - 1))
                ins.then_inc(down_done, 1)


def slot_attention(nc, core, a):
    ITERS, EPS, L = 3, 1e-6, "A3"
    NT = B * SC
    VW = D + 1
    G3 = 3 * D
    with ExitStack() as ctx:
        sb = lambda n, s, dt=F32: ctx.enter_context(nc.sbuf_tensor(f"{L}_{n}", s, dt))
        sem = lambda n: core.sem(f"{L}_{n}")
        wqkv = sb("wqkv", [P, 3, DC, D])
        wih, whh = sb("wih", [P, DC, G3]), sb("whh", [P, DC, G3])
        norms = sb("norms", [P, 2, DC])
        bih, bhh = sb("bih", [T, G3]), sb("bhh", [T, G3])
        rows = sb("rows", [SP_, NT, D])
        junk = sb("junk", [P, D])
        sq, rs = sb("sq", [SP_, NT]), sb("rs", [SP_, NT])
        rowsT = sb("rowsT", [P, DC, S])
        kT = sb("kT", [P, DC, B * S])
        v = sb("v", [SP_, NT, VW])
        slots = core.xn
        slot_sq, slot_rs = sb("slot_sq", [T, B]), sb("slot_rs", [T, B])
        sn = sb("sn", [T, B, D])
        snT, slotsT, qT = core.xnT, sb("slotsT", [P, DC, N]), sb("qT", [P, DC, N])
        npeak, total = sb("npeak", [SP_, SC]), sb("total", [SP_, SC])
        attn = sb("attn", [SP_, 2, SC, T])
        rsum = sb("rsum", [T, 1])
        upd, updT = sb("upd", [T, 2, D]), sb("updT", [P, 2, DC, T])
        rz, nn = sb("rz", [T, 2 * D]), sb("nn", [T, D])
        nh, diff = sb("nh", [T, D]), sb("diff", [T, D])
        w_loaded, rows_loaded = sem("w_loaded"), sem("rows_loaded")
        dve_order, act_order = sem("dve_order"), sem("act_order")
        var_ready, std_ready = sem("var_ready"), sem("std_ready")
        sq_ready, ms_ready, root_ready = sem("sq_ready"), sem("ms_ready"), sem("root_ready")
        rows_ready, rows_turned, rowsT_ready = sem("rows_ready"), sem("rows_turned"), sem("rowsT_ready")
        kv_done, k_taken, v_taken = sem("kv_done"), sem("k_taken"), sem("v_taken")
        slots_ready, slots_turned, slotsT_ready = sem("slots_ready"), sem("slots_turned"), sem("slotsT_ready")
        slot_sq_ready, sn_ready, sn_turned, snT_ready = sem("slot_sq_ready"), sem("sn_ready"), sem("sn_turned"), sem("snT_ready")
        q_done, q_ready = sem("q_done"), sem("q_ready")
        scores_done, shifted, exp_done, attn_ready = sem("scores_done"), sem("shifted"), sem("exp_done"), sem("attn_ready")
        upd_done, upd_ready, upd_turned, updT_ready = sem("upd_done"), sem("upd_ready"), sem("upd_turned"), sem("updT_ready")
        gates_done, rz_ready, rz_tanh = sem("gates_done"), sem("rz_ready"), sem("rz_tanh")
        n_ready, n_tanh, slot_new = sem("n_ready"), sem("n_tanh"), sem("slot_new")
        block = ctx.enter_context(nc.Block())

        @block.sync
        def _(sp):
            sp.dma_start(rows[:, :, :], a["ctx_rows"]).then_inc(rows_loaded, 16)
            sp.dma_start(norms[:, :, :], a["A3_norms"]).then_inc(w_loaded, 16)
            sp.dma_start(wqkv[:, :, :, :], a["A3_wqkv"]).then_inc(w_loaded, 16)
            for dst, name in ((wih, "A3_wih"), (whh, "A3_whh")):
                sp.dma_start(dst[:, :, :], a[name]).then_inc(w_loaded, 16)
            for dst, name in ((bih, "A3_bih"), (bhh, "A3_bhh")):
                sp.dma_start(dst[:, :], a[name]).then_inc(w_loaded, 16)

        @block.vector
        def _(dve):
            link = Link(dve, dve_order)
            layer_norm_rows(core, link, 1, dve, core.x, core.xn, var_ready, std_ready)
            nc.vector.memset(v[:, :, D:VW], 1.0).then_inc(v_taken, 1)
            nc.vector.engine_nop().then_inc(slot_new, B)
            dve.wait_ge(w_loaded, 96)
            link(nc.vector.tensor_tensor(bih[:, 0:2 * D], bih[:, 0:2 * D], bhh[:, 0:2 * D], ALU.add))
            dve.wait_ge(sq_ready, NT)
            nc.vector.tensor_scalar(rs[:, :], sq[:, :], 1.0 / D, EPS, ALU.mult, ALU.add).then_inc(ms_ready, 1)
            dve.wait_ge(root_ready, 1)
            link(nc.vector.reciprocal(rs[:, :], rs[:, :]))
            for t in range(NT):
                nc.vector.tensor_scalar(rows[:, t, :], rows[:, t, :], rs[:, t:t + 1], None,
                                        ALU.mult).then_inc(rows_ready, 1)
            for b in range(B):
                for c in range(DC):
                    dve.wait_ge(rows_turned, b * DC + c + 1)
                    if b:
                        dve.wait_ge(kv_done, b * (DC + SC))
                    nc.vector.tensor_scalar(rowsT[:, c, :], core.bank[c][:, 0:S], norms[:, 1, c:c + 1], None,
                                            ALU.mult).then_inc(rowsT_ready, 1)
                for k in range(SC):
                    dve.wait_ge(kv_done, b * (DC + SC) + DC + k + 1)
                    nc.vector.tensor_copy(v[:, b * SC + k, 0:D],
                                          core.bank[4 + k][0:SP_, 0:D]).then_inc(v_taken, 1)

            def softmax(it, b):
                dve.wait_ge(scores_done, it * B + b + 1)
                src = core.bank[b % 2][0:SP_, 0:SC * T].rearrange("p (k t) -> p k t", t=T)
                over = lambda t: t.unsqueeze(2).broadcast_to([SP_, SC, T])
                link(nc.vector.tensor_reduce(npeak[:, :], src, AX.X, ALU.max, negate=True))
                if b >= 2:
                    dve.wait_ge(upd_done, it * B + b - 1)
                nc.vector.tensor_tensor(attn[:, b % 2, :, :], src, over(npeak[:, :]), ALU.add
                                        ).then_inc(shifted, 1)
                dve.wait_ge(exp_done, it * B + b + 1)
                link(nc.vector.tensor_reduce(total[:, :], attn[:, b % 2, :, :], AX.X, ALU.add))
                link(nc.vector.reciprocal(total[:, :], total[:, :]))
                nc.vector.tensor_tensor(attn[:, b % 2, :, :], attn[:, b % 2, :, :], over(total[:, :]), ALU.mult
                                        ).then_inc(attn_ready, 1)

            def means(it, b):
                dve.wait_ge(upd_done, it * B + b + 1)
                src = core.bank[2 + b % 2]
                link(nc.vector.tensor_scalar(rsum[:, :], src[0:T, D:VW], EPS, None, ALU.add))
                link(nc.vector.reciprocal(rsum[:, :], rsum[:, :]))
                nc.vector.tensor_scalar(upd[:, b % 2, :], src[0:T, 0:D], rsum[:, 0:1], None, ALU.mult
                                        ).then_inc(upd_ready, 1)

            def gates(it, b):
                dve.wait_ge(gates_done, it * B + b + 1)
                dve.wait_ge(slot_new, it * B + b + B)
                nc.vector.tensor_tensor(rz[:, :], core.bank[6][0:T, :], bih[:, 0:2 * D], ALU.add
                                        ).then_inc(rz_ready, 1)
                link(nc.vector.tensor_tensor(nn[:, :], core.bank[7][0:T, 0:D], bih[:, 2 * D:G3], ALU.add))
                link(nc.vector.tensor_tensor(nh[:, :], core.bank[7][0:T, D:2 * D], bhh[:, 2 * D:G3], ALU.add))
                dve.wait_ge(rz_tanh, it * B + b + 1)
                link(nc.vector.tensor_scalar(rz[:, :], rz[:, :], 0.5, 0.5, ALU.mult, ALU.add))
                link(nc.vector.tensor_tensor(nh[:, :], nh[:, :], rz[:, 0:D], ALU.mult))
                nc.vector.tensor_tensor(nn[:, :], nn[:, :], nh[:, :], ALU.add).then_inc(n_ready, 1)
                dve.wait_ge(n_tanh, it * B + b + 1)
                link(nc.vector.tensor_tensor(diff[:, :], slots[:, b, :], nn[:, :], ALU.subtract))
                link(nc.vector.tensor_tensor(diff[:, :], diff[:, :], rz[:, D:2 * D], ALU.mult))
                nc.vector.tensor_tensor(slots[:, b, :], diff[:, :], nn[:, :], ALU.add).then_inc(slot_new, 1)

            per_iter = 1 + B * (3 + 2 + 6)
            start = link.count
            with dve.Fori(0, ITERS) as it:
                link.base = it * per_iter
                dve.wait_ge(slot_sq_ready, it * B + B)
                nc.vector.tensor_scalar(slot_rs[:, :], slot_sq[:, :], 1.0 / D, EPS, ALU.mult, ALU.add
                                        ).then_inc(ms_ready, 1)
                dve.wait_ge(root_ready, it + 2)
                link(nc.vector.reciprocal(slot_rs[:, :], slot_rs[:, :]))
                for b in range(B):
                    nc.vector.tensor_scalar(sn[:, b, :], slots[:, b, :], slot_rs[:, b:b + 1], None, ALU.mult
                                            ).then_inc(sn_ready, 1)
                for c in range(DC):
                    for half in range(2):
                        dve.wait_ge(sn_turned, it * 4 + 2 * c + half + 1)
                        nc.vector.tensor_scalar(snT[:, c, half * HALF:(half + 1) * HALF],
                                                core.bank[2 * c + half][:, 0:HALF], norms[:, 0, c:c + 1], None,
                                                ALU.mult).then_inc(snT_ready, 1)
                for m in range(DC):
                    for half in range(2):
                        dve.wait_ge(q_done, it * 4 + 2 * m + half + 1)
                        nc.vector.tensor_scalar(qT[:, m, half * HALF:(half + 1) * HALF],
                                                core.bank[2 * m + half][:, 0:HALF], D ** -0.5, None,
                                                ALU.mult).then_inc(q_ready, 1)
                for s in range(B + 3):
                    if s < B:
                        softmax(it, s)
                    if 1 <= s <= B:
                        means(it, s - 1)
                    if s >= 3:
                        gates(it, s - 3)
                assert link.count == start + per_iter
            dve.wait_ge(slot_new, (ITERS + 1) * B)
            nc.vector.tensor_tensor(core.x[:, :, :], core.x[:, :, :], slots[:, :, :], ALU.add)

        @block.scalar
        def _(act):
            link = Link(act, act_order)
            act.wait_ge(rows_loaded, 16)
            for t in range(NT):
                nc.scalar.activation(junk[0:SP_, :], rows[:, t, :], ACT.Square,
                                     accum_out=sq[:, t:t + 1]).then_inc(sq_ready, 1)
                act.wait_ge(sq_ready, t + 1)
            root_step(core, act, 1, var_ready, std_ready)
            act.wait_ge(ms_ready, 1)
            nc.scalar.activation(rs[:, :], rs[:, :], ACT.Sqrt).then_inc(root_ready, 1)
            for b in range(B):
                for m in range(DC):
                    act.wait_ge(kv_done, b * (DC + SC) + m + 1)
                    nc.scalar.activation(kT[:, m, b * S:(b + 1) * S], core.bank[2 + m][:, 0:S],
                                         ACT.Copy).then_inc(k_taken, 1)
            act.wait_ge(dve_order, 4)
            with act.Fori(0, ITERS) as it:
                for b in range(B):
                    act.wait_ge(slot_new, it * B + b + 1)
                    nc.scalar.activation(junk[0:T, :], slots[:, b, :], ACT.Square,
                                         accum_out=slot_sq[:, b:b + 1]).then_inc(slot_sq_ready, 1)
                    act.wait_ge(slot_sq_ready, it * B + b + 1)
                act.wait_ge(ms_ready, it + 2)
                nc.scalar.activation(slot_rs[:, :], slot_rs[:, :], ACT.Sqrt).then_inc(root_ready, 1)
                for g in range(4):
                    act.wait_ge(slots_turned, it * 4 + g + 1)
                    c, half = g // 2, g % 2
                    nc.scalar.activation(slotsT[:, c, half * HALF:(half + 1) * HALF],
                                         core.bank[4 + g][:, 0:HALF], ACT.Copy).then_inc(slotsT_ready, 1)
                for s in range(B + 3):
                    if s < B:
                        act.wait_ge(shifted, it * B + s + 1)
                        nc.scalar.activation(attn[:, s % 2, :, :], attn[:, s % 2, :, :], ACT.Exp
                                             ).then_inc(exp_done, 1)
                    if 2 <= s < B + 2:
                        b = s - 2
                        act.wait_ge(upd_turned, it * B + b + 1)
                        nc.scalar.activation(updT[:, b % 2, :, :],
                                             core.bank[4 + b % 2][:, 0:DC * T].rearrange("p (c t) -> p c t", t=T),
                                             ACT.Copy).then_inc(updT_ready, 1)
                    if s >= 3:
                        b = s - 3
                        act.wait_ge(rz_ready, it * B + b + 1)
                        nc.scalar.activation(rz[:, :], rz[:, :], ACT.Tanh, scale=0.5).then_inc(rz_tanh, 1)
                        act.wait_ge(n_ready, it * B + b + 1)
                        nc.scalar.activation(nn[:, :], nn[:, :], ACT.Tanh).then_inc(n_tanh, 1)

        @block.tensor
        def _(pe):
            pe.wait_ge(w_loaded, 96)
            for b in range(B):
                pe.wait_ge(rows_ready, SC * (b + 1))
                for c in range(DC):
                    if b:
                        pe.wait_ge(rowsT_ready, (b - 1) * DC + c + 1)
                    for k in range(SC):
                        ins = pe.transpose(core.bank[c][:, k * SP_:(k + 1) * SP_],
                                           rows[:, b * SC + k, c * P:(c + 1) * P], core.ident[0:SP_, 0:SP_])
                    ins.then_inc(rows_turned, 1)
                pe.wait_ge(rowsT_ready, b * DC + DC)
                for m in range(DC):
                    if b:
                        pe.wait_ge(k_taken, (b - 1) * DC + m + 1)
                    for c in range(DC):
                        ins = pe.matmul(core.bank[2 + m][:, 0:S], wqkv[:, 1, c, m * P:(m + 1) * P],
                                        rowsT[:, c, :], start=(c == 0), stop=(c == DC - 1))
                    ins.then_inc(kv_done, 1)
                for k in range(SC):
                    if b:
                        pe.wait_ge(v_taken, 1 + (b - 1) * SC + k + 1)
                    for c in range(DC):
                        ins = pe.matmul(core.bank[4 + k][0:SP_, 0:D], rowsT[:, c, k * SP_:(k + 1) * SP_],
                                        wqkv[:, 2, c, :], start=(c == 0), stop=(c == DC - 1))
                    ins.then_inc(kv_done, 1)
            pe.wait_ge(k_taken, B * DC)
            pe.wait_ge(v_taken, 1 + NT)

            with pe.Fori(0, ITERS) as it:
                pe.wait_ge(sn_ready, it * B + B)
                transpose_rows(core, pe, sn, [0, 1, 2, 3], sn_turned)
                transpose_rows(core, pe, slots, [4, 5, 6, 7], slots_turned)
                pe.wait_ge(snT_ready, it * 4 + 4)
                for m in range(DC):
                    for half in range(2):
                        for c in range(DC):
                            ins = pe.matmul(core.bank[2 * m + half][:, 0:HALF], wqkv[:, 0, c, m * P:(m + 1) * P],
                                            snT[:, c, half * HALF:(half + 1) * HALF],
                                            start=(c == 0), stop=(c == DC - 1))
                        ins.then_inc(q_done, 1)
                pe.wait_ge(q_ready, it * 4 + 4)
                pe.wait_ge(slotsT_ready, it * 4 + 4)
                for s in range(B + 3):
                    if s < B:
                        if s >= 2:
                            pe.wait_ge(shifted, it * B + s - 1)
                        for k in range(SC):
                            t = s * SC + k
                            for c in range(DC):
                                ins = pe.matmul(core.bank[s % 2][0:SP_, k * T:(k + 1) * T],
                                                kT[:, c, t * SP_:(t + 1) * SP_], qT[:, c, s * T:(s + 1) * T],
                                                start=(c == 0), stop=(c == DC - 1))
                        ins.then_inc(scores_done, 1)
                    if 1 <= s <= B:
                        b = s - 1
                        pe.wait_ge(attn_ready, it * B + b + 1)
                        if b >= 2:
                            pe.wait_ge(upd_ready, it * B + b - 1)
                        for k in range(SC):
                            ins = pe.matmul(core.bank[2 + b % 2][0:T, 0:VW], attn[:, b % 2, k, :],
                                            v[:, b * SC + k, :], start=(k == 0), stop=(k == SC - 1))
                        ins.then_inc(upd_done, 1)
                    if 2 <= s < B + 2:
                        b = s - 2
                        pe.wait_ge(upd_ready, it * B + b + 1)
                        if b >= 2:
                            pe.wait_ge(updT_ready, it * B + b - 1)
                        for c in range(DC):
                            ins = pe.transpose(core.bank[4 + b % 2][:, c * T:(c + 1) * T],
                                               upd[:, b % 2, c * P:(c + 1) * P], core.ident[0:T, 0:T])
                        ins.then_inc(upd_turned, 1)
                    if s >= 3:
                        b = s - 3
                        pe.wait_ge(updT_ready, it * B + b + 1)
                        if b:
                            pe.wait_ge(n_ready, it * B + b)
                        bt = slice(b * T, (b + 1) * T)
                        for c in range(DC):
                            pe.matmul(core.bank[6][0:T, :], updT[:, b % 2, c, :], wih[:, c, 0:2 * D],
                                      start=(c == 0), stop=False)
                        for c in range(DC):
                            pe.matmul(core.bank[6][0:T, :], slotsT[:, c, bt], whh[:, c, 0:2 * D],
                                      start=False, stop=(c == DC - 1))
                        for c in range(DC):
                            pe.matmul(core.bank[7][0:T, 0:D], updT[:, b % 2, c, :], wih[:, c, 2 * D:G3],
                                      start=(c == 0), stop=(c == DC - 1))
                        for c in range(DC):
                            ins = pe.matmul(core.bank[7][0:T, D:2 * D], slotsT[:, c, bt], whh[:, c, 2 * D:G3],
                                            start=(c == 0), stop=(c == DC - 1))
                        ins.then_inc(gates_done, 1)


def tile_ffn(nc, core, a):
    NT, C, G, K, CH, L = 64, 8, 16, 8, 64, "F3"
    W = C + NT
    TW = 2 * G + G + G + 1 + D
    with ExitStack() as ctx:
        sb = lambda n, s, dt=F32: ctx.enter_context(nc.sbuf_tensor(f"{L}_{n}", s, dt))
        sem = lambda n: core.sem(f"{L}_{n}")
        raw = sb("raw", [P, DC, NT])
        low, sig = sb("low", [P, DC, NT]), sb("sig", [P, DC, W])
        mean, neg = sb("mean", [P, DC, C]), sb("neg", [P, DC, C])
        knots, steps = sb("knots", [T, K]), sb("steps", [T, K - 1])
        temp, out_scale = sb("temp", [T, 1]), sb("out_scale", [T, 1])
        cw1, cb1 = sb("cw1", [P, DC, CH]), sb("cb1", [CH, 1])
        cw2, cb2 = sb("cw2", [CH, 2]), sb("cb2", [T, B, 2])
        table = sb("table", [NT, TW])
        gamma, beta = sb("gamma", [T, D]), sb("beta", [T, D])
        hT = sb("hT", [CH, N])
        comp = sb("comp", [T, B, 2])
        where, cell = sb("where", [T, B, W]), sb("cell", [T, B, W])
        base, slope, part = sb("base", [T, B, W]), sb("slope", [T, B, W]), sb("part", [T, B, W])
        places = sb("places", [T, B, C])
        peak = sb("peak", [T, B])
        cluster, local = sb("cluster", [T, B, C]), sb("local", [T, B, C])
        chosen = sb("chosen", [T, B, C])
        spread = sb("spread", [T, B, C, C])
        onehot, onehotT = sb("onehot", [T, B, NT]), sb("onehotT", [NT, N])
        prm = sb("prm", [T, B, TW])
        hidden, hidden2 = sb("hidden", [T, B, G]), sb("hidden2", [T, B, G])
        mag = sb("mag", [T, B])
        w_loaded, dve_order = sem("w_loaded"), sem("dve_order")
        var_ready, std_ready, turned, xT_ready = sem("var_ready"), sem("std_ready"), sem("turned"), sem("xT_ready")
        placed, sig_ready, scores_done, scaled = sem("placed"), sem("sig_ready"), sem("scores_done"), sem("scaled")
        exp_done, h_done, h_ready = sem("exp_done"), sem("h_done"), sem("h_ready")
        comp_done, comp_ready, comp_tanh = sem("comp_done"), sem("comp_ready"), sem("comp_tanh")
        onehot_ready, onehot_turned, onehotT_ready = sem("onehot_ready"), sem("onehot_turned"), sem("onehotT_ready")
        prm_done, prm_ready = sem("prm_done"), sem("prm_ready")
        block = ctx.enter_context(nc.Block())
        LOADS = [(raw[:, :, :], "F3_raw"), (knots[:, :], "F3_knots"), (temp[:, :], "F3_temp"),
                 (out_scale[:, :], "F3_out_scale"), (cw1[:, :, :], "F3_cw1"), (cb1[:, :], "F3_cb1"),
                 (cw2[:, :], "F3_cw2"), (cb2[:, :, :], "F3_cb2"), (table[:, :], "F3_table"),
                 (gamma[:, :], "F3_gamma"), (beta[:, :], "F3_beta")]

        @block.sync
        def _(sp):
            for dst, name in LOADS:
                sp.dma_start(dst, a[name]).then_inc(w_loaded, 16)

        @block.gpsimd
        def _(pool):
            count_down(nc, pool, places[:, :, :], C, placed)

        @block.vector
        def _(dve):
            link = Link(dve, dve_order)
            tt, ts = nc.vector.tensor_tensor, nc.vector.tensor_scalar
            layer_norm_rows(core, link, 1, dve, core.x, core.xn, var_ready, std_ready)
            take_features(core, dve, turned, xT_ready)
            dve.wait_ge(w_loaded, 16 * len(LOADS))
            q = sig[:, :, C:W]
            link(ts(q, raw[:, :, :], 0.3, None, ALU.is_gt))
            link(ts(low[:, :, :], raw[:, :, :], -0.3, None, ALU.is_lt))
            link(tt(q, q, low[:, :, :], ALU.subtract))
            link(tt(q, q, raw[:, :, :], ALU.subtract))
            link(tt(q, q, raw[:, :, :], ALU.add))
            link(nc.vector.tensor_reduce(mean[:, :, :], q.rearrange("p c (g t) -> p c g t", t=C), AX.X, ALU.add))
            link(ts(neg[:, :, :], mean[:, :, :], 0.0, None, ALU.is_lt))
            link(ts(mean[:, :, :], mean[:, :, :], 0.0, None, ALU.is_gt))
            tt(sig[:, :, 0:C], mean[:, :, :], neg[:, :, :], ALU.subtract).then_inc(sig_ready, 1)
            link(tt(steps[:, :], knots[:, 1:K], knots[:, 0:K - 1], ALU.subtract))
            link(ts(temp[:, :], temp[:, :], 1e-6, None, ALU.add))
            link(nc.vector.reciprocal(temp[:, :], temp[:, :]))
            for half in range(2):
                dve.wait_ge(scores_done, half + 1)
                ts(where[:, half * HB:(half + 1) * HB, :],
                   core.bank[4 + half][0:T, 0:HB * W].rearrange("p (b w) -> p b w", w=W),
                   temp[:, 0:1], None, ALU.mult).then_inc(scaled, 1)
            dve.wait_ge(exp_done, 1)
            w = where[:, :, :]
            link(ts(w, w, 1.0, None, ALU.add))
            link(nc.vector.reciprocal(w, w))
            link(ts(w, w, K - 1.0, None, ALU.mult))
            link(ts(cell[:, :, :], w, 1.0, None, ALU.is_ge))
            for k in range(2, K - 1):
                link(nc.vector.scalar_tensor_tensor(out=cell[:, :, :], in0=w, scalar=float(k), in1=cell[:, :, :],
                                                    op0=ALU.is_ge, op1=ALU.add))
            link(tt(w, w, cell[:, :, :], ALU.subtract))
            for dst, values in ((base, knots), (slope, steps)):
                link(ts(dst[:, :, :], cell[:, :, :], 0.0, values[:, 0:1], ALU.is_equal, ALU.mult))
                for k in range(1, K - 1):
                    link(ts(part[:, :, :], cell[:, :, :], float(k), values[:, k:k + 1], ALU.is_equal, ALU.mult))
                    link(tt(dst[:, :, :], dst[:, :, :], part[:, :, :], ALU.add))
            link(tt(w, w, slope[:, :, :], ALU.mult))
            link(tt(w, w, base[:, :, :], ALU.add))
            dve.wait_ge(placed, 1)

            def first_best(pick, value):
                over = peak[:, :].unsqueeze(2).broadcast_to([T, B, C])
                link(nc.vector.tensor_reduce(peak[:, :], value, AX.X, ALU.max))
                link(tt(pick, value, over, ALU.is_equal))
                link(tt(pick, pick, places[:, :, :], ALU.mult))
                link(nc.vector.tensor_reduce(peak[:, :], pick, AX.X, ALU.max))
                link(tt(pick, places[:, :, :], over, ALU.is_equal))

            first_best(cluster[:, :, :], where[:, :, 0:C])
            for b in range(B):
                last = tt(spread[:, b, :, :], where[:, b, C:W].rearrange("p (c t) -> p t c", t=C),
                          cluster[:, b, :].unsqueeze(1).broadcast_to([T, C, C]), ALU.mult)
            link(last)
            link(nc.vector.tensor_reduce(chosen[:, :, :], spread[:, :, :, :], AX.X, ALU.add))
            first_best(local[:, :, :], chosen[:, :, :])
            for b in range(B):
                tt(onehot[:, b, :].rearrange("p (c t) -> p c t", t=C),
                   cluster[:, b, :].unsqueeze(2).broadcast_to([T, C, C]),
                   local[:, b, :].unsqueeze(1).broadcast_to([T, C, C]), ALU.mult).then_inc(onehot_ready, 1)
            for half in range(2):
                dve.wait_ge(onehot_turned, half + 1)
                nc.vector.tensor_copy(onehotT[:, half * HALF:(half + 1) * HALF],
                                      core.bank[2 + half][0:NT, 0:HALF]).then_inc(onehotT_ready, 1)
            dve.wait_ge(comp_done, 1)
            tt(comp[:, :, :], core.bank[6][0:T, 0:2 * B].rearrange("p (b i) -> p b i", i=2), cb2[:, :, :],
               ALU.add).then_inc(comp_ready, 1)
            dve.wait_ge(comp_tanh, 1)
            dve.wait_ge(prm_ready, B)
            wide = lambda t: t.broadcast_to([T, B, G])
            h, h2 = hidden[:, :, :], hidden2[:, :, :]
            link(tt(h, prm[:, :, 0:G], wide(comp[:, :, 0:1]), ALU.mult))
            link(tt(h2, prm[:, :, G:2 * G], wide(comp[:, :, 1:2]), ALU.mult))
            link(tt(h, h, h2, ALU.add))
            link(tt(h, h, prm[:, :, 2 * G:3 * G], ALU.add))
            link(ts(h, h, 0.0, None, ALU.max))
            link(tt(h, h, prm[:, :, 3 * G:4 * G], ALU.mult))
            link(nc.vector.tensor_reduce(mag[:, :], h, AX.X, ALU.add))
            link(tt(mag[:, :], mag[:, :], prm[:, :, 4 * G], ALU.add))
            for b in range(B):
                way = prm[:, b, 4 * G + 1:TW]
                last = ts(way, way, mag[:, b:b + 1], out_scale[:, 0:1], ALU.mult, ALU.mult)
            link(last)
            y = core.xn
            link(tt(y[:, :, :], y[:, :, :], prm[:, :, 4 * G + 1:TW], ALU.add))
            layer_norm_rows(core, link, 2, dve, y, y, var_ready, std_ready)
            for b in range(B):
                last = tt(y[:, b, :], y[:, b, :], gamma[:, :], ALU.mult)
            link(last)
            for b in range(B):
                last = tt(y[:, b, :], y[:, b, :], beta[:, :], ALU.add)
            link(last)
            tt(core.x[:, :, :], core.x[:, :, :], y[:, :, :], ALU.add)

        @block.scalar
        def _(act):
            root_step(core, act, 1, var_ready, std_ready)
            act.wait_ge(w_loaded, 16 * len(LOADS))
            for half in range(2):
                act.wait_ge(h_done, half + 1)
                nc.scalar.activation(hT[:, half * HALF:(half + 1) * HALF], core.bank[half][0:CH, 0:HALF],
                                     ACT.Gelu, bias=cb1[:, 0:1]).then_inc(h_ready, 1)
            act.wait_ge(scaled, 2)
            nc.scalar.activation(where[:, :, :], where[:, :, :], ACT.Exp, scale=-1.0).then_inc(exp_done, 1)
            for b in range(B):
                act.wait_ge(prm_done, b + 1)
                nc.scalar.activation(prm[:, b, :], core.bank[b % 2][0:T, 0:TW], ACT.Copy).then_inc(prm_ready, 1)
            act.wait_ge(comp_ready, 1)
            nc.scalar.activation(comp[:, :, :], comp[:, :, :], ACT.Tanh).then_inc(comp_tanh, 1)
            root_step(core, act, 2, var_ready, std_ready)

        @block.tensor
        def _(pe):
            norm_to_features(core, pe, dve_order, turned)
            pe.wait_ge(xT_ready, 4)
            pe.wait_ge(w_loaded, 16 * len(LOADS))
            for half in range(2):
                for c in range(DC):
                    ins = pe.matmul(core.bank[half][0:CH, 0:HALF], cw1[:, c, :],
                                    core.xnT[:, c, half * HALF:(half + 1) * HALF],
                                    start=(c == 0), stop=(c == DC - 1))
                ins.then_inc(h_done, 1)
            pe.wait_ge(sig_ready, 1)
            for b in range(B):
                for c in range(DC):
                    ins = pe.matmul(core.bank[4 + b // HB][0:T, (b % HB) * W:(b % HB + 1) * W],
                                    core.xnT[:, c, b * T:(b + 1) * T], sig[:, c, :],
                                    start=(c == 0), stop=(c == DC - 1))
                if b % HB == HB - 1:
                    ins.then_inc(scores_done, 1)
            pe.wait_ge(h_ready, 2)
            for b in range(B):
                ins = pe.matmul(core.bank[6][0:T, 2 * b:2 * b + 2], hT[:, b * T:(b + 1) * T], cw2[:, :],
                                start=True, stop=True)
            ins.then_inc(comp_done, 1)
            pe.wait_ge(onehot_ready, B)
            for half in range(2):
                for q in range(HB):
                    ins = pe.transpose(core.bank[2 + half][0:NT, q * T:(q + 1) * T], onehot[:, half * HB + q, :],
                                       core.ident[0:T, 0:T])
                ins.then_inc(onehot_turned, 1)
            pe.wait_ge(onehotT_ready, 2)
            for b in range(B):
                if b >= 2:
                    pe.wait_ge(prm_ready, b - 1)
                pe.matmul(core.bank[b % 2][0:T, 0:TW], onehotT[:, b * T:(b + 1) * T], table[:, :],
                          start=True, stop=True).then_inc(prm_done, 1)


def store(nc, core, out):
    with ExitStack() as ctx:
        out_stored = core.sem("out_stored")
        block = ctx.enter_context(nc.Block())

        @block.sync
        def _(sp):
            sp.dma_start(out.rearrange("b t d -> t b d"), core.x[:, :, :]).then_inc(out_stored, 16)
            sp.wait_ge(out_stored, 16)


PHASES = range(1, 9)


def program(nc, a, out):
    with ExitStack() as ctx:
        core = Core(nc, ctx)
        setup(nc, core, a)
        with ExitStack() as early:
            ctx_zT = early.enter_context(nc.sbuf_tensor("ctx_zT", [P, DC, B * S], F32))
            context_norm(nc, core, a, ctx_zT)
            if 1 in PHASES:
                latent_attention(nc, core, a, ctx_zT, "L0", True)
            if 2 in PHASES:
                routed_experts(nc, core, a, "F0", 16, 512, 1, ACT.Silu, True)
            if 3 in PHASES:
                causal_attention(nc, core, a)
            if 4 in PHASES:
                quantized_ffn(nc, core, a)
            if 5 in PHASES:
                latent_attention(nc, core, a, ctx_zT, "L2", False)
        core.recycle()
        if 6 in PHASES:
            routed_experts(nc, core, a, "F2", 8, 1024, 2, ACT.Gelu, False)
        if 7 in PHASES:
            slot_attention(nc, core, a)
        if 8 in PHASES:
            tile_ffn(nc, core, a)
        store(nc, core, out)


def arrays_of(i):
    import numpy as np

    def chunks(w):
        return w.reshape(w.shape[0] // P, P, w.shape[1]).transpose(1, 0, 2)

    def rows(v, n=T):
        return np.broadcast_to(v.reshape(1, -1), (n, v.size))

    def cols(v):
        return v.reshape(-1, P).T

    a = {}
    a["x"] = i["x"].transpose(1, 0, 2)
    a["ctx_rows"] = i["ctx_1024"].reshape(B * SC, SP_, D).transpose(1, 0, 2)
    a["mask"] = np.broadcast_to(i["mask_BxS2_bk0"][None], (T, B, S))
    for L, g in (("L0", ("ln_x_g", "ln_x_b", "ln_l_g", "ln_l_b")), ("L2", ("g1", "b1", "g2", "b2"))):
        a[f"{L}_gains"] = np.stack([cols(i[f"{L}_xattn_{n}"]) for n in g], axis=1)
        a[f"{L}_wq"] = chunks(i[f"{L}_xattn_Wq"])
        a[f"{L}_wkv"] = chunks(i[f"{L}_xattn_Wkv"])
        a[f"{L}_wout"] = chunks(i[f"{L}_xattn_Wout"])
    a["L0_gain_o"] = rows(i["L0_xattn_ln_o_g"])
    a["L0_off_o"] = rows(i["L0_xattn_ln_o_b"])
    a["F0_gate"] = chunks(i["L0_ffn_Wg"].T)
    a["F0_w_up"] = i["L0_ffn_W1"].transpose(0, 2, 1).reshape(16, DC, P, 512).transpose(0, 2, 1, 3)
    a["F0_w_down"] = i["L0_ffn_W2"].transpose(0, 2, 1).reshape(16, 4, P, D).transpose(0, 2, 1, 3)
    a["F2_gate"] = chunks(i["L2_ffn_expert_tokens"].T)
    for n, k, w in (("up", 2, i["L2_ffn_W1"]), ("mid", 8, i["L2_ffn_W2"]), ("down", 8, i["L2_ffn_W3"])):
        a[f"F2_w_{n}"] = w.reshape(8, k, P, w.shape[2]).transpose(0, 2, 1, 3)
    a["F2_b_hid"] = np.stack([i[f"L2_ffn_b{n}"].reshape(8, 8, P).transpose(0, 2, 1) for n in (1, 2)], axis=2)
    a["F2_b_down"] = np.broadcast_to(i["L2_ffn_b3"][:, None, :], (8, P, D))
    a["A1_wqk"] = np.stack([chunks(i["L1_xattn_Wq"].T), chunks(i["L1_xattn_Wk"].T)], axis=1)
    a["A1_wv"], a["A1_wo"] = chunks(i["L1_xattn_Wv"].T), chunks(i["L1_xattn_Wo"].T)
    a["A1_bv"], a["A1_bo"] = rows(i["L1_xattn_bv"]), rows(i["L1_xattn_bo"])
    for n in ("bq", "bk"):
        a[f"A1_{n}"] = i[f"L1_xattn_{n}"].reshape(4, 4, 16).transpose(1, 2, 0)
    a["A1_ctxT"] = i["ctx_1024"][:, :T].reshape(N, DC, P).transpose(2, 1, 0)
    a["F1_w"] = np.stack([chunks(i[f"L1_ffn_w_{n}"]).reshape(P, -1) for n in ("gate", "up", "down")], axis=1)
    a["A3_wqkv"] = np.stack([chunks(i[f"L3_xattn_W{n}"].T) for n in "qkv"], axis=1)
    a["A3_wih"], a["A3_whh"] = chunks(i["L3_xattn_gru_wih"].T), chunks(i["L3_xattn_gru_whh"].T)
    a["A3_bih"], a["A3_bhh"] = rows(i["L3_xattn_gru_bih"]), rows(i["L3_xattn_gru_bhh"])
    a["A3_norms"] = np.stack([cols(i[f"L3_xattn_{n}_norm_w"]) for n in ("slot", "input")], axis=1)
    f = {n: i[f"L3_ffn_{n}"] for n in ("signatures_raw", "knot_values", "temperature", "compress_w1",
                                       "compress_b1", "compress_w2", "compress_b2", "spline_w1", "spline_b1",
                                       "spline_w2", "spline_b2", "directions", "norm_gamma", "norm_beta",
                                       "output_scale")}
    a["F3_raw"] = chunks(f["signatures_raw"].T)
    a["F3_knots"], a["F3_temp"] = rows(f["knot_values"]), rows(f["temperature"])
    a["F3_out_scale"] = rows(f["output_scale"])
    a["F3_cw1"], a["F3_cb1"] = chunks(f["compress_w1"]), f["compress_b1"].reshape(-1, 1)
    a["F3_cw2"] = f["compress_w2"]
    a["F3_cb2"] = np.broadcast_to(f["compress_b2"].reshape(1, 1, 2), (T, B, 2))
    a["F3_table"] = np.concatenate([f["spline_w1"].reshape(64, 32), f["spline_b1"], f["spline_w2"].reshape(64, 16),
                                    f["spline_b2"], f["directions"]], axis=1)
    a["F3_gamma"], a["F3_beta"] = rows(f["norm_gamma"]), rows(f["norm_beta"])
    return {k: np.ascontiguousarray(v) for k, v in a.items()}


def kernel(**inputs):
    import numpy as np
    import concourse.bacc as bacc
    from concourse.bass_utils import run_bass_kernel_spmd

    nc = bacc.Bacc("TRN2", target_bir_lowering=False, num_devices=1)
    arrays = arrays_of({k: np.asarray(v) for k, v in inputs.items()})
    aps = {k: nc.dram_tensor(f"in_{k}", v.shape, mybir.dt.from_np(v.dtype), kind="ExternalInput").ap()
           for k, v in arrays.items()}
    out = nc.dram_tensor("out", (B, T, D), F32, kind="ExternalOutput").ap()
    program(nc, aps, out)
    r = run_bass_kernel_spmd(nc, [{f"in_{k}": v for k, v in arrays.items()}], core_ids=[0])
    return r.results[0]["out"]
```

```python
from contextlib import ExitStack

import concourse.bass as bass
from concourse import mybir

F32 = mybir.dt.float32
U8 = mybir.dt.uint8
ALU = mybir.AluOpType
ACT = mybir.ActivationFunctionType
AX = mybir.AxisListType

B = 8
T = 112
S = 375
D = 256
P = 128
DC = D // P
N = B * T
HALF = N // 2
HB = B // 2
SC = 3
SP_ = S // SC
LN_EPS = 1e-5
RMS_EPS = 1e-6
F32R, U32 = mybir.dt.float32r, mybir.dt.uint32
UPPER = 0xFFFFF000
BIG = 3.0e38
ROUND = 12582912.0


class Link:

    def __init__(self, eng, sem):
        self.eng, self.sem, self.count, self.base = eng, sem, 0, None

    def __call__(self, ins):
        ins.then_inc(self.sem, 1)
        self.count += 1
        self.eng.wait_ge(self.sem, self.count if self.base is None else self.base + self.count)


class Core:

    def __init__(self, nc, ctx):
        def sb(name, shape, dt=F32):
            return ctx.enter_context(nc.sbuf_tensor(name, shape, dt))

        self.nc = nc
        self.sems = []
        self.x = sb("x_sb", [T, B, D])
        self.xn = sb("xn_sb", [T, B, D])
        self.xnT = sb("xnT_sb", [P, DC, N])
        self.ident = sb("ident", [P, P])
        self.stats = sb("stats", [T, B, 6])
        self.moments = sb("moments", [T, B, 2])
        self.std = sb("std", [T, B])
        self.rstd = sb("rstd", [T, B])
        self.carrier = sb("carrier", [T, 1])
        self.ctx_rrms = sb("ctx_rrms", [SP_, B * SC])
        self.bank = [ctx.enter_context(nc.psum_tensor(f"bank{i}", [P, 512], F32)) for i in range(8)]

    def sem(self, name):
        self.sems.append(self.nc.alloc_semaphore(name))
        return self.sems[-1]

    def recycle(self):
        self.nc.clear_and_free_semaphores(self.sems)
        self.nc.all_engine_barrier()
        self.sems = []


def layer_norm_rows(core, link, act_turn, dve, src, dst, sem_var, sem_std, seen=False):
    nc = core.nc
    if not seen:
        for b in range(B):
            last = nc.vector.bn_stats(core.stats[:, b, :], src[:, b, :])
        link(last)
    for b in range(B):
        last = nc.vector.bn_aggr(core.moments[:, b, :], core.stats[:, b, :])
    link(last)
    nc.vector.tensor_scalar(core.std[:, :], core.moments[:, :, 1], LN_EPS, None, ALU.add).then_inc(sem_var, 1)
    dve.wait_ge(sem_std, act_turn)
    link(nc.vector.reciprocal(core.rstd[:, :], core.std[:, :]))
    for b in range(B):
        last = nc.vector.tensor_scalar(dst[:, b, :], src[:, b, :], core.moments[:, b, 0:1],
                                       core.rstd[:, b:b + 1], ALU.subtract, ALU.mult)
    link(last)


def root_step(core, act, turn, sem_var, sem_std):
    act.wait_ge(sem_var, turn)
    core.nc.scalar.activation(core.std[:, :], core.std[:, :], ACT.Sqrt).then_inc(sem_std, 1)


def transpose_rows(core, pe, src, banks, sem_done):
    for c in range(DC):
        for half in range(2):
            for q in range(HB):
                ins = pe.transpose(core.bank[banks[2 * c + half]][:, q * T:(q + 1) * T],
                                   src[:, half * HB + q, c * P:(c + 1) * P], core.ident[0:T, 0:T])
            ins.then_inc(sem_done, 1)


def begin(nc, core, a, ctx_zT):
    with ExitStack() as ctx:
        sb = lambda n, s, dt=F32: ctx.enter_context(nc.sbuf_tensor(n, s, dt))
        sem = lambda n: core.sem(n)
        NT = B * SC
        rows = sb("cn_rows", [SP_, NT, D])
        stats = sb("cn_stats", [SP_, NT, 6])
        mom = sb("cn_mom", [SP_, NT, 2])
        std = sb("cn_std", [SP_, NT])
        rstd = sb("cn_rstd", [SP_, NT])
        loaded = [sem(f"cn_loaded{i}") for i in range(2)]
        order, var_ready, std_ready = sem("cn_order"), sem("cn_var"), sem("cn_std_ready")
        z_ready, turned, taken = sem("cn_z_ready"), sem("cn_turned"), sem("cn_taken")
        x_loaded, zeroed, ident_made = sem("x_loaded"), sem("ident_zeroed"), sem("ident_made")
        x_var, x_std = sem("x_var"), sem("x_std")
        block = ctx.enter_context(nc.Block())

        @block.gpsimd
        def _(pool):
            nc.gpsimd.memset(core.ident[:, :], 0.0).then_inc(zeroed, 1)
            pool.wait_ge(zeroed, 1)
            nc.gpsimd.affine_select(out=core.ident[:, :], in_=core.ident[:, :], compare_op=ALU.not_equal,
                                    fill=1.0, base=0, pattern=[[-1, P]], channel_multiplier=1
                                    ).then_inc(ident_made, 1)

        @block.sync
        def _(sp):
            sp.dma_start(core.x[:, :, :], a["x"]).then_inc(x_loaded, 16)
            for i in range(2):
                h = slice(i * NT // 2, (i + 1) * NT // 2)
                sp.dma_start(rows[:, h, :], a["ctx_rows"][:, h, :]).then_inc(loaded[i], 16)

        @block.vector
        def _(dve):
            link = Link(dve, order)
            dve.wait_ge(x_loaded, 16)
            layer_norm_rows(core, link, 1, dve, core.x, core.xn, x_var, x_std)
            layer_norm_rows(core, link, 2, dve, core.xn, core.xn, x_var, x_std)
            for t in range(NT):
                if t % (NT // 2) == 0:
                    dve.wait_ge(loaded[t // (NT // 2)], 16)
                last = nc.vector.bn_stats(stats[:, t, :], rows[:, t, :])
            link(last)
            for t in range(NT):
                last = nc.vector.bn_aggr(mom[:, t, :], stats[:, t, :])
            link(last)
            rms = core.ctx_rrms
            link(nc.vector.tensor_tensor(rms[:, :], mom[:, :, 0], mom[:, :, 0], ALU.mult))
            link(nc.vector.tensor_tensor(rms[:, :], rms[:, :], mom[:, :, 1], ALU.add))
            nc.vector.tensor_scalar(rms[:, :], rms[:, :], RMS_EPS, None, ALU.add)
            nc.vector.tensor_scalar(std[:, :], mom[:, :, 1], LN_EPS, None, ALU.add).then_inc(var_ready, 1)
            dve.wait_ge(std_ready, 1)
            nc.vector.reciprocal(rms[:, :], rms[:, :])
            link(nc.vector.reciprocal(rstd[:, :], std[:, :]))
            for t in range(NT):
                nc.vector.tensor_scalar(rows[:, t, :], rows[:, t, :], mom[:, t, 0:1], rstd[:, t:t + 1],
                                        ALU.subtract, ALU.mult).then_inc(z_ready, 1)
                if t % SC == SC - 1 and t >= 2 * SC - 1:
                    g = t // SC - 1
                    dve.wait_ge(turned, 2 * g + 1)
                    nc.vector.tensor_copy(ctx_zT[:, 0, g * S:(g + 1) * S],
                                          core.bank[(2 * g) % 4][:, 0:S]).then_inc(taken, 1)
            dve.wait_ge(turned, 2 * B - 1)
            nc.vector.tensor_copy(ctx_zT[:, 0, (B - 1) * S:B * S],
                                  core.bank[(2 * B - 2) % 4][:, 0:S]).then_inc(taken, 1)

        @block.scalar
        def _(act):
            for turn in (1, 2):
                root_step(core, act, turn, x_var, x_std)
            act.wait_ge(var_ready, 1)
            nc.scalar.activation(core.ctx_rrms[:, :], core.ctx_rrms[:, :], ACT.Sqrt)
            nc.scalar.activation(std[:, :], std[:, :], ACT.Sqrt).then_inc(std_ready, 1)
            for g in range(B):
                act.wait_ge(turned, 2 * g + 2)
                nc.scalar.activation(ctx_zT[:, 1, g * S:(g + 1) * S], core.bank[(2 * g + 1) % 4][:, 0:S],
                                     ACT.Copy).then_inc(std_ready, 1)

        @block.tensor
        def _(pe):
            pe.wait_ge(ident_made, 1)
            for g in range(B):
                pe.wait_ge(z_ready, SC * (g + 1))
                for c in range(DC):
                    if g >= 2 and c == 0:
                        pe.wait_ge(taken, g - 1)
                    if g >= 2 and c == 1:
                        pe.wait_ge(std_ready, g)
                    for k in range(SC):
                        ins = pe.transpose(core.bank[(2 * g + c) % 4][:, k * SP_:(k + 1) * SP_],
                                           rows[:, g * SC + k, c * P:(c + 1) * P], core.ident[0:SP_, 0:SP_])
                    ins.then_inc(turned, 1)


def latent_attention(nc, core, a, ctx_zT, L, masked, normed):
    H, HD = 16, 64
    INNER = H * HD
    KEYS = S + T
    KC = 4
    KL = [min(P, KEYS - k * P) for k in range(KC)]
    JC = INNER // P
    with ExitStack() as ctx:
        sb = lambda n, s, dt=F32: ctx.enter_context(nc.sbuf_tensor(f"{L}_{n}", s, dt))
        sem = lambda n: core.sem(f"{L}_{n}")
        wq = sb("wq", [P, DC, INNER])
        wout = sb("wout", [P, JC, D])
        gains = sb("gains", [P, 4, DC])
        kvT = sb("kvT", [P, DC, KEYS])
        qT, kT = sb("qT", [P, JC, T]), sb("kT", [P, JC, KEYS])
        v = sb("v", [P, KC, INNER])
        probs = sb("probs", [T, 4, KEYS])
        probsT = sb("probsT", [P, 4, KC, T])
        peak, npeak, total = sb("peak", [T, H]), sb("npeak", [T, H]), sb("total", [T, H])
        rtotal = sb("rtotal", [T, H])
        heads, headsT = sb("heads", [T, INNER]), sb("headsT", [P, JC, T])
        EVEN = KEYS + KEYS % 2
        w_parts = [sb(f"wkv_{n}", [P, DC, 2 * INNER], F32R) for n in ("high", "low")]
        kv_parts = [sb(f"kvT_{n}", [P, DC, EVEN], F32R) for n in ("high", "low")]
        bits = sb("bits", [P, INNER], U32)
        wkv = v.rearrange("p (c k) i -> p c (k i)", c=DC)
        if masked:
            mask_u8 = sb("mask_u8", [T, B, S], U8)
            bias = sb("bias", [T, KEYS])
            masked_s = sb("masked_s", [T, 4, KEYS])
            gain_o, off_o = sb("gain_o", [T, D]), sb("off_o", [T, D])
            raw = sb("raw", [T, B, D])
        w_loaded, wkv_loaded, w_split = sem("w_loaded"), sem("wkv_loaded"), sem("w_split")
        small_loaded = sem("small_loaded")
        dve_order, var_ready, std_ready = sem("dve_order"), sem("var_ready"), sem("std_ready")
        turned, latents_ready, kv_ready = sem("turned"), sem("latents_ready"), sem("kv_ready")
        proj_done, qk_taken, v_taken = sem("proj_done"), sem("qk_taken"), sem("v_taken")
        scores_done, peak_ready, exp_done = sem("scores_done"), sem("peak_ready"), sem("exp_done")
        probs_turned, pv_done = sem("probs_turned"), sem("pv_done")
        even_ready, odd_ready = sem("even_ready"), sem("odd_ready")
        heads_ready, heads_turned, headsT_ready = sem("heads_ready"), sem("heads_turned"), sem("headsT_ready")
        out_done, out_taken = sem("out_done"), sem("out_taken")
        QG, KG, VG = 2, JC, 2 * KC
        G = QG + KG + VG
        NORMS = 0 if normed else 2
        NP = H // 2
        TURNED, HEADS, OUT = (4, 5), (6, 7), 7
        block = ctx.enter_context(nc.Block())

        @block.sync
        def _(sp):
            sp.dma_start(wkv, a[f"{L}_wkv"]).then_inc(wkv_loaded, 16)
            sp.dma_start(gains[:, :, :], a[f"{L}_gains"]).then_inc(small_loaded, 16)
            if masked:
                sp.dma_start(mask_u8[:, :, :], a["mask"]).then_inc(small_loaded, 16)
                sp.dma_start(gain_o[:, :], a[f"{L}_gain_o"]).then_inc(small_loaded, 16)
                sp.dma_start(off_o[:, :], a[f"{L}_off_o"]).then_inc(small_loaded, 16)
            sp.dma_start(wq[:, :, :], a[f"{L}_wq"]).then_inc(w_loaded, 16)
            sp.dma_start(wout[:, :, :], a[f"{L}_wout"]).then_inc(w_loaded, 16)

        @block.vector
        def _(dve):
            link = Link(dve, dve_order)
            for n in range(NORMS):
                layer_norm_rows(core, link, n + 1, dve, core.xn if n else core.x, core.xn, var_ready, std_ready,
                                seen=n == 0)
            dve.wait_ge(small_loaded, 64 if masked else 16)
            for c in range(DC):
                for half in range(2):
                    dve.wait_ge(turned, 2 * c + half + 1)
                    last = nc.vector.tensor_scalar(
                        core.xnT[:, c, half * HALF:(half + 1) * HALF], core.bank[4 + 2 * c + half][:, 0:HALF],
                        gains[:, 2, c:c + 1], gains[:, 3, c:c + 1], ALU.mult, ALU.add)
            link(last)
            if masked:
                link(nc.vector.memset(bias[:, :], 0.0))
                link(nc.vector.tensor_tensor(core.x[:, :, :], core.x[:, :, :],
                                             off_o[:, :].unsqueeze(1).broadcast_to([T, B, D]), ALU.add))

            def split(whole, high, low):
                upper = bits[:, 0:whole.shape[-1]]
                link(nc.vector.tensor_scalar(upper, whole.bitcast(U32), UPPER, None, ALU.bitwise_and))
                link(nc.vector.tensor_copy(high, upper.bitcast(F32)))
                return nc.vector.tensor_tensor(low, whole, high.bitcast(F32), ALU.subtract)

            def prepare(b):
                for c in range(DC):
                    nc.vector.tensor_scalar(kvT[:, c, 0:S], ctx_zT[:, c, bass.ds(b * S, S)],
                                            gains[:, 0, c:c + 1], gains[:, 1, c:c + 1], ALU.mult, ALU.add)
                link(nc.vector.tensor_copy(kvT[:, :, S:KEYS], core.xnT[:, :, bass.ds(b * T, T)]))

            def split_chunk(c):
                split(kvT[:, c, :], *[part[:, c, 0:KEYS] for part in kv_parts]).then_inc(kv_ready, 1)

            for part in kv_parts if EVEN > KEYS else ():
                link(nc.vector.tensor_scalar(part[:, :, KEYS:EVEN], core.xnT[:, :, 0:EVEN - KEYS], 0.0, None,
                                             ALU.mult))
            prepare(0)
            for c in range(DC):
                split_chunk(c)
            dve.wait_ge(wkv_loaded, 16)
            for half in range(2):
                cols = slice(half * INNER, (half + 1) * INNER)
                for c in range(DC):
                    if c or half:
                        dve.wait_ge(w_split, half * DC + c)
                    split(wkv[:, c, cols], *[part[:, c, cols] for part in w_parts]).then_inc(w_split, 1)

            def tail(b):
                dve.wait_ge(exp_done, b * NP + NP)
                link(nc.vector.reciprocal(rtotal[:, :], total[:, :]))
                dve.wait_ge(pv_done, b * NP + NP)
                for g in range(2):
                    nc.vector.tensor_tensor(
                        heads[:, g * 512:(g + 1) * 512].rearrange("p (h d) -> p h d", d=HD),
                        core.bank[HEADS[g]][0:T, :].rearrange("p (h d) -> p h d", d=HD),
                        rtotal[:, g * 8:(g + 1) * 8].unsqueeze(2).broadcast_to([T, 8, HD]),
                        ALU.mult).then_inc(heads_ready, 1)

            def take_product(b):
                dve.wait_ge(out_done, b + 1)
                if masked:
                    nc.vector.tensor_copy(raw[:, b, :], core.bank[OUT][0:T, 0:D])
                    nc.vector.bn_stats(core.stats[:, b, :], core.bank[OUT][0:T, 0:D]).then_inc(out_taken, 1)
                else:
                    link(nc.vector.tensor_tensor(core.x[:, b, :], core.x[:, b, :], core.bank[OUT][0:T, 0:D],
                                                 ALU.add))
                    nc.vector.memset(core.carrier[:, :], 0.0)
                    nc.vector.bn_stats(core.stats[:, b, :], core.x[:, b, :]).then_inc(out_taken, 1)

            def find_peaks(b, p):
                dve.wait_ge(scores_done, b * NP + p + 1)
                if masked and p >= 2:
                    dve.wait_ge(exp_done, b * NP + p - 1)
                if masked:
                    nc.vector.memset(core.carrier[:, :], 0.0)
                for h in (2 * p, 2 * p + 1):
                    src = core.bank[(h + 2) % 4][0:T, 0:KEYS]
                    if masked:
                        last = nc.vector.tensor_tensor_reduce(masked_s[:, h % 4, :], src, bias[:, :], 1.0,
                                                              -BIG, ALU.add, ALU.max, peak[:, h:h + 1])
                    else:
                        last = nc.vector.tensor_reduce(npeak[:, h:h + 1], src, AX.X, ALU.max, negate=True)
                if masked:
                    link(last)
                    last = nc.vector.tensor_scalar(npeak[:, 2 * p:2 * p + 2], peak[:, 2 * p:2 * p + 2],
                                                   -1.0, None, ALU.mult)
                last.then_inc(peak_ready, 1)

            def batch(b, first, last_batch):
                if not first:
                    tail(b - 1)
                if masked:
                    link(nc.vector.tensor_scalar(bias[:, 0:S], mask_u8[:, b, :], -1.0, BIG, ALU.add, ALU.mult))
                for n in range(VG):
                    dve.wait_ge(proj_done, b * G + QG + KG + n + 1)
                    nc.vector.tensor_copy(v[0:KL[n // 2], n // 2, (n % 2) * 512:(n % 2 + 1) * 512],
                                          core.bank[(QG + KG + n) % 4][0:KL[n // 2], :]).then_inc(v_taken, 1)
                find_peaks(b, 0)
                for p in range(NP):
                    if p + 1 < NP:
                        find_peaks(b, p + 1)
                    if p == 0 and not first:
                        take_product(b - 1)
                    dve.wait_ge(probs_turned, b * NP + p + 1)
                    if p >= 2:
                        dve.wait_ge(pv_done, b * NP + p - 1)
                    nc.vector.tensor_copy(
                        probsT[:, 2 * (p % 2), :, :],
                        core.bank[TURNED[0]][:, 0:KC * T].rearrange("p (k t) -> p k t", t=T)
                        ).then_inc(even_ready, 1)
                    if not last_batch:
                        if p == 2:
                            prepare(b + 1)
                        if p in (3, 4):
                            split_chunk(p - 3)

            per_batch = 1 + (1 + NP if masked else 1) + 1 + 2 * DC
            batch(0, True, False)
            start = link.count
            with dve.Fori(1, B - 1) as b:
                link.base = (b - 1) * per_batch
                batch(b, False, False)
                assert link.count == start + per_batch
            link.base, link.count = None, start + (B - 2) * per_batch
            batch(B - 1, False, True)
            tail(B - 1)
            take_product(B - 1)
            if masked:
                dve.wait_ge(out_taken, B)
                layer_norm_rows(core, link, NORMS + 1, dve, raw, raw, var_ready, std_ready, seen=True)
                link(nc.vector.tensor_tensor(raw[:, :, :], raw[:, :, :],
                                             gain_o[:, :].unsqueeze(1).broadcast_to([T, B, D]), ALU.mult))
                nc.vector.tensor_tensor(core.x[:, :, :], core.x[:, :, :], raw[:, :, :], ALU.add)

        @block.scalar
        def _(act):
            for n in range(NORMS):
                root_step(core, act, n + 1, var_ready, std_ready)

            def keys(b, j):
                act.wait_ge(proj_done, b * G + QG + j + 1)
                nc.scalar.activation(kT[:, j, :], core.bank[(QG + j) % 4][:, 0:KEYS],
                                     ACT.Copy).then_inc(qk_taken, 1)

            def turned_heads(b):
                for g in range(2):
                    act.wait_ge(heads_turned, b * 2 + g + 1)
                    nc.scalar.activation(headsT[:, 4 * g:4 * g + 4, :],
                                         core.bank[TURNED[g]][:, 0:4 * T].rearrange("p (j t) -> p j t", t=T),
                                         ACT.Copy).then_inc(headsT_ready, 1)

            def exponentials(b, p):
                act.wait_ge(peak_ready, b * NP + p + 1)
                if p >= 2:
                    act.wait_ge(probs_turned, b * NP + p - 1)
                for h in (2 * p, 2 * p + 1):
                    src = masked_s[:, h % 4, :] if masked else core.bank[(h + 2) % 4][0:T, 0:KEYS]
                    ins = nc.scalar.activation(probs[:, h % 4, :], src, ACT.Exp, bias=npeak[:, h:h + 1],
                                               accum_out=total[:, h:h + 1])
                ins.then_inc(exp_done, 1)

            def batch(b, first):
                for g in range(QG):
                    act.wait_ge(proj_done, b * G + g + 1)
                    nc.scalar.activation(qT[:, 4 * g:4 * g + 4, :],
                                         core.bank[g][:, 0:4 * T].rearrange("p (j t) -> p j t", t=T),
                                         ACT.Copy, scale=HD ** -0.5).then_inc(qk_taken, 1)
                for j in range(JC):
                    if j == JC // 2 and not first:
                        turned_heads(b - 1)
                    keys(b, j)
                if not first:
                    act.wait_ge(heads_ready, b * 2)
                exponentials(b, 0)
                for p in range(NP):
                    if p + 1 < NP:
                        exponentials(b, p + 1)
                    act.wait_ge(probs_turned, b * NP + p + 1)
                    nc.scalar.activation(
                        probsT[:, 2 * (p % 2) + 1, :, :],
                        core.bank[TURNED[1]][:, 0:KC * T].rearrange("p (k t) -> p k t", t=T),
                        ACT.Copy).then_inc(odd_ready, 1)

            batch(0, True)
            with act.Fori(1, B) as b:
                batch(b, False)
            turned_heads(B - 1)
            if masked:
                root_step(core, act, NORMS + 1, var_ready, std_ready)

        @block.tensor
        def _(pe):
            if NORMS:
                pe.wait_ge(dve_order, 3 + 4)
            transpose_rows(core, pe, core.xn, [4, 5, 6, 7], turned)
            pe.wait_ge(w_loaded, 32)

            def project(out, operands):
                pairs = [(w_parts[m], kv_parts[n]) for m, n in ((0, 0), (0, 1), (1, 0))]
                steps = [(w, kv, c) for w, kv in pairs for c in range(DC)]
                for n, step in enumerate(steps):
                    left, right = operands(*step)
                    ins = pe.matmul(out, left, right, start=(n == 0), stop=(n == len(steps) - 1))
                return ins

            def keys(b, j):
                n = QG + j
                if n >= 4:
                    pe.wait_ge(qk_taken, b * (QG + KG) + n - 3)
                ins = project(core.bank[n % 4][:, 0:EVEN],
                              lambda w, kv, c: (w[:, c, j * P:(j + 1) * P], kv[:, c, :]))
                ins.then_inc(proj_done, 1)

            def turn_heads(b):
                for g in range(2):
                    pe.wait_ge(heads_ready, b * 2 + 2)
                    for j in range(4 * g, 4 * g + 4):
                        ins = pe.transpose(core.bank[TURNED[g]][:, (j % 4) * T:(j % 4 + 1) * T],
                                           heads[:, j * P:(j + 1) * P], core.ident[0:T, 0:T])
                    ins.then_inc(heads_turned, 1)

            def product(b):
                pe.wait_ge(headsT_ready, b * 2 + 2)
                for j in range(JC):
                    ins = pe.matmul(core.bank[OUT][0:T, 0:D], headsT[:, j, :], wout[:, j, :],
                                    start=(j == 0), stop=(j == JC - 1))
                ins.then_inc(out_done, 1)

            def scores(b, p):
                if p >= 2:
                    pe.wait_ge(peak_ready, b * NP + p - 1)
                    if not masked:
                        pe.wait_ge(exp_done, b * NP + p - 1)
                for h in (2 * p, 2 * p + 1):
                    r = slice((h % 2) * HD, (h % 2 + 1) * HD)
                    ins = pe.matmul(core.bank[(h + 2) % 4][0:T, 0:KEYS], qT[r, h // 2, :], kT[r, h // 2, :],
                                    start=True, stop=True)
                ins.then_inc(scores_done, 1)

            def values(b, p):
                pe.wait_ge(even_ready, b * NP + p + 1)
                pe.wait_ge(odd_ready, b * NP + p + 1)
                for h in (2 * p, 2 * p + 1):
                    for k in range(KC):
                        ins = pe.matmul(core.bank[HEADS[h // 8]][0:T, (h % 8) * HD:(h % 8 + 1) * HD],
                                        probsT[0:KL[k], h % 4, k, :],
                                        v[0:KL[k], k, h * HD:(h + 1) * HD],
                                        start=(k == 0), stop=(k == KC - 1))
                ins.then_inc(pv_done, 1)

            def batch(b, first):
                pe.wait_ge(kv_ready, b * DC + DC)
                for g in range(QG):
                    for j in range(4 * g, 4 * g + 4):
                        for c in range(DC):
                            ins = pe.matmul(core.bank[g][:, (j % 4) * T:(j % 4 + 1) * T],
                                            wq[:, c, j * P:(j + 1) * P], kvT[:, c, S:KEYS],
                                            start=(c == 0), stop=(c == DC - 1))
                    ins.then_inc(proj_done, 1)
                if first:
                    pe.wait_ge(w_split, DC)
                for j in range(JC):
                    if j == JC // 2 and not first:
                        turn_heads(b - 1)
                    keys(b, j)
                if first:
                    pe.wait_ge(w_split, 2 * DC)
                for i in range(VG):
                    n = QG + KG + i
                    k, hf = i // 2, i % 2
                    if i < 4:
                        pe.wait_ge(qk_taken, b * (QG + KG) + n - 3)
                    else:
                        pe.wait_ge(v_taken, b * VG + i - 3)
                    end = min((k + 1) * P, EVEN)
                    ins = project(core.bank[n % 4][0:end - k * P, :],
                                  lambda w, kv, c: (kv[:, c, k * P:end],
                                                    w[:, c, INNER + hf * 512:INNER + (hf + 1) * 512]))
                    ins.then_inc(proj_done, 1)
                pe.wait_ge(v_taken, b * VG + VG - 2)
                scores(b, 0)
                pe.wait_ge(v_taken, b * VG + VG)
                scores(b, 1)
                if not first:
                    product(b - 1)
                for p in range(NP):
                    pe.wait_ge(exp_done, b * NP + p + 1)
                    if p >= 1:
                        pe.wait_ge(even_ready, b * NP + p)
                        pe.wait_ge(odd_ready, b * NP + p)
                    for h in (2 * p, 2 * p + 1):
                        for k in range(KC):
                            ins = pe.transpose(core.bank[TURNED[h % 2]][0:KL[k], k * T:(k + 1) * T],
                                               probs[:, h % 4, k * P:k * P + KL[k]], core.ident[0:T, 0:T])
                    ins.then_inc(probs_turned, 1)
                    if p + 2 < NP:
                        scores(b, p + 2)
                    if p >= 1:
                        values(b, p - 1)
                values(b, NP - 1)

            batch(0, True)
            with pe.Fori(1, B) as b:
                batch(b, False)
            turn_heads(B - 1)
            product(B - 1)


def norm_to_features(core, pe, order, turned, seen=False):
    pe.wait_ge(order, 3 if seen else 4)
    transpose_rows(core, pe, core.xn, [0, 1, 2, 3], turned)


def take_features(core, dve, turned, xT_ready, first=1):
    for c in range(DC):
        for half in range(2):
            dve.wait_ge(turned, 2 * c + half + first)
            core.nc.vector.tensor_copy(core.xnT[:, c, half * HALF:(half + 1) * HALF],
                                       core.bank[2 * c + half][:, 0:HALF]).then_inc(xT_ready, 1)


def count_down(nc, pool, tile, E, sem):
    nc.gpsimd.iota(tile, pattern=[[0, B], [-1, E]], base=E, channel_multiplier=0,
                   allow_small_or_imprecise_dtypes=True).then_inc(sem, 1)


def top_two(nc, link, value, E, places, peak, rank, pick1, pick2, work):
    over = lambda t: t.unsqueeze(2).broadcast_to([T, B, E])
    for pick, src in ((pick1, value), (pick2, work)):
        link(nc.vector.tensor_reduce(peak[:, :], src[:, :, :], AX.X, ALU.max))
        link(nc.vector.tensor_tensor(pick[:, :, :], src[:, :, :], over(peak[:, :]), ALU.is_equal))
        link(nc.vector.tensor_tensor(pick[:, :, :], pick[:, :, :], places[:, :, :], ALU.mult))
        link(nc.vector.tensor_reduce(rank[:, :], pick[:, :, :], AX.X, ALU.max))
        link(nc.vector.tensor_tensor(pick[:, :, :], places[:, :, :], over(rank[:, :]), ALU.is_equal))
        if pick is pick1:
            link(nc.vector.tensor_scalar(work[:, :, :], pick1[:, :, :], -BIG, None, ALU.mult))
            link(nc.vector.tensor_tensor(work[:, :, :], work[:, :, :], value[:, :, :], ALU.add))


def routed_experts(nc, core, a, L, E, I, hidden, act_func, softmax, aside=None):
    IC = I // P
    TILES = (2 * N - E) // P + E
    NBUF = 3 if hidden == 2 else 5
    EARLY = 1 if hidden == 2 else 3
    ROUNDS = -(-TILES // NBUF)
    TILES = ROUNDS * NBUF
    MG = 2
    GR = IC // MG
    with ExitStack() as ctx:
        sb = lambda n, s, dt=F32: ctx.enter_context(nc.sbuf_tensor(f"{L}_{n}", s, dt))
        sem = lambda n: core.sem(f"{L}_{n}")
        gate = sb("gate", [P, DC, E])
        w_up, w_down = sb("w_up", [P, NBUF, DC, I]), sb("w_down", [P, NBUF, IC, D])
        offsets = hidden == 2
        if offsets:
            w_mid = sb("w_mid", [P, NBUF, IC, I])
            b_hid = sb("b_hid", [P, NBUF, 2, IC])
            b_down = sb("b_down", [P, NBUF, D])
        rows = sb("rows", [P, NBUF, D])
        rowsT = sb("rowsT", [P, DC, P])
        h1T = sb("h1T", [P, IC, P])
        h2T = sb("h2T", [P, IC, P]) if offsets else h1T
        result = sb("result", [P, NBUF, D])
        zeros = sb("zeros", [P, D])
        if offsets:
            got = w_mid[0:T, 0].rearrange("p k i -> p (k i)")[:, 0:2 * B * D].rearrange(
                "p (n b d) -> p n b d", n=2, b=B)
        else:
            got = sb("got", [T, 2, B, D])
        places, prob, work = sb("places", [T, B, E]), sb("prob", [T, B, E]), sb("work", [T, B, E])
        pick1, pick2, both = sb("pick1", [T, B, E]), sb("pick2", [T, B, E]), sb("both", [T, B, E])
        peak, rank, total = sb("peak", [T, B]), sb("rank", [T, B]), sb("total", [T, B])
        weight = sb("weight", [T, 2, B])
        earlier, ones = sb("earlier", [T, T]), sb("ones", [T, T])
        here, upto = sb("here", [T, E, B]), sb("upto", [T, E, B])
        going = sb("going", [T, E, B])
        steps, over_steps = sb("steps", [T, E, N // P]), sb("over_steps", [T, E, N // P])
        reached, at = sb("reached", [1, TILES, E - 1]), sb("at", [T, B, E])
        tiles, first = sb("tiles", [T, E]), sb("first", [T, E])
        slot = sb("slot", [T, B, E])
        slot_f, slot_u = sb("slot_f", [T, 2, B]), sb("slot_u", [T, 2, B], mybir.dt.uint32)
        tile_no, owner = sb("tile_no", [1, TILES]), sb("owner", [1, TILES])
        owner_i = sb("owner_i", [1, TILES], mybir.dt.int32)
        sorted_rows = nc.dram_tensor(f"{L}_sorted_rows", ((TILES + 1) * P, D), F32).ap()
        sorted_out = nc.dram_tensor(f"{L}_sorted_out", (TILES * P, D), F32).ap()

        gate_loaded = sem("gate_loaded")
        w_loaded = [sem(f"w_loaded{i}") for i in range(NBUF)]
        x_loaded = [sem(f"x_loaded{i}") for i in range(NBUF)]
        dve_order, var_ready, std_ready, turned = sem("dve_order"), sem("var_ready"), sem("std_ready"), sem("turned")
        xT_ready, made, logits_done = sem("xT_ready"), sem("made"), sem("logits_done")
        shifted, exp_done = sem("shifted"), sem("exp_done")
        both_ready, prefix_done = sem("both_ready"), sem("prefix_done")
        slots_ready, owner_ready = sem("slots_ready"), sem("owner_ready")
        zero_made, zero_filled, scattered = sem("zero_made"), sem("zero_filled"), sem("scattered")
        rows_turned, rowsT_ready = sem("rows_turned"), sem("rowsT_ready")
        hid_done, h_ready, down_done, result_ready = sem("hid_done"), sem("h_ready"), sem("down_done"), sem("result_ready")
        stored = sem("stored")
        gathered = [sem(f"gathered{b}") for b in range(B)]
        W_DMAS = 5 if offsets else 2
        HG = hidden * GR
        DOWN = (4, 5, 7)
        block = ctx.enter_context(nc.Block())

        @block.sync
        def _(sp):
            sp.dma_start(gate[:, :, :], a[f"{L}_gate"]).then_inc(gate_loaded, 16)
            if aside:
                aside.load(sp, a)
            sp.wait_ge(zero_made, 1)
            sp.dma_start(sorted_rows.rearrange("(t p) d -> p t d", p=P),
                         zeros[:, :].unsqueeze(1).broadcast_to([P, TILES + 1, D])).then_inc(zero_filled, 16)

            def load_weights(tile, s):
                e = sp.value_load(owner_i[0:1, bass.ds(tile, 1)], min_val=0, max_val=E - 1)
                e = bass.ds(e, 1)
                sp.dma_start(w_up[:, s], a[f"{L}_w_up"][e][0]).then_inc(w_loaded[s], 16)
                if offsets:
                    sp.dma_start(b_hid[:, s], a[f"{L}_b_hid"][e][0]).then_inc(w_loaded[s], 16)
                    sp.dma_start(w_mid[:, s], a[f"{L}_w_mid"][e][0]).then_inc(w_loaded[s], 16)
                    sp.dma_start(b_down[:, s], a[f"{L}_b_down"][e][0]).then_inc(w_loaded[s], 16)
                sp.dma_start(w_down[:, s], a[f"{L}_w_down"][e][0]).then_inc(w_loaded[s], 16)

            def load_rows(tile, s):
                sp.dma_start(rows[:, s, :], sorted_rows[bass.ds(tile * P, P), :]).then_inc(x_loaded[s], 16)

            def store_result(tile, s):
                sp.wait_ge(result_ready, tile + 1)
                sp.dma_start(sorted_out[bass.ds(tile * P, P), :], result[:, s, :]).then_inc(stored, 16)

            sp.wait_ge(owner_ready, 1)
            for s in range(EARLY):
                load_weights(s, s)
            sp.wait_ge(scattered, 16 * 2 * B)
            for s in range(NBUF):
                if s >= EARLY:
                    load_weights(s, s)
                load_rows(s, s)
            with sp.Fori(0, ROUNDS - 1) as r:
                for s in range(NBUF):
                    store_result(r * NBUF + s, s)
                    load_weights(r * NBUF + NBUF + s, s)
                    load_rows(r * NBUF + NBUF + s, s)
            for s in range(NBUF):
                if s == 0:
                    sp.wait_ge(down_done, TILES - NBUF + 1)
                    load_rows(TILES, 0)
                store_result(TILES - NBUF + s, s)

        @block.gpsimd
        def _(pool):
            nc.gpsimd.memset(zeros[:, :], 0.0).then_inc(zero_made, 1)
            count_down(nc, pool, places[:, :, :], E, made)
            nc.gpsimd.iota(tile_no[:, :], pattern=[[1, TILES]], base=0, channel_multiplier=0,
                           allow_small_or_imprecise_dtypes=True).then_inc(made, 1)
            nc.gpsimd.memset(ones[:, :], 1.0).then_inc(made, 1)
            nc.gpsimd.iota(steps[:, :, :], pattern=[[0, E], [P, N // P]], base=0, channel_multiplier=0,
                           allow_small_or_imprecise_dtypes=True).then_inc(made, 1)
            nc.gpsimd.memset(going[:, :, 1:B], 1.0).then_inc(made, 1)
            nc.gpsimd.memset(going[:, :, 0:1], 0.0).then_inc(made, 1)
            pool.wait_ge(made, 6)
            nc.gpsimd.affine_select(out=earlier[:, :], in_=ones[:, :], compare_op=ALU.is_gt, fill=0.0, base=0,
                                    pattern=[[1, T]], channel_multiplier=-1).then_inc(made, 1)
            pool.wait_ge(zero_filled, 16)
            pool.wait_ge(slots_ready, 1)
            for n in range(2):
                for b in range(B):
                    nc.gpsimd.indirect_dma_start(
                        out=sorted_rows, out_offset=bass.IndirectOffsetOnAxis(slot_u[:, n, b:b + 1], 0),
                        in_=core.xn[:, b, :], in_offset=None).then_inc(scattered, 16)
            pool.wait_ge(stored, 16 * (NBUF + TILES))
            for b in range(B):
                for n in range(2):
                    nc.gpsimd.indirect_dma_start(
                        out=got[:, n, b, :], out_offset=None, in_=sorted_out,
                        in_offset=bass.IndirectOffsetOnAxis(slot_u[:, n, b:b + 1], 0)).then_inc(gathered[b], 16)

        @block.vector
        def _(dve):
            link = Link(dve, dve_order)
            tt, ts, reduce = nc.vector.tensor_tensor, nc.vector.tensor_scalar, nc.vector.tensor_reduce
            layer_norm_rows(core, link, 1, dve, core.x, core.xn, var_ready, std_ready, seen=offsets)
            take_features(core, dve, turned, xT_ready)
            dve.wait_ge(logits_done, 1)
            logits = core.bank[4][0:T, 0:B * E].rearrange("p (b e) -> p b e", e=E)
            over = lambda t: t.unsqueeze(2).broadcast_to([T, B, E])
            if softmax:
                link(reduce(peak[:, :], logits, AX.X, ALU.max))
                tt(prob[:, :, :], logits, over(peak[:, :]), ALU.subtract).then_inc(shifted, 1)
                dve.wait_ge(exp_done, 1)
                link(reduce(total[:, :], prob[:, :, :], AX.X, ALU.add))
                link(nc.vector.reciprocal(total[:, :], total[:, :]))
                link(tt(prob[:, :, :], prob[:, :, :], over(total[:, :]), ALU.mult))
            else:
                link(nc.vector.tensor_copy(prob[:, :, :], logits))
            dve.wait_ge(made, 7)
            top_two(nc, link, prob, E, places, peak, rank, pick1, pick2, work)
            tt(both[:, :, :], pick1[:, :, :], pick2[:, :, :], ALU.add).then_inc(both_ready, 1)
            dve.wait_ge(prefix_done, 1)
            flat = lambda t: t.rearrange("p e b -> p (e b)")
            sums = core.bank[5][0:T, 0:B * E].rearrange("p (b e) -> p b e", e=E)
            link(nc.vector.tensor_copy(here[:, :, :], sums.rearrange("p b e -> p e b")))
            link(nc.vector.tensor_tensor_scan(flat(upto[:, :, :]), flat(going[:, :, :]), flat(here[:, :, :]), 0.0,
                                              ALU.mult, ALU.add))
            link(tt(over_steps[:, :, :], upto[:, :, B - 1].unsqueeze(2).broadcast_to([T, E, N // P]),
                    steps[:, :, :], ALU.is_gt))
            link(reduce(tiles[:, :], over_steps[:, :, :], AX.X, ALU.add))
            link(nc.vector.tensor_tensor_scan(first[:, :], ones[:, 0:E], tiles[:, :], 0.0, ALU.mult, ALU.add))
            link(tt(first[:, :], first[:, :], tiles[:, :], ALU.subtract))
            link(tt(slot[:, :, :], upto[:, :, :].rearrange("p e b -> p b e"), sums, ALU.subtract))
            link(tt(slot[:, :, :], slot[:, :, :],
                    core.bank[6][0:T, 0:B * E].rearrange("p (b e) -> p b e", e=E), ALU.add))
            link(nc.vector.scalar_tensor_tensor(out=slot[:, :, :], in0=first[:, :].unsqueeze(1).broadcast_to([T, B, E]),
                                                scalar=float(P), in1=slot[:, :, :], op0=ALU.mult, op1=ALU.add))
            for n, pick in enumerate((pick1, pick2)):
                link(tt(at[:, :, :], pick[:, :, :], slot[:, :, :], ALU.mult))
                link(reduce(slot_f[:, n, :], at[:, :, :], AX.X, ALU.add))
            nc.vector.tensor_copy(slot_u[:, :, :], slot_f[:, :, :]).then_inc(slots_ready, 1)
            link(tt(reached[:, :, :], tile_no[:, :].unsqueeze(2).broadcast_to([1, TILES, E - 1]),
                    first[0:1, 1:E].unsqueeze(1).broadcast_to([1, TILES, E - 1]), ALU.is_ge))
            link(reduce(owner[:, :], reached[:, :, :], AX.X, ALU.add))
            nc.vector.tensor_copy(owner_i[:, :], owner[:, :]).then_inc(owner_ready, 1)
            if softmax:
                for n, pick in enumerate((pick1, pick2)):
                    link(tt(work[:, :, :], pick[:, :, :], prob[:, :, :], ALU.mult))
                    link(reduce(weight[:, n, :], work[:, :, :], AX.X, ALU.add))
            else:
                link(nc.vector.memset(weight[:, :, :], 0.5))

            def take_rows(tile, s):
                dve.wait_ge(rows_turned, tile + 1)
                nc.vector.tensor_copy(rowsT[:, :, :],
                                      core.bank[6][:, 0:DC * P].rearrange("p (c t) -> p c t", t=P)
                                      ).then_inc(rowsT_ready, 1)

            def take_result(tile, s):
                dve.wait_ge(down_done, tile + 1)
                dve.wait_ge(stored, tile * 16 + 16)
                dst, src = result[:, s, :], core.bank[DOWN[s % 3]][:, 0:D]
                if offsets:
                    ins = tt(dst, src, b_down[:, s, :], ALU.add)
                else:
                    ins = nc.vector.tensor_copy(dst, src)
                ins.then_inc(result_ready, 1)

            if aside:
                for m in range(3):
                    aside.quantize(dve, link, m)
            nc.vector.engine_nop().then_inc(stored, 16 * NBUF)
            take_rows(0, 0)
            with dve.Fori(0, ROUNDS) as r:
                for s in range(NBUF):
                    take_rows(r * NBUF + s + 1, s + 1)
                    take_result(r * NBUF + s, s)
            for b in range(B):
                dve.wait_ge(gathered[b], 32)
                for n in range(2):
                    link(nc.vector.scalar_tensor_tensor(out=core.x[:, b, :], in0=got[:, n, b, :],
                                                        scalar=weight[:, n, b:b + 1], in1=core.x[:, b, :],
                                                        op0=ALU.mult, op1=ALU.add))
                nc.vector.bn_stats(core.stats[:, b, :], core.x[:, b, :])

        @block.scalar
        def _(act):
            root_step(core, act, 1, var_ready, std_ready)
            if softmax:
                act.wait_ge(shifted, 1)
                nc.scalar.activation(prob[:, :, :], prob[:, :, :], ACT.Exp).then_inc(exp_done, 1)
            with act.Fori(0, ROUNDS) as r:
                for s in range(NBUF):
                    if offsets:
                        act.wait_ge(w_loaded[s], r * 16 * W_DMAS + 16 * W_DMAS)
                    for g in range(HG):
                        layer, q = g // GR, g % GR
                        dst = (h1T, h2T)[layer]
                        act.wait_ge(hid_done, (r * NBUF + s) * HG + g + 1)
                        if offsets:
                            for m in range(q * MG, (q + 1) * MG):
                                ins = nc.scalar.activation(dst[:, m, :],
                                                           core.bank[g % 4][:, (m % MG) * P:(m % MG + 1) * P],
                                                           act_func, bias=b_hid[:, s, layer, m:m + 1])
                        else:
                            ins = nc.scalar.activation(
                                dst[:, q * MG:(q + 1) * MG, :],
                                core.bank[g % 4][:, 0:MG * P].rearrange("p (m t) -> p m t", t=P), act_func)
                        ins.then_inc(h_ready, 1)

        @block.tensor
        def _(pe):
            norm_to_features(core, pe, dve_order, turned, seen=offsets)
            pe.wait_ge(xT_ready, 4)
            pe.wait_ge(gate_loaded, 16)
            for b in range(B):
                for c in range(DC):
                    ins = pe.matmul(core.bank[4][0:T, b * E:(b + 1) * E], core.xnT[:, c, b * T:(b + 1) * T],
                                    gate[:, c, :], start=(c == 0), stop=(c == DC - 1))
            ins.then_inc(logits_done, 1)
            pe.wait_ge(both_ready, 1)
            pe.matmul(core.bank[5][0:T, 0:B * E], ones[:, :], both[:, :, :].rearrange("p b e -> p (b e)"),
                      start=True, stop=True)
            pe.matmul(core.bank[6][0:T, 0:B * E], earlier[:, :], both[:, :, :].rearrange("p b e -> p (b e)"),
                      start=True, stop=True).then_inc(prefix_done, 1)

            def turn_rows(round_, s, tile):
                pe.wait_ge(x_loaded[s % NBUF], round_ * 16 + 16)
                for c in range(DC):
                    ins = pe.transpose(core.bank[6][:, c * P:(c + 1) * P], rows[:, s % NBUF, c * P:(c + 1) * P],
                                       core.ident[:, :])
                ins.then_inc(rows_turned, 1)

            pe.wait_ge(slots_ready, 1)
            turn_rows(0, 0, 0)
            with pe.Fori(0, ROUNDS) as r:
                for s in range(NBUF):
                    tile = r * NBUF + s
                    pe.wait_ge(w_loaded[s], r * 16 * W_DMAS + 16 * W_DMAS)
                    pe.wait_ge(rowsT_ready, tile + 1)
                    for layer in range(hidden):
                        w, src, K = ((w_up, None, DC), (w_mid if offsets else None, h1T, IC))[layer]
                        for q in range(GR):
                            g = layer * GR + q
                            if g >= 4:
                                pe.wait_ge(h_ready, tile * HG + g - 3)
                            for m in range(q * MG, (q + 1) * MG):
                                for k in range(K):
                                    if layer and q == 0 and m == 0 and k % MG == 0 and k:
                                        pe.wait_ge(h_ready, tile * HG + k // MG + 1)
                                    rhs = h1T[:, k, :] if layer else rowsT[:, k, :]
                                    ins = pe.matmul(core.bank[g % 4][:, (m % MG) * P:(m % MG + 1) * P],
                                                    w[:, s, k, m * P:(m + 1) * P], rhs,
                                                    start=(k == 0), stop=(k == K - 1))
                            ins.then_inc(hid_done, 1)
                    turn_rows(r + (1 if s + 1 == NBUF else 0), s + 1, tile + 1)
                    for k in range(IC):
                        if k % MG == 0:
                            pe.wait_ge(h_ready, tile * HG + (hidden - 1) * GR + k // MG + 1)
                        ins = pe.matmul(core.bank[DOWN[s % 3]][:, 0:D], h2T[:, k, :], w_down[:, s, k, :],
                                        start=(k == 0), stop=(k == IC - 1))
                    ins.then_inc(down_done, 1)


def causal_attention(nc, core, a):
    H, HD, PAD, L = 16, 16, 32, "A1"
    J = H // 4
    with ExitStack() as ctx:
        sb = lambda n, s, dt=F32: ctx.enter_context(nc.sbuf_tensor(f"{L}_{n}", s, dt))
        sem = lambda n: core.sem(f"{L}_{n}")
        wqk = sb("wqk", [P, 2, DC, D])
        padded = sb("padded", [P, 2, DC, H, PAD])
        wv, wo = sb("wv", [P, DC, D]), sb("wo", [P, DC, D])
        bqk = sb("bqk", [P, 2, J])
        bv, bo = sb("bv", [T, D]), sb("bo", [T, D])
        ctxT = sb("ctxT", [P, DC, N])
        rowsT = sb("rowsT", [P, DC, T])
        causal = sb("causal", [T, 4, T])
        qT, kT = sb("qT", [P, J, T]), sb("kT", [P, J, T])
        v = sb("v", [T, D])
        score, prob = sb("score", [T, J, 4, T]), sb("prob", [T, J, 4, T])
        probT = sb("probT", [T, J, 4, T])
        npeak, total, rtotal = sb("npeak", [T, H]), sb("total", [T, H]), sb("rtotal", [T, H])
        heads, headsT = sb("heads", [T, D]), sb("headsT", [P, DC, T])
        w_loaded = sem("w_loaded")
        dve_order, var_ready, std_ready, turned = sem("dve_order"), sem("var_ready"), sem("std_ready"), sem("turned")
        xT_ready, zeroed, masked = sem("xT_ready"), sem("zeroed"), sem("masked")
        padded_ready, rows_ready, proj_done = sem("padded_ready"), sem("rows_ready"), sem("proj_done")
        qk_ready, v_ready, scores_done = sem("qk_ready"), sem("v_ready"), sem("scores_done")
        peak_ready, exp_done, probs_turned = sem("peak_ready"), sem("exp_done"), sem("probs_turned")
        probT_ready, pv_done, heads_ready = sem("probT_ready"), sem("pv_done"), sem("heads_ready")
        heads_turned, headsT_ready, out_done = sem("heads_turned"), sem("headsT_ready"), sem("out_done")
        block = ctx.enter_context(nc.Block())

        @block.sync
        def _(sp):
            sp.wait_ge(zeroed, 1)
            for n, name in enumerate(("A1_bq", "A1_bk")):
                for r in range(4):
                    sp.dma_start(bqk[r * PAD:r * PAD + HD, n, :], a[name][r]).then_inc(w_loaded, 16)
            sp.dma_start(wqk[:, :, :, :], a["A1_wqk"]).then_inc(w_loaded, 16)
            sp.dma_start(ctxT[:, :, :], a["A1_ctxT"]).then_inc(w_loaded, 16)
            sp.dma_start(wv[:, :, :], a["A1_wv"]).then_inc(w_loaded, 16)
            sp.dma_start(wo[:, :, :], a["A1_wo"]).then_inc(w_loaded, 16)
            sp.dma_start(bv[:, :], a["A1_bv"]).then_inc(w_loaded, 16)
            sp.dma_start(bo[:, :], a["A1_bo"]).then_inc(w_loaded, 16)
        LOADS = 14 * 16

        @block.gpsimd
        def _(pool):
            nc.gpsimd.memset(bqk[:, :, :], 0.0).then_inc(zeroed, 1)
            nc.gpsimd.memset(padded[:, :, :, :, :], 0.0).then_inc(zeroed, 1)
            nc.gpsimd.memset(causal[:, :, :], 0.0).then_inc(zeroed, 1)
            pool.wait_ge(zeroed, 3)
            nc.gpsimd.affine_select(out=causal[:, :, :], in_=causal[:, :, :], compare_op=ALU.is_ge,
                                    fill=-BIG, base=0, pattern=[[0, 4], [-1, T]],
                                    channel_multiplier=1).then_inc(masked, 1)

        @block.vector
        def _(dve):
            link = Link(dve, dve_order)
            layer_norm_rows(core, link, 1, dve, core.x, core.xn, var_ready, std_ready, seen=True)
            take_features(core, dve, turned, xT_ready)
            dve.wait_ge(w_loaded, LOADS)
            dve.wait_ge(zeroed, 3)
            for n in range(2):
                for c in range(DC):
                    nc.vector.tensor_copy(padded[:, n, c, :, 0:HD],
                                          wqk[:, n, c, :].rearrange("p (h d) -> p h d", d=HD)
                                          ).then_inc(padded_ready, 1)
            dve.wait_ge(masked, 1)
            nc.vector.tensor_copy(rowsT[:, :, :], ctxT[:, :, 0:T]).then_inc(rows_ready, 1)

            def take_values(b, last_batch):
                dve.wait_ge(proj_done, b * 3 + 3)
                nc.vector.tensor_tensor(v[:, :], core.bank[6][0:T, 0:D], bv[:, :], ALU.add).then_inc(v_ready, 1)
                if not last_batch:
                    nc.vector.tensor_copy(rowsT[:, :, :],
                                          ctxT[:, :, bass.ds((b + 1) * T, T)]).then_inc(rows_ready, 1)

            def take_product(b):
                dve.wait_ge(out_done, b + 1)
                link(nc.vector.tensor_tensor(core.x[:, b, :], core.x[:, b, :], core.bank[7][0:T, D:2 * D],
                                             ALU.add))
                link(nc.vector.tensor_tensor(core.x[:, b, :], core.x[:, b, :], bo[:, :], ALU.add))
                nc.vector.memset(core.carrier[:, :], 0.0)
                nc.vector.bn_stats(core.stats[:, b, :], core.x[:, b, :])

            def batch(b, first, last_batch):
                for j in range(J):
                    dve.wait_ge(scores_done, b * J + j + 1)
                    link(nc.vector.scalar_tensor_tensor(
                        out=score[:, j, :, :], in0=core.bank[j][0:T, 0:4 * T].rearrange("p (r t) -> p r t", t=T),
                        scalar=HD ** -0.5, in1=causal[:, :, :], op0=ALU.mult, op1=ALU.add))
                    nc.vector.tensor_reduce(npeak[:, 4 * j:4 * j + 4], score[:, j, :, :], AX.X, ALU.max,
                                            negate=True).then_inc(peak_ready, 1)
                if not first:
                    take_product(b - 1)
                for j in range(J):
                    dve.wait_ge(probs_turned, b * J + j + 1)
                    nc.vector.tensor_copy(probT[:, j, :, :],
                                          core.bank[j][0:T, 0:4 * T].rearrange("p (r t) -> p r t", t=T)
                                          ).then_inc(probT_ready, 1)
                dve.wait_ge(exp_done, b * H + H)
                link(nc.vector.reciprocal(rtotal[:, :], total[:, :]))
                dve.wait_ge(pv_done, b + 1)
                nc.vector.tensor_tensor(
                    heads[:, :].rearrange("p (h d) -> p h d", d=HD),
                    core.bank[7][0:T, 0:D].rearrange("p (h d) -> p h d", d=HD),
                    rtotal[:, :].unsqueeze(2).broadcast_to([T, H, HD]), ALU.mult).then_inc(heads_ready, 1)

            per_batch = J + 3
            take_values(0, False)
            batch(0, True, False)
            take_values(1, False)
            start = link.count
            with dve.Fori(1, B - 2) as b:
                link.base = (b - 1) * per_batch
                batch(b, False, False)
                take_values(b + 1, False)
                assert link.count == start + per_batch
            link.base, link.count = None, start + (B - 3) * per_batch
            batch(B - 2, False, False)
            take_values(B - 1, True)
            batch(B - 1, False, True)
            take_product(B - 1)

        @block.scalar
        def _(act):
            root_step(core, act, 1, var_ready, std_ready)
            act.wait_ge(w_loaded, LOADS)

            def queries_keys(b, first):
                if not first:
                    act.wait_ge(scores_done, b * J)
                for n, dst in enumerate((qT, kT)):
                    act.wait_ge(proj_done, b * 3 + n + 1)
                    for j in range(J):
                        ins = nc.scalar.activation(dst[:, j, :], core.bank[4 + n][:, j * T:(j + 1) * T],
                                                   ACT.Identity, bias=bqk[:, n, j:j + 1])
                    ins.then_inc(qk_ready, 1)

            def turned_heads(b):
                act.wait_ge(heads_turned, b + 1)
                nc.scalar.activation(headsT[:, :, :],
                                     core.bank[6][:, D:D + DC * T].rearrange("p (c t) -> p c t", t=T),
                                     ACT.Copy).then_inc(headsT_ready, 1)

            def batch(b, first):
                if not first:
                    turned_heads(b - 1)
                for j in range(J):
                    act.wait_ge(peak_ready, b * J + j + 1)
                    for r in range(4):
                        h = 4 * r + j
                        nc.scalar.activation(prob[:, j, r, :], score[:, j, r, :], ACT.Exp,
                                             bias=npeak[:, 4 * j + r:4 * j + r + 1],
                                             accum_out=total[:, h:h + 1]).then_inc(exp_done, 1)

            queries_keys(0, True)
            batch(0, True)
            queries_keys(1, False)
            with act.Fori(1, B - 1) as b:
                batch(b, False)
                queries_keys(b + 1, False)
            batch(B - 1, False)
            turned_heads(B - 1)

        @block.tensor
        def _(pe):
            norm_to_features(core, pe, dve_order, turned, seen=True)
            pe.wait_ge(xT_ready, 4)
            pe.wait_ge(padded_ready, 2 * DC)

            def queries_keys(b):
                for n, src in enumerate((core.xnT, ctxT)):
                    for j in range(J):
                        for c in range(DC):
                            ins = pe.matmul(core.bank[4 + n][:, j * T:(j + 1) * T],
                                            padded[:, n, c, 4 * j:4 * j + 4, :].rearrange("p h d -> p (h d)"),
                                            src[:, c, bass.ds(b * T, T)], start=(c == 0), stop=(c == DC - 1))
                    ins.then_inc(proj_done, 1)

            def new_values(b):
                pe.wait_ge(rows_ready, b + 1)
                for c in range(DC):
                    ins = pe.matmul(core.bank[6][0:T, 0:D], rowsT[:, c, :], wv[:, c, :],
                                    start=(c == 0), stop=(c == DC - 1))
                ins.then_inc(proj_done, 1)

            def turn_heads(b):
                pe.wait_ge(heads_ready, b + 1)
                for c in range(DC):
                    ins = pe.transpose(core.bank[6][:, D + c * T:D + (c + 1) * T], heads[:, c * P:(c + 1) * P],
                                       core.ident[0:T, 0:T])
                ins.then_inc(heads_turned, 1)

            def product(b):
                pe.wait_ge(headsT_ready, b + 1)
                for c in range(DC):
                    ins = pe.matmul(core.bank[7][0:T, D:2 * D], headsT[:, c, :], wo[:, c, :],
                                    start=(c == 0), stop=(c == DC - 1))
                ins.then_inc(out_done, 1)

            def batch(b, first, last_batch):
                pe.wait_ge(qk_ready, b * 2 + 2)
                if not first:
                    pe.wait_ge(probT_ready, b * J)
                for j in range(J):
                    for r in range(4):
                        g = slice(r * PAD, (r + 1) * PAD)
                        ins = pe.matmul(core.bank[r][0:T, j * T:(j + 1) * T], qT[g, j, :], kT[g, j, :],
                                        start=True, stop=True)
                        if j == J - 1:
                            ins.then_inc(scores_done, 1)
                pe.wait_ge(v_ready, b + 1)
                if not first:
                    turn_heads(b - 1)
                if not last_batch:
                    queries_keys(b + 1)
                if not first:
                    product(b - 1)
                if not last_batch:
                    new_values(b + 1)

                def values(j):
                    pe.wait_ge(probT_ready, b * J + j + 1)
                    for r in range(4):
                        h = 4 * r + j
                        ins = pe.matmul(core.bank[7][0:T, h * HD:(h + 1) * HD], probT[:, j, r, :],
                                        v[:, h * HD:(h + 1) * HD], start=True, stop=True)
                    return ins

                for j in range(J):
                    pe.wait_ge(exp_done, b * H + 4 * j + 4)
                    for r in range(4):
                        ins = pe.transpose(core.bank[j][0:T, r * T:(r + 1) * T], prob[:, j, r, :],
                                           core.ident[0:T, 0:T])
                    ins.then_inc(probs_turned, 1)
                    if j >= 1:
                        values(j - 1)
                values(J - 1).then_inc(pv_done, 1)

            queries_keys(0)
            new_values(0)
            batch(0, True, False)
            with pe.Fori(1, B - 1) as b:
                batch(b, False, False)
            batch(B - 1, False, True)
            turn_heads(B - 1)
            product(B - 1)


F1_I, F1_BLOCK = 768, 32


class BlockWeights:
    W_MAX, TINY = 7.0, 1e-12

    def __init__(self, nc, core, ctx):
        self.nc, self.size = nc, F1_I * D // P
        self.blocks = self.size // F1_BLOCK
        self.w = ctx.enter_context(nc.sbuf_tensor("F1_w", [P, 3, self.size], F32))
        self.scale = ctx.enter_context(nc.sbuf_tensor("F1_w_scale", [P, 3, self.blocks], F32))
        self.rscale = ctx.enter_context(nc.sbuf_tensor("F1_w_rscale", [P, 3, self.blocks], F32))
        self.loaded, self.ready = core.sem("F1_w_loaded"), core.sem("F1_w_ready")

    def load(self, sp, a):
        sp.dma_start(self.w[:, :, :], a["F1_w"]).then_inc(self.loaded, 16)

    def quantize(self, dve, link, m):
        v = self.nc.vector
        dve.wait_ge(self.loaded, 16)
        w = self.w[:, m, :]
        blocks = w.rearrange("p (n k) -> p n k", k=F1_BLOCK)
        over = lambda t: t.unsqueeze(2).broadcast_to([P, self.blocks, F1_BLOCK])
        scale, rscale = self.scale[:, m, :], self.rscale[:, m, :]
        link(v.tensor_reduce(scale, blocks, AX.X, ALU.max, apply_absolute_value=True))
        link(v.tensor_scalar(scale, scale, 1.0 / self.W_MAX, self.TINY, ALU.mult, ALU.max))
        link(v.reciprocal(rscale, scale))
        link(v.tensor_tensor(blocks, blocks, over(rscale), ALU.mult))
        link(v.tensor_scalar(w, w, ROUND, -ROUND, ALU.add, ALU.add))
        link(v.tensor_scalar(w, w, -self.W_MAX - 1.0, self.W_MAX, ALU.max, ALU.min))
        v.tensor_tensor(blocks, blocks, over(scale), ALU.mult).then_inc(self.ready, 1)


def quantized_ffn(nc, core, a, weights):
    I, L = F1_I, "F1"
    IC = I // P
    A_MAX, TINY = 32767.0, 1e-12
    w = weights.w
    with ExitStack() as ctx:
        sb = lambda n, s, dt=F32: ctx.enter_context(nc.sbuf_tensor(f"{L}_{n}", s, dt))
        sem = lambda n: core.sem(f"{L}_{n}")
        gate_upT = sb("gate_upT", [P, 2, DC, I])
        downT = sb("downT", [P, IC, D])
        gate_up = sb("gate_up", [P, 2, IC, N])
        sig = sb("sig", [P, IC, N])
        local = sb("local", [P, 2, 2 * IC])
        amax, most = sb("amax", [P, 5]), sb("most", [P, 5])
        scale, rscale = sb("scale", [P, 5]), sb("rscale", [P, 5])
        dve_order = sem("dve_order")
        var_ready, std_ready, turned, xT_ready = sem("var_ready"), sem("std_ready"), sem("turned"), sem("xT_ready")
        w_turned, wT_ready = sem("w_turned"), sem("wT_ready")
        cleared, amax_ready, most_ready = sem("cleared"), sem("amax_ready"), sem("most_ready")
        xq_ready, gu_done, gu_taken, gu_seen = sem("xq_ready"), sem("gu_done"), sem("gu_taken"), sem("gu_seen")
        gate_ready, sig_ready, o_ready = sem("gate_ready"), sem("sig_ready"), sem("o_ready")
        down_done, x_added = sem("down_done"), sem("x_added")
        NG = 2 * IC
        block = ctx.enter_context(nc.Block())

        @block.gpsimd
        def _(pool):
            nc.gpsimd.memset(amax[:, :], 0.0).then_inc(cleared, 1)
            for n in range(5):
                pool.wait_ge(amax_ready, n + 1)
                nc.gpsimd.partition_all_reduce(most[:, n:n + 1], amax[:, n:n + 1], P,
                                               bass.bass_isa.ReduceOp.max).then_inc(most_ready, 1)

        @block.vector
        def _(dve):
            link = Link(dve, dve_order)
            layer_norm_rows(core, link, 1, dve, core.x, core.xn, var_ready, std_ready, seen=True)

            def scales(n):
                dve.wait_ge(most_ready, n + 1)
                link(nc.vector.tensor_scalar(scale[:, n:n + 1], most[:, n:n + 1], 1.0 / A_MAX, TINY,
                                             ALU.mult, ALU.max))
                link(nc.vector.reciprocal(rscale[:, n:n + 1], scale[:, n:n + 1]))

            def quantize(t, n, rows=P):
                link(nc.vector.tensor_scalar(t, t, rscale[0:rows, n:n + 1], ROUND, ALU.mult, ALU.add))
                return nc.vector.tensor_scalar(t, t, -ROUND, scale[0:rows, n:n + 1], ALU.add, ALU.mult)

            def see(n):
                dve.wait_ge(gu_done, n + 1)
                nc.vector.tensor_reduce(local[:, n // NG, n % NG:n % NG + 1], core.bank[n % 4][:, 0:HALF],
                                        AX.X, ALU.max, apply_absolute_value=True).then_inc(gu_seen, 1)

            dve.wait_ge(cleared, 1)
            nc.vector.tensor_reduce(amax[0:T, 0:1], core.xn[:, :, :], AX.XY, ALU.max,
                                    apply_absolute_value=True).then_inc(amax_ready, 1)
            scales(0)
            quantize(core.xn[:, :, :], 0, T).then_inc(xq_ready, 1)
            take_features(core, dve, turned, xT_ready)
            for n in range(NG):
                see(n)
            dve.wait_ge(gu_seen, NG)
            nc.vector.tensor_reduce(amax[:, 1:2], local[:, 0, :], AX.X, ALU.max).then_inc(amax_ready, 1)
            for n in range(NG, 2 * NG):
                see(n)
                k = n - NG
                if k == 1:
                    scales(1)
                    dve.wait_ge(gu_taken, NG)
                if k in (3, 6, 9):
                    third = gate_up[:, 0, (k // 3 - 1) * IC // 3:k // 3 * IC // 3]
                    quantize(third, 1).then_inc(gate_ready, 1)
            dve.wait_ge(gu_seen, 2 * NG)
            nc.vector.tensor_reduce(amax[:, 2:3], local[:, 1, :], AX.X, ALU.max).then_inc(amax_ready, 1)
            dve.wait_ge(sig_ready, 3)
            link(nc.vector.tensor_scalar(sig[:, :, :], sig[:, :, :], 65536.0, ROUND, ALU.mult, ALU.add))
            link(nc.vector.tensor_scalar(sig[:, :, :], sig[:, :, :], -ROUND, 65535.0, ALU.add, ALU.min))
            g = gate_up[:, 0]

            def maximum(n):
                nc.vector.tensor_reduce(amax[:, n:n + 1], g, AX.XY, ALU.max, apply_absolute_value=True
                                        ).then_inc(amax_ready, 1)

            link(nc.vector.scalar_tensor_tensor(out=g, in0=sig[:, :, :], scalar=1.0 / 65536.0, in1=g,
                                                op0=ALU.mult, op1=ALU.mult))
            maximum(3)
            scales(2)
            dve.wait_ge(gu_taken, 2 * NG)
            link(quantize(gate_up[:, 1], 2))
            scales(3)
            link(quantize(g, 3))
            link(nc.vector.tensor_tensor(g, g, gate_up[:, 1], ALU.mult))
            maximum(4)
            scales(4)
            for half in range(2):
                quantize(g[:, :, half * HALF:(half + 1) * HALF], 4).then_inc(o_ready, 1)
            for b in range(B):
                dve.wait_ge(down_done, b + 1)
                nc.vector.tensor_tensor(core.x[:, b, :], core.x[:, b, :], core.bank[4 + b % 4][0:T, 0:D],
                                        ALU.add).then_inc(x_added, 1)
                dve.wait_ge(x_added, b + 1)
                nc.vector.bn_stats(core.stats[:, b, :], core.x[:, b, :])

        @block.scalar
        def _(act):
            root_step(core, act, 1, var_ready, std_ready)
            for g in range(9):
                act.wait_ge(w_turned, g + 1)
                if g < 6:
                    dst = gate_upT[:, g // 3, :, (g % 3) * 2 * P:(g % 3 + 1) * 2 * P]
                    src = core.bank[4 + g % 4][:, :].rearrange("p (c i) -> p c i", c=DC)
                else:
                    dst = downT[:, 2 * (g - 6):2 * (g - 6) + 2, :]
                    src = core.bank[4 + g % 4][:, :].rearrange("p (i d) -> p i d", i=2)
                nc.scalar.activation(dst, src, ACT.Copy).then_inc(wT_ready, 1)
            for n in range(2 * 2 * IC):
                act.wait_ge(gu_seen, n + 1)
                m, half = n % (2 * IC) // 2, n % 2
                nc.scalar.activation(gate_up[:, n // (2 * IC), m, half * HALF:(half + 1) * HALF],
                                     core.bank[n % 4][:, 0:HALF], ACT.Copy).then_inc(gu_taken, 1)
                if n - NG in (5, 8, 11):
                    k = (n - NG - 5) // 3
                    third = slice(k * IC // 3, (k + 1) * IC // 3)
                    act.wait_ge(gate_ready, k + 1)
                    nc.scalar.activation(sig[:, third, :], gate_up[:, 0, third], ACT.Sigmoid
                                         ).then_inc(sig_ready, 1)

        @block.tensor
        def _(pe):
            pe.wait_ge(weights.ready, 3)
            for g in range(9):
                if g >= 4:
                    pe.wait_ge(wT_ready, g - 3)
                for q in range(4):
                    if g < 6:
                        c, i = q // 2, (g % 3) * 2 + q % 2
                        piece = w[:, g // 3, i * D + c * P:i * D + (c + 1) * P]
                    else:
                        c, i = q % 2, (g - 6) * 2 + q // 2
                        piece = w[:, 2, c * I + i * P:c * I + (i + 1) * P]
                    ins = pe.transpose(core.bank[4 + g % 4][:, q * P:(q + 1) * P], piece, core.ident[:, :])
                ins.then_inc(w_turned, 1)
            pe.wait_ge(xq_ready, 1)
            transpose_rows(core, pe, core.xn, [0, 1, 2, 3], turned)
            pe.wait_ge(xT_ready, 4)
            pe.wait_ge(wT_ready, 9)
            for n in range(2 * 2 * IC):
                m, half = n % (2 * IC) // 2, n % 2
                if n >= 4:
                    pe.wait_ge(gu_taken, n - 3)
                for c in range(DC):
                    ins = pe.matmul(core.bank[n % 4][:, 0:HALF], gate_upT[:, n // (2 * IC), c, m * P:(m + 1) * P],
                                    core.xnT[:, c, half * HALF:(half + 1) * HALF],
                                    start=(c == 0), stop=(c == DC - 1))
                ins.then_inc(gu_done, 1)
            for b in range(B):
                pe.wait_ge(o_ready, b // HB + 1)
                if b >= 4:
                    pe.wait_ge(x_added, b - 3)
                for m in range(IC):
                    ins = pe.matmul(core.bank[4 + b % 4][0:T, 0:D], gate_up[:, 0, m, b * T:(b + 1) * T],
                                    downT[:, m, :], start=(m == 0), stop=(m == IC - 1))
                ins.then_inc(down_done, 1)


def slot_attention(nc, core, a):
    ITERS, EPS, L = 3, RMS_EPS, "A3"
    NT = B * SC
    VW = D + 1
    G3 = 3 * D
    with ExitStack() as ctx:
        sb = lambda n, s, dt=F32: ctx.enter_context(nc.sbuf_tensor(f"{L}_{n}", s, dt))
        sem = lambda n: core.sem(f"{L}_{n}")
        wqkv = sb("wqkv", [P, 3, DC, D])
        wih, whh = sb("wih", [P, DC, G3]), sb("whh", [P, DC, G3])
        norms = sb("norms", [P, 2, DC])
        bih, bhh = sb("bih", [T, G3]), sb("bhh", [T, G3])
        rows = sb("rows", [SP_, NT, D])
        rowsT = sb("rowsT", [P, 2, DC, S])
        kT = sb("kT", [P, DC, B * S])
        v = sb("v", [SP_, NT, VW])
        slots = core.xn
        slot_rs = sb("slot_rs", [T, B])
        sn = sb("sn", [T, B, D])
        snT, slotsT, qT = core.xnT, sb("slotsT", [P, DC, N]), sb("qT", [P, DC, N])
        npeak, total = sb("npeak", [SP_, SC]), sb("total", [SP_, SC])
        attn = sb("attn", [SP_, 2, SC, T])
        rsum = sb("rsum", [T, 1])
        upd, updT = sb("upd", [T, 2, D]), sb("updT", [P, 2, DC, T])
        rz, nn = sb("rz", [T, 2 * D]), sb("nn", [T, D])
        nh, diff = sb("nh", [T, D]), sb("diff", [T, D])
        LOADS = 4
        w_loaded, kv_loaded = sem("w_loaded"), sem("kv_loaded")
        rows_loaded = [sem(f"rows_loaded{i}") for i in range(LOADS)]
        dve_order, act_order = sem("dve_order"), sem("act_order")
        var_ready, std_ready = sem("var_ready"), sem("std_ready")
        ms_ready, root_ready = sem("ms_ready"), sem("root_ready")
        rows_ready, rows_turned, rowsT_ready = sem("rows_ready"), sem("rows_turned"), sem("rowsT_ready")
        kv_done, k_taken, v_taken = sem("kv_done"), sem("k_taken"), sem("v_taken")
        slots_ready, slots_turned, slotsT_ready = sem("slots_ready"), sem("slots_turned"), sem("slotsT_ready")
        sn_ready, sn_turned, snT_ready = sem("sn_ready"), sem("sn_turned"), sem("snT_ready")
        q_done, q_ready = sem("q_done"), sem("q_ready")
        scores_done, shifted, exp_done, attn_ready = sem("scores_done"), sem("shifted"), sem("exp_done"), sem("attn_ready")
        upd_done, upd_ready, upd_turned, updT_ready = sem("upd_done"), sem("upd_ready"), sem("upd_turned"), sem("updT_ready")
        gates_done, rz_ready, rz_tanh = sem("gates_done"), sem("rz_ready"), sem("rz_tanh")
        n_ready, n_tanh, slot_new = sem("n_ready"), sem("n_tanh"), sem("slot_new")
        stats_ready = sem("stats_ready")

        def gate_banks(b):
            return (core.bank[0], core.bank[1]) if b == B - 2 else (core.bank[6], core.bank[7])

        block = ctx.enter_context(nc.Block())

        @block.sync
        def _(sp):
            for i in range(LOADS):
                part = slice(i * NT // LOADS, (i + 1) * NT // LOADS)
                sp.dma_start(rows[:, part, :], a["ctx_rows"][:, part, :]).then_inc(rows_loaded[i], 16)
                if i == 0:
                    sp.dma_start(norms[:, :, :], a["A3_norms"]).then_inc(kv_loaded, 16)
                    sp.dma_start(wqkv[:, :, :, :], a["A3_wqkv"]).then_inc(kv_loaded, 16)
            for dst, name in ((wih, "A3_wih"), (whh, "A3_whh")):
                sp.dma_start(dst[:, :, :], a[name]).then_inc(w_loaded, 16)
            for dst, name in ((bih, "A3_bih"), (bhh, "A3_bhh")):
                sp.dma_start(dst[:, :], a[name]).then_inc(w_loaded, 16)

        @block.vector
        def _(dve):
            link = Link(dve, dve_order)
            layer_norm_rows(core, link, 1, dve, core.x, core.xn, var_ready, std_ready, seen=True)
            nc.vector.memset(v[:, :, D:VW], 1.0).then_inc(v_taken, 1)
            nc.vector.engine_nop().then_inc(slot_new, B)
            dve.wait_ge(kv_loaded, 32)

            def scale_rows(b):
                dve.wait_ge(rows_loaded[b * LOADS // B], 16)
                for t in range(b * SC, (b + 1) * SC):
                    ins = nc.vector.tensor_scalar(rows[:, t, :], rows[:, t, :], core.ctx_rrms[:, t:t + 1], None,
                                                  ALU.mult)
                ins.then_inc(rows_ready, 1)

            def take_rows(b):
                for c in range(DC):
                    dve.wait_ge(rows_turned, b * DC + c + 1)
                    if b >= 2:
                        dve.wait_ge(kv_done, (b - 1) * (DC + SC))
                    nc.vector.tensor_scalar(rowsT[:, b % 2, c, :], core.bank[c][:, 0:S], norms[:, 1, c:c + 1],
                                            None, ALU.mult).then_inc(rowsT_ready, 1)

            scale_rows(0)
            scale_rows(1)
            take_rows(0)
            for b in range(B):
                if b + 2 < B:
                    scale_rows(b + 2)
                if b + 1 < B:
                    take_rows(b + 1)
                for k in range(SC):
                    dve.wait_ge(kv_done, b * (DC + SC) + DC + k + 1)
                    nc.vector.tensor_copy(v[:, b * SC + k, 0:D],
                                          core.bank[4 + k][0:SP_, 0:D]).then_inc(v_taken, 1)
            dve.wait_ge(w_loaded, 64)
            link(nc.vector.tensor_tensor(bih[:, 0:2 * D], bih[:, 0:2 * D], bhh[:, 0:2 * D], ALU.add))

            def softmax(it, b):
                dve.wait_ge(scores_done, it * B + b + 1)
                src = core.bank[b % 2][0:SP_, 0:SC * T].rearrange("p (k t) -> p k t", t=T)
                over = lambda t: t.unsqueeze(2).broadcast_to([SP_, SC, T])
                link(nc.vector.tensor_reduce(npeak[:, :], src, AX.X, ALU.max, negate=True))
                if b >= 2:
                    dve.wait_ge(upd_done, it * B + b - 1)
                nc.vector.tensor_tensor(attn[:, b % 2, :, :], src, over(npeak[:, :]), ALU.add
                                        ).then_inc(shifted, 1)
                dve.wait_ge(exp_done, it * B + b + 1)
                link(nc.vector.tensor_reduce(total[:, :], attn[:, b % 2, :, :], AX.X, ALU.add))
                link(nc.vector.reciprocal(total[:, :], total[:, :]))
                nc.vector.tensor_tensor(attn[:, b % 2, :, :], attn[:, b % 2, :, :], over(total[:, :]), ALU.mult
                                        ).then_inc(attn_ready, 1)

            def means(it, b):
                dve.wait_ge(upd_done, it * B + b + 1)
                src = core.bank[2 + b % 2]
                link(nc.vector.tensor_scalar(rsum[:, :], src[0:T, D:VW], EPS, None, ALU.add))
                link(nc.vector.reciprocal(rsum[:, :], rsum[:, :]))
                nc.vector.tensor_scalar(upd[:, b % 2, :], src[0:T, 0:D], rsum[:, 0:1], None, ALU.mult
                                        ).then_inc(upd_ready, 1)

            def gates(it, b):
                dve.wait_ge(gates_done, it * B + b + 1)
                dve.wait_ge(slot_new, it * B + b + B)
                both, new = gate_banks(b)
                nc.vector.tensor_tensor(rz[:, :], both[0:T, :], bih[:, 0:2 * D], ALU.add
                                        ).then_inc(rz_ready, 1)
                link(nc.vector.tensor_tensor(nn[:, :], new[0:T, 0:D], bih[:, 2 * D:G3], ALU.add))
                link(nc.vector.tensor_tensor(nh[:, :], new[0:T, D:2 * D], bhh[:, 2 * D:G3], ALU.add))
                dve.wait_ge(rz_tanh, it * B + b + 1)
                link(nc.vector.tensor_scalar(rz[:, :], rz[:, :], 0.5, 0.5, ALU.mult, ALU.add))
                link(nc.vector.tensor_tensor(nh[:, :], nh[:, :], rz[:, 0:D], ALU.mult))
                nc.vector.tensor_tensor(nn[:, :], nn[:, :], nh[:, :], ALU.add).then_inc(n_ready, 1)
                dve.wait_ge(n_tanh, it * B + b + 1)
                link(nc.vector.tensor_tensor(diff[:, :], slots[:, b, :], nn[:, :], ALU.subtract))
                link(nc.vector.tensor_tensor(diff[:, :], diff[:, :], rz[:, D:2 * D], ALU.mult))
                nc.vector.tensor_tensor(slots[:, b, :], diff[:, :], nn[:, :], ALU.add).then_inc(slot_new, 1)
                dve.wait_ge(slot_new, it * B + b + 1 + B)
                nc.vector.bn_stats(core.stats[:, b, :], slots[:, b, :]).then_inc(stats_ready, 1)

            for b in range(B):
                nc.vector.bn_stats(core.stats[:, b, :], slots[:, b, :]).then_inc(stats_ready, 1)
            per_iter = 4 + B * (3 + 2 + 6)
            start = link.count
            with dve.Fori(0, ITERS) as it:
                link.base = it * per_iter
                dve.wait_ge(stats_ready, it * B + B)
                nc.vector.memset(slot_rs[:, :], 0.0)
                for b in range(B):
                    last = nc.vector.bn_aggr(core.moments[:, b, :], core.stats[:, b, :])
                link(last)
                link(nc.vector.tensor_tensor(slot_rs[:, :], core.moments[:, :, 0], core.moments[:, :, 0], ALU.mult))
                link(nc.vector.tensor_tensor(slot_rs[:, :], slot_rs[:, :], core.moments[:, :, 1], ALU.add))
                nc.vector.tensor_scalar(slot_rs[:, :], slot_rs[:, :], EPS, None, ALU.add).then_inc(ms_ready, 1)
                dve.wait_ge(root_ready, it + 1)
                link(nc.vector.reciprocal(slot_rs[:, :], slot_rs[:, :]))
                for b in range(B):
                    nc.vector.tensor_scalar(sn[:, b, :], slots[:, b, :], slot_rs[:, b:b + 1], None, ALU.mult
                                            ).then_inc(sn_ready, 1)
                for half in range(2):
                    for c in range(DC):
                        dve.wait_ge(sn_turned, it * 4 + 2 * half + c + 1)
                        nc.vector.tensor_scalar(snT[:, c, half * HALF:(half + 1) * HALF],
                                                core.bank[2 * half + c][:, 0:HALF], norms[:, 0, c:c + 1], None,
                                                ALU.mult).then_inc(snT_ready, 1)
                for half in range(2):
                    for m in range(DC):
                        dve.wait_ge(q_done, it * 4 + 2 * half + m + 1)
                        nc.vector.tensor_scalar(qT[:, m, half * HALF:(half + 1) * HALF],
                                                core.bank[2 * half + m][:, 0:HALF], D ** -0.5, None,
                                                ALU.mult).then_inc(q_ready, 1)
                for s in range(B + 3):
                    if s < B:
                        softmax(it, s)
                    if 1 <= s <= B:
                        means(it, s - 1)
                    if s >= 3:
                        gates(it, s - 3)
                assert link.count == start + per_iter
            dve.wait_ge(slot_new, (ITERS + 1) * B)
            nc.vector.tensor_tensor(core.x[:, :, :], core.x[:, :, :], slots[:, :, :], ALU.add)

        @block.scalar
        def _(act):
            link = Link(act, act_order)
            root_step(core, act, 1, var_ready, std_ready)
            for b in range(B):
                for m in range(DC):
                    act.wait_ge(kv_done, b * (DC + SC) + m + 1)
                    nc.scalar.activation(kT[:, m, b * S:(b + 1) * S], core.bank[2 + m][:, 0:S],
                                         ACT.Copy).then_inc(k_taken, 1)
            with act.Fori(0, ITERS) as it:
                act.wait_ge(ms_ready, it + 1)
                nc.scalar.activation(slot_rs[:, :], slot_rs[:, :], ACT.Sqrt).then_inc(root_ready, 1)
                for g in range(4):
                    act.wait_ge(slots_turned, it * 4 + g + 1)
                    c, half = g // 2, g % 2
                    nc.scalar.activation(slotsT[:, c, half * HALF:(half + 1) * HALF],
                                         core.bank[4 + g][:, 0:HALF], ACT.Copy).then_inc(slotsT_ready, 1)
                for s in range(B + 3):
                    if s < B:
                        act.wait_ge(shifted, it * B + s + 1)
                        nc.scalar.activation(attn[:, s % 2, :, :], attn[:, s % 2, :, :], ACT.Exp
                                             ).then_inc(exp_done, 1)
                    if 2 <= s < B + 2:
                        b = s - 2
                        act.wait_ge(upd_turned, it * B + b + 1)
                        nc.scalar.activation(updT[:, b % 2, :, :],
                                             core.bank[4 + b % 2][:, 0:DC * T].rearrange("p (c t) -> p c t", t=T),
                                             ACT.Copy).then_inc(updT_ready, 1)
                    if s >= 3:
                        b = s - 3
                        act.wait_ge(rz_ready, it * B + b + 1)
                        nc.scalar.activation(rz[:, :], rz[:, :], ACT.Tanh, scale=0.5).then_inc(rz_tanh, 1)
                        act.wait_ge(n_ready, it * B + b + 1)
                        nc.scalar.activation(nn[:, :], nn[:, :], ACT.Tanh).then_inc(n_tanh, 1)

        @block.tensor
        def _(pe):
            def turn_rows(b):
                pe.wait_ge(rows_ready, b + 1)
                for c in range(DC):
                    if b:
                        pe.wait_ge(rowsT_ready, (b - 1) * DC + c + 1)
                    for k in range(SC):
                        ins = pe.transpose(core.bank[c][:, k * SP_:(k + 1) * SP_],
                                           rows[:, b * SC + k, c * P:(c + 1) * P], core.ident[0:SP_, 0:SP_])
                    ins.then_inc(rows_turned, 1)

            turn_rows(0)
            pe.wait_ge(kv_loaded, 32)
            for b in range(B):
                if b + 1 < B:
                    turn_rows(b + 1)
                pe.wait_ge(rowsT_ready, b * DC + DC)
                for m in range(DC):
                    if b:
                        pe.wait_ge(k_taken, (b - 1) * DC + m + 1)
                    for c in range(DC):
                        ins = pe.matmul(core.bank[2 + m][:, 0:S], wqkv[:, 1, c, m * P:(m + 1) * P],
                                        rowsT[:, b % 2, c, :], start=(c == 0), stop=(c == DC - 1))
                    ins.then_inc(kv_done, 1)
                for k in range(SC):
                    if b:
                        pe.wait_ge(v_taken, 1 + (b - 1) * SC + k + 1)
                    for c in range(DC):
                        ins = pe.matmul(core.bank[4 + k][0:SP_, 0:D], rowsT[:, b % 2, c, k * SP_:(k + 1) * SP_],
                                        wqkv[:, 2, c, :], start=(c == 0), stop=(c == DC - 1))
                    ins.then_inc(kv_done, 1)
            pe.wait_ge(w_loaded, 64)
            pe.wait_ge(k_taken, B * DC)
            pe.wait_ge(v_taken, 1 + NT)

            with pe.Fori(0, ITERS) as it:
                for half in range(2):
                    pe.wait_ge(sn_ready, it * B + (half + 1) * HB)
                    for c in range(DC):
                        for q in range(HB):
                            ins = pe.transpose(core.bank[2 * half + c][:, q * T:(q + 1) * T],
                                               sn[:, half * HB + q, c * P:(c + 1) * P], core.ident[0:T, 0:T])
                        ins.then_inc(sn_turned, 1)
                transpose_rows(core, pe, slots, [4, 5, 6, 7], slots_turned)
                for half in range(2):
                    pe.wait_ge(snT_ready, it * 4 + 2 * half + 2)
                    for m in range(DC):
                        for c in range(DC):
                            ins = pe.matmul(core.bank[2 * half + m][:, 0:HALF], wqkv[:, 0, c, m * P:(m + 1) * P],
                                            snT[:, c, half * HALF:(half + 1) * HALF],
                                            start=(c == 0), stop=(c == DC - 1))
                        ins.then_inc(q_done, 1)
                pe.wait_ge(q_ready, it * 4 + 4)
                pe.wait_ge(slotsT_ready, it * 4 + 4)
                for s in range(B + 3):
                    if s < B:
                        if s >= 2:
                            pe.wait_ge(shifted, it * B + s - 1)
                        for k in range(SC):
                            t = s * SC + k
                            for c in range(DC):
                                ins = pe.matmul(core.bank[s % 2][0:SP_, k * T:(k + 1) * T],
                                                kT[:, c, t * SP_:(t + 1) * SP_], qT[:, c, s * T:(s + 1) * T],
                                                start=(c == 0), stop=(c == DC - 1))
                        ins.then_inc(scores_done, 1)
                    if 1 <= s <= B:
                        b = s - 1
                        pe.wait_ge(attn_ready, it * B + b + 1)
                        if b >= 2:
                            pe.wait_ge(upd_ready, it * B + b - 1)
                        for k in range(SC):
                            ins = pe.matmul(core.bank[2 + b % 2][0:T, 0:VW], attn[:, b % 2, k, :],
                                            v[:, b * SC + k, :], start=(k == 0), stop=(k == SC - 1))
                        ins.then_inc(upd_done, 1)
                    if 2 <= s < B + 2:
                        b = s - 2
                        pe.wait_ge(upd_ready, it * B + b + 1)
                        if b >= 2:
                            pe.wait_ge(updT_ready, it * B + b - 1)
                        for c in range(DC):
                            ins = pe.transpose(core.bank[4 + b % 2][:, c * T:(c + 1) * T],
                                               upd[:, b % 2, c * P:(c + 1) * P], core.ident[0:T, 0:T])
                        ins.then_inc(upd_turned, 1)
                    if s >= 3:
                        b = s - 3
                        pe.wait_ge(updT_ready, it * B + b + 1)
                        if b and b != B - 2:
                            pe.wait_ge(n_ready, it * B + (b - 1 if b == B - 1 else b))
                        both, new = gate_banks(b)
                        bt = slice(b * T, (b + 1) * T)
                        for c in range(DC):
                            pe.matmul(both[0:T, :], updT[:, b % 2, c, :], wih[:, c, 0:2 * D],
                                      start=(c == 0), stop=False)
                        for c in range(DC):
                            pe.matmul(both[0:T, :], slotsT[:, c, bt], whh[:, c, 0:2 * D],
                                      start=False, stop=(c == DC - 1))
                        for c in range(DC):
                            pe.matmul(new[0:T, 0:D], updT[:, b % 2, c, :], wih[:, c, 2 * D:G3],
                                      start=(c == 0), stop=(c == DC - 1))
                        for c in range(DC):
                            ins = pe.matmul(new[0:T, D:2 * D], slotsT[:, c, bt], whh[:, c, 2 * D:G3],
                                            start=(c == 0), stop=(c == DC - 1))
                        ins.then_inc(gates_done, 1)


def tile_ffn(nc, core, a):
    NT, C, G, K, CH, L = 64, 8, 16, 8, 64, "F3"
    W = C + NT
    TW = 2 * G + G + G + 1 + D
    with ExitStack() as ctx:
        sb = lambda n, s, dt=F32: ctx.enter_context(nc.sbuf_tensor(f"{L}_{n}", s, dt))
        sem = lambda n: core.sem(f"{L}_{n}")
        raw = sb("raw", [P, DC, NT])
        low, sig = sb("low", [P, DC, NT]), sb("sig", [P, DC, W])
        mean, neg = sb("mean", [P, DC, C]), sb("neg", [P, DC, C])
        knots, steps = sb("knots", [T, K]), sb("steps", [T, K - 1])
        temp, out_scale = sb("temp", [T, 1]), sb("out_scale", [T, 1])
        cw1, cb1 = sb("cw1", [P, DC, CH]), sb("cb1", [CH, 1])
        cw2, cb2 = sb("cw2", [CH, 2]), sb("cb2", [T, B, 2])
        table = sb("table", [NT, TW])
        gamma, beta = sb("gamma", [T, D]), sb("beta", [T, D])
        hT = sb("hT", [CH, N])
        comp = sb("comp", [T, B, 2])
        where, cell = sb("where", [T, B, W]), sb("cell", [T, B, C])
        base, slope, part = sb("base", [T, B, C]), sb("slope", [T, B, C]), sb("part", [T, B, C])
        places = sb("places", [T, B, C])
        peak = sb("peak", [T, B])
        cluster, local = sb("cluster", [T, B, C]), sb("local", [T, B, C])
        chosen = sb("chosen", [T, B, C])
        spread = sb("spread", [T, B, C, C])
        onehot, onehotT = sb("onehot", [T, B, NT]), sb("onehotT", [NT, N])
        prm = sb("prm", [T, B, TW])
        hidden, hidden2 = sb("hidden", [T, B, G]), sb("hidden2", [T, B, G])
        mag = sb("mag", [T, B])
        w_loaded, dve_order = sem("w_loaded"), sem("dve_order")
        var_ready, std_ready, turned, xT_ready = sem("var_ready"), sem("std_ready"), sem("turned"), sem("xT_ready")
        placed, sig_ready, scores_done, scaled = sem("placed"), sem("sig_ready"), sem("scores_done"), sem("scaled")
        exp_done, h_done, h_ready = sem("exp_done"), sem("h_done"), sem("h_ready")
        comp_done, comp_ready, comp_tanh = sem("comp_done"), sem("comp_ready"), sem("comp_tanh")
        onehot_ready, onehot_turned, onehotT_ready = sem("onehot_ready"), sem("onehot_turned"), sem("onehotT_ready")
        prm_done, prm_ready = sem("prm_done"), sem("prm_ready")
        block = ctx.enter_context(nc.Block())
        LOADS = [(raw[:, :, :], "F3_raw"), (knots[:, :], "F3_knots"), (temp[:, :], "F3_temp"),
                 (out_scale[:, :], "F3_out_scale"), (cw1[:, :, :], "F3_cw1"), (cb1[:, :], "F3_cb1"),
                 (cw2[:, :], "F3_cw2"), (cb2[:, :, :], "F3_cb2"), (table[:, :], "F3_table"),
                 (gamma[:, :], "F3_gamma"), (beta[:, :], "F3_beta")]

        @block.sync
        def _(sp):
            for dst, name in LOADS:
                sp.dma_start(dst, a[name]).then_inc(w_loaded, 16)

        @block.gpsimd
        def _(pool):
            count_down(nc, pool, places[:, :, :], C, placed)

        @block.vector
        def _(dve):
            link = Link(dve, dve_order)
            tt, ts = nc.vector.tensor_tensor, nc.vector.tensor_scalar
            layer_norm_rows(core, link, 1, dve, core.x, core.xn, var_ready, std_ready)
            take_features(core, dve, turned, xT_ready)
            dve.wait_ge(w_loaded, 16 * len(LOADS))
            q = sig[:, :, C:W]
            link(ts(q, raw[:, :, :], 0.3, None, ALU.is_gt))
            link(ts(low[:, :, :], raw[:, :, :], -0.3, None, ALU.is_lt))
            link(tt(q, q, low[:, :, :], ALU.subtract))
            link(tt(q, q, raw[:, :, :], ALU.subtract))
            link(tt(q, q, raw[:, :, :], ALU.add))
            link(nc.vector.tensor_reduce(mean[:, :, :], q.rearrange("p c (g t) -> p c g t", t=C), AX.X, ALU.add))
            link(ts(neg[:, :, :], mean[:, :, :], 0.0, None, ALU.is_lt))
            link(ts(mean[:, :, :], mean[:, :, :], 0.0, None, ALU.is_gt))
            tt(sig[:, :, 0:C], mean[:, :, :], neg[:, :, :], ALU.subtract).then_inc(sig_ready, 1)
            link(tt(steps[:, :], knots[:, 1:K], knots[:, 0:K - 1], ALU.subtract))
            link(ts(temp[:, :], temp[:, :], 1e-6, None, ALU.add))
            link(nc.vector.reciprocal(temp[:, :], temp[:, :]))
            link(tt(core.x[:, :, :], core.x[:, :, :], beta[:, :].unsqueeze(1).broadcast_to([T, B, D]), ALU.add))
            for half in range(2):
                dve.wait_ge(scores_done, half + 1)
                ts(where[:, half * HB:(half + 1) * HB, :],
                   core.bank[4 + half][0:T, 0:HB * W].rearrange("p (b w) -> p b w", w=W),
                   temp[:, 0:1], None, ALU.mult).then_inc(scaled, 1)
            def calibrate(w, turn):
                dve.wait_ge(exp_done, turn)
                link(ts(w, w, 1.0, None, ALU.add))
                link(nc.vector.reciprocal(w, w))
                link(ts(w, w, K - 1.0, None, ALU.mult))
                link(ts(cell[:, :, :], w, 1.0, None, ALU.is_ge))
                for k in range(2, K - 1):
                    link(nc.vector.scalar_tensor_tensor(out=cell[:, :, :], in0=w, scalar=float(k),
                                                        in1=cell[:, :, :], op0=ALU.is_ge, op1=ALU.add))
                link(tt(w, w, cell[:, :, :], ALU.subtract))
                for dst, values in ((base, knots), (slope, steps)):
                    link(ts(dst[:, :, :], cell[:, :, :], 0.0, values[:, 0:1], ALU.is_equal, ALU.mult))
                    for k in range(1, K - 1):
                        link(ts(part[:, :, :], cell[:, :, :], float(k), values[:, k:k + 1], ALU.is_equal,
                                ALU.mult))
                        link(tt(dst[:, :, :], dst[:, :, :], part[:, :, :], ALU.add))
                link(tt(w, w, slope[:, :, :], ALU.mult))
                link(tt(w, w, base[:, :, :], ALU.add))

            dve.wait_ge(placed, 1)

            def first_best(pick, value):
                over = peak[:, :].unsqueeze(2).broadcast_to([T, B, C])
                link(nc.vector.tensor_reduce(peak[:, :], value, AX.X, ALU.max))
                link(tt(pick, value, over, ALU.is_equal))
                link(tt(pick, pick, places[:, :, :], ALU.mult))
                link(nc.vector.tensor_reduce(peak[:, :], pick, AX.X, ALU.max))
                link(tt(pick, places[:, :, :], over, ALU.is_equal))

            calibrate(where[:, :, 0:C], 1)
            first_best(cluster[:, :, :], where[:, :, 0:C])
            for b in range(B):
                last = tt(spread[:, b, :, :], where[:, b, C:W].rearrange("p (c t) -> p t c", t=C),
                          cluster[:, b, :].unsqueeze(1).broadcast_to([T, C, C]), ALU.mult)
            link(last)
            nc.vector.tensor_reduce(chosen[:, :, :], spread[:, :, :, :], AX.X, ALU.add).then_inc(scaled, 1)
            calibrate(chosen[:, :, :], 2)
            first_best(local[:, :, :], chosen[:, :, :])
            for b in range(B):
                tt(onehot[:, b, :].rearrange("p (c t) -> p c t", t=C),
                   cluster[:, b, :].unsqueeze(2).broadcast_to([T, C, C]),
                   local[:, b, :].unsqueeze(1).broadcast_to([T, C, C]), ALU.mult).then_inc(onehot_ready, 1)
            for half in range(2):
                dve.wait_ge(onehot_turned, half + 1)
                nc.vector.tensor_copy(onehotT[:, half * HALF:(half + 1) * HALF],
                                      core.bank[2 + half][0:NT, 0:HALF]).then_inc(onehotT_ready, 1)
            dve.wait_ge(comp_done, 1)
            tt(comp[:, :, :], core.bank[6][0:T, 0:2 * B].rearrange("p (b i) -> p b i", i=2), cb2[:, :, :],
               ALU.add).then_inc(comp_ready, 1)
            dve.wait_ge(comp_tanh, 1)
            dve.wait_ge(prm_ready, B)
            wide = lambda t: t.broadcast_to([T, B, G])
            h, h2 = hidden[:, :, :], hidden2[:, :, :]
            link(tt(h, prm[:, :, 0:G], wide(comp[:, :, 0:1]), ALU.mult))
            link(tt(h2, prm[:, :, G:2 * G], wide(comp[:, :, 1:2]), ALU.mult))
            link(tt(h, h, h2, ALU.add))
            link(tt(h, h, prm[:, :, 2 * G:3 * G], ALU.add))
            link(ts(h, h, 0.0, None, ALU.max))
            link(tt(h, h, prm[:, :, 3 * G:4 * G], ALU.mult))
            link(nc.vector.tensor_reduce(mag[:, :], h, AX.X, ALU.add))
            link(tt(mag[:, :], mag[:, :], prm[:, :, 4 * G], ALU.add))
            for b in range(B):
                way = prm[:, b, 4 * G + 1:TW]
                last = ts(way, way, mag[:, b:b + 1], out_scale[:, 0:1], ALU.mult, ALU.mult)
            link(last)
            y = core.xn
            link(tt(y[:, :, :], y[:, :, :], prm[:, :, 4 * G + 1:TW], ALU.add))
            layer_norm_rows(core, link, 2, dve, y, y, var_ready, std_ready)
            link(tt(y[:, :, :], y[:, :, :], gamma[:, :].unsqueeze(1).broadcast_to([T, B, D]), ALU.mult))
            tt(core.x[:, :, :], core.x[:, :, :], y[:, :, :], ALU.add)

        @block.scalar
        def _(act):
            root_step(core, act, 1, var_ready, std_ready)
            act.wait_ge(w_loaded, 16 * len(LOADS))
            for half in range(2):
                act.wait_ge(h_done, half + 1)
                nc.scalar.activation(hT[:, half * HALF:(half + 1) * HALF], core.bank[half][0:CH, 0:HALF],
                                     ACT.Gelu, bias=cb1[:, 0:1]).then_inc(h_ready, 1)
            act.wait_ge(scaled, 2)
            nc.scalar.activation(where[:, :, 0:C], where[:, :, 0:C], ACT.Exp, scale=-1.0).then_inc(exp_done, 1)
            act.wait_ge(scaled, 3)
            nc.scalar.activation(chosen[:, :, :], chosen[:, :, :], ACT.Exp, scale=-1.0).then_inc(exp_done, 1)
            for b in range(B):
                act.wait_ge(prm_done, b + 1)
                nc.scalar.activation(prm[:, b, :], core.bank[b % 2][0:T, 0:TW], ACT.Copy).then_inc(prm_ready, 1)
            act.wait_ge(comp_ready, 1)
            nc.scalar.activation(comp[:, :, :], comp[:, :, :], ACT.Tanh).then_inc(comp_tanh, 1)
            root_step(core, act, 2, var_ready, std_ready)

        @block.tensor
        def _(pe):
            norm_to_features(core, pe, dve_order, turned)
            pe.wait_ge(xT_ready, 4)
            pe.wait_ge(w_loaded, 16 * len(LOADS))
            for half in range(2):
                for c in range(DC):
                    ins = pe.matmul(core.bank[half][0:CH, 0:HALF], cw1[:, c, :],
                                    core.xnT[:, c, half * HALF:(half + 1) * HALF],
                                    start=(c == 0), stop=(c == DC - 1))
                ins.then_inc(h_done, 1)
            pe.wait_ge(sig_ready, 1)
            for b in range(B):
                for c in range(DC):
                    ins = pe.matmul(core.bank[4 + b // HB][0:T, (b % HB) * W:(b % HB + 1) * W],
                                    core.xnT[:, c, b * T:(b + 1) * T], sig[:, c, :],
                                    start=(c == 0), stop=(c == DC - 1))
                if b % HB == HB - 1:
                    ins.then_inc(scores_done, 1)
            pe.wait_ge(h_ready, 2)
            for b in range(B):
                ins = pe.matmul(core.bank[6][0:T, 2 * b:2 * b + 2], hT[:, b * T:(b + 1) * T], cw2[:, :],
                                start=True, stop=True)
            ins.then_inc(comp_done, 1)
            pe.wait_ge(onehot_ready, B)
            for half in range(2):
                for q in range(HB):
                    ins = pe.transpose(core.bank[2 + half][0:NT, q * T:(q + 1) * T], onehot[:, half * HB + q, :],
                                       core.ident[0:T, 0:T])
                ins.then_inc(onehot_turned, 1)
            pe.wait_ge(onehotT_ready, 2)
            for b in range(B):
                if b >= 2:
                    pe.wait_ge(prm_ready, b - 1)
                pe.matmul(core.bank[b % 2][0:T, 0:TW], onehotT[:, b * T:(b + 1) * T], table[:, :],
                          start=True, stop=True).then_inc(prm_done, 1)


def store(nc, core, out):
    with ExitStack() as ctx:
        out_stored = core.sem("out_stored")
        block = ctx.enter_context(nc.Block())

        @block.sync
        def _(sp):
            sp.dma_start(out.rearrange("b t d -> t b d"), core.x[:, :, :]).then_inc(out_stored, 16)
            sp.wait_ge(out_stored, 16)


PHASES = range(1, 9)


def program(nc, a, out):
    with ExitStack() as ctx:
        core = Core(nc, ctx)
        with ExitStack() as early:
            ctx_zT = early.enter_context(nc.sbuf_tensor("ctx_zT", [P, DC, B * S], F32))
            begin(nc, core, a, ctx_zT)
            if 1 in PHASES:
                latent_attention(nc, core, a, ctx_zT, "L0", True, True)
            weights = BlockWeights(nc, core, early)
            if 2 in PHASES:
                routed_experts(nc, core, a, "F0", 16, 512, 1, ACT.Silu, True, weights)
            if 3 in PHASES:
                causal_attention(nc, core, a)
            if 4 in PHASES:
                quantized_ffn(nc, core, a, weights)
            if 5 in PHASES:
                latent_attention(nc, core, a, ctx_zT, "L2", False, False)
        core.recycle()
        if 6 in PHASES:
            routed_experts(nc, core, a, "F2", 8, 1024, 2, ACT.Gelu, False)
        if 7 in PHASES:
            slot_attention(nc, core, a)
        if 8 in PHASES:
            tile_ffn(nc, core, a)
        store(nc, core, out)


def arrays_of(i):
    import numpy as np

    def chunks(w):
        return w.reshape(w.shape[0] // P, P, w.shape[1]).transpose(1, 0, 2)

    def rows(v, n=T):
        return np.broadcast_to(v.reshape(1, -1), (n, v.size))

    def cols(v):
        return v.reshape(-1, P).T

    a = {}
    a["x"] = i["x"].transpose(1, 0, 2)
    a["ctx_rows"] = i["ctx_1024"].reshape(B * SC, SP_, D).transpose(1, 0, 2)
    a["mask"] = np.broadcast_to(i["mask_BxS2_bk0"][None], (T, B, S))
    for L, g in (("L0", ("ln_x_g", "ln_x_b", "ln_l_g", "ln_l_b")), ("L2", ("g1", "b1", "g2", "b2"))):
        a[f"{L}_gains"] = np.stack([cols(i[f"{L}_xattn_{n}"]) for n in g], axis=1)
        a[f"{L}_wq"] = chunks(i[f"{L}_xattn_Wq"])
        a[f"{L}_wkv"] = chunks(i[f"{L}_xattn_Wkv"])
        a[f"{L}_wout"] = chunks(i[f"{L}_xattn_Wout"])
    a["L0_gain_o"] = rows(i["L0_xattn_ln_o_g"])
    a["L0_off_o"] = rows(i["L0_xattn_ln_o_b"])
    a["F0_gate"] = chunks(i["L0_ffn_Wg"].T)
    a["F0_w_up"] = i["L0_ffn_W1"].transpose(0, 2, 1).reshape(16, DC, P, 512).transpose(0, 2, 1, 3)
    a["F0_w_down"] = i["L0_ffn_W2"].transpose(0, 2, 1).reshape(16, 4, P, D).transpose(0, 2, 1, 3)
    a["F2_gate"] = chunks(i["L2_ffn_expert_tokens"].T)
    for n, k, w in (("up", 2, i["L2_ffn_W1"]), ("mid", 8, i["L2_ffn_W2"]), ("down", 8, i["L2_ffn_W3"])):
        a[f"F2_w_{n}"] = w.reshape(8, k, P, w.shape[2]).transpose(0, 2, 1, 3)
    a["F2_b_hid"] = np.stack([i[f"L2_ffn_b{n}"].reshape(8, 8, P).transpose(0, 2, 1) for n in (1, 2)], axis=2)
    a["F2_b_down"] = np.broadcast_to(i["L2_ffn_b3"][:, None, :], (8, P, D))
    a["A1_wqk"] = np.stack([chunks(i["L1_xattn_Wq"].T), chunks(i["L1_xattn_Wk"].T)], axis=1)
    a["A1_wv"], a["A1_wo"] = chunks(i["L1_xattn_Wv"].T), chunks(i["L1_xattn_Wo"].T)
    a["A1_bv"], a["A1_bo"] = rows(i["L1_xattn_bv"]), rows(i["L1_xattn_bo"])
    for n in ("bq", "bk"):
        a[f"A1_{n}"] = i[f"L1_xattn_{n}"].reshape(4, 4, 16).transpose(1, 2, 0)
    a["A1_ctxT"] = i["ctx_1024"][:, :T].reshape(N, DC, P).transpose(2, 1, 0)
    a["F1_w"] = np.stack([chunks(i[f"L1_ffn_w_{n}"]).reshape(P, -1) for n in ("gate", "up", "down")], axis=1)
    a["A3_wqkv"] = np.stack([chunks(i[f"L3_xattn_W{n}"].T) for n in "qkv"], axis=1)
    a["A3_wih"], a["A3_whh"] = chunks(i["L3_xattn_gru_wih"].T), chunks(i["L3_xattn_gru_whh"].T)
    a["A3_bih"], a["A3_bhh"] = rows(i["L3_xattn_gru_bih"]), rows(i["L3_xattn_gru_bhh"])
    a["A3_norms"] = np.stack([cols(i[f"L3_xattn_{n}_norm_w"]) for n in ("slot", "input")], axis=1)
    f = {n: i[f"L3_ffn_{n}"] for n in ("signatures_raw", "knot_values", "temperature", "compress_w1",
                                       "compress_b1", "compress_w2", "compress_b2", "spline_w1", "spline_b1",
                                       "spline_w2", "spline_b2", "directions", "norm_gamma", "norm_beta",
                                       "output_scale")}
    a["F3_raw"] = chunks(f["signatures_raw"].T)
    a["F3_knots"], a["F3_temp"] = rows(f["knot_values"]), rows(f["temperature"])
    a["F3_out_scale"] = rows(f["output_scale"])
    a["F3_cw1"], a["F3_cb1"] = chunks(f["compress_w1"]), f["compress_b1"].reshape(-1, 1)
    a["F3_cw2"] = f["compress_w2"]
    a["F3_cb2"] = np.broadcast_to(f["compress_b2"].reshape(1, 1, 2), (T, B, 2))
    a["F3_table"] = np.concatenate([f["spline_w1"].reshape(64, 32), f["spline_b1"], f["spline_w2"].reshape(64, 16),
                                    f["spline_b2"], f["directions"]], axis=1)
    a["F3_gamma"], a["F3_beta"] = rows(f["norm_gamma"]), rows(f["norm_beta"])
    return {k: np.ascontiguousarray(v) for k, v in a.items()}


def kernel(**inputs):
    import numpy as np
    import concourse.bacc as bacc
    from concourse.bass_utils import run_bass_kernel_spmd

    nc = bacc.Bacc("TRN2", target_bir_lowering=False, num_devices=1)
    arrays = arrays_of({k: np.asarray(v) for k, v in inputs.items()})
    aps = {k: nc.dram_tensor(f"in_{k}", v.shape, mybir.dt.from_np(v.dtype), kind="ExternalInput").ap()
           for k, v in arrays.items()}
    out = nc.dram_tensor("out", (B, T, D), F32, kind="ExternalOutput").ap()
    program(nc, aps, out)
    r = run_bass_kernel_spmd(nc, [{f"in_{k}": v for k, v in arrays.items()}], core_ids=[0])
    return r.results[0]["out"]
```
